# Optimizing a Trainium2 kernel written in Bass

```python
import numpy as np
import jax
import jax.numpy as jnp

def _softmax(x, axis=-1):
    return jax.nn.softmax(x, axis=axis)

def _gelu(x):
    return jax.nn.gelu(x, approximate=True)

def _silu(x):
    return jax.nn.silu(x)

def _sigmoid(x):
    return jax.nn.sigmoid(x)

def _layernorm(x, axis=-1, eps=1e-05):
    m = jnp.mean(x, axis=axis, keepdims=True)
    v = jnp.var(x, axis=axis, keepdims=True)
    return (x - m) / jnp.sqrt(v + eps)

def _scatter_add(tgt, idx, src, axis=0):
    return tgt.at[idx].add(src)

def _segment_sum(src, seg, n):
    return jax.ops.segment_sum(src, seg, n)
kernel_name = 'mk_recurrent_d1_jaxref_r2_9886c4'

def setup_inputs(seed: int=0):
    np.random.seed(seed)
    _w = jnp.asarray

    def _L0_attn_setup():
        import jax, jax.numpy as jnp
        import numpy as np
        D_MODEL = 512
        NUM_HEADS = 16
        HEAD_DIM = D_MODEL // NUM_HEADS
        THETA = 10000.0
        B, T = (4, 1024)

        def _cos_sin(seq_len, head_dim, theta):
            freqs = 1.0 / theta ** (jnp.arange(0, head_dim, 2, dtype=jnp.float32) / head_dim)
            t = jnp.arange(seq_len, dtype=jnp.float32)
            angles = jnp.outer(t, freqs)
            return jnp.concatenate([jnp.cos(angles), jnp.sin(angles)], axis=-1)

        def _apply_rope(x, cos_sin):
            x1 = x[..., 0::2]
            x2 = x[..., 1::2]
            half = x.shape[-1] // 2
            cos = cos_sin[:, :half]
            sin = cos_sin[:, half:]
            out = jnp.stack([x1 * cos - x2 * sin, x1 * sin + x2 * cos], axis=-1)
            return out.reshape(x.shape)
        key = jax.random.key(seed)
        k1, k2, k3 = jax.random.split(key, 3)
        x = jax.random.normal(k1, (B, T, D_MODEL), dtype=jnp.float32)
        W_qkv = jax.random.normal(k2, (3 * D_MODEL, D_MODEL), dtype=jnp.float32) * D_MODEL ** (-0.5)
        W_out = jax.random.normal(k3, (D_MODEL, D_MODEL), dtype=jnp.float32) * D_MODEL ** (-0.5)
        return {'x': x, 'W_qkv': W_qkv, 'W_out': W_out}
    _L0_attn_in = _L0_attn_setup()

    def _L0_ffn_setup():
        import jax, jax.numpy as jnp
        import numpy as np
        EMBED = 512
        NUM_EXPERTS = 8
        TOP_K = 2
        key = jax.random.key(seed)
        ks = jax.random.split(key, 6)
        scale = EMBED ** (-0.5)
        return {'x': jax.random.normal(ks[0], (4, 2048, EMBED), jnp.float32), 'router_w': jax.random.normal(ks[1], (EMBED, NUM_EXPERTS), jnp.float32) * scale, 'router_b': jnp.zeros((NUM_EXPERTS,), jnp.float32), 'we_gate': jax.random.normal(ks[2], (NUM_EXPERTS, EMBED, EMBED), jnp.float32) * scale, 'we_up': jax.random.normal(ks[3], (NUM_EXPERTS, EMBED, EMBED), jnp.float32) * scale, 'we_down': jax.random.normal(ks[4], (NUM_EXPERTS, EMBED, EMBED), jnp.float32) * scale}
    _L0_ffn_in = _L0_ffn_setup()
    _d = {'L0_attn_x': _L0_attn_in['x'], 'L0_attn_W_qkv': _L0_attn_in['W_qkv'], 'L0_attn_W_out': _L0_attn_in['W_out'], 'L0_ffn_router_w': _L0_ffn_in['router_w'], 'L0_ffn_router_b': _L0_ffn_in['router_b'], 'L0_ffn_we_gate': _L0_ffn_in['we_gate'], 'L0_ffn_we_up': _L0_ffn_in['we_up'], 'L0_ffn_we_down': _L0_ffn_in['we_down']}
    _x0 = _d['L0_attn_x']
    _d['L0_attn_x'] = jax.random.normal(jax.random.fold_in(jax.random.key(seed), 1), (4, 2048, 512), dtype=_x0.dtype)
    del _x0
    return _d

def reference(L0_attn_x, L0_attn_W_qkv, L0_attn_W_out, L0_ffn_router_w, L0_ffn_router_b, L0_ffn_we_gate, L0_ffn_we_up, L0_ffn_we_down):

    def _L0_attn_ref(x, W_qkv, W_out):
        import jax, jax.numpy as jnp
        import numpy as np
        D_MODEL = 512
        NUM_HEADS = 16
        HEAD_DIM = D_MODEL // NUM_HEADS
        THETA = 10000.0
        B, T = (4, 1024)

        def _cos_sin(seq_len, head_dim, theta):
            freqs = 1.0 / theta ** (jnp.arange(0, head_dim, 2, dtype=jnp.float32) / head_dim)
            t = jnp.arange(seq_len, dtype=jnp.float32)
            angles = jnp.outer(t, freqs)
            return jnp.concatenate([jnp.cos(angles), jnp.sin(angles)], axis=-1)

        def _apply_rope(x, cos_sin):
            x1 = x[..., 0::2]
            x2 = x[..., 1::2]
            half = x.shape[-1] // 2
            cos = cos_sin[:, :half]
            sin = cos_sin[:, half:]
            out = jnp.stack([x1 * cos - x2 * sin, x1 * sin + x2 * cos], axis=-1)
            return out.reshape(x.shape)
        Bsz, Tlen, _ = x.shape
        qkv = jnp.einsum('bti,oi->bto', x, W_qkv)
        qkv = qkv.reshape(Bsz, Tlen, 3 * NUM_HEADS, HEAD_DIM).transpose(0, 2, 1, 3)
        q, k, v = jnp.split(qkv, 3, axis=1)
        cos_sin = _cos_sin(Tlen, HEAD_DIM, THETA)
        q = _apply_rope(q, cos_sin)
        k = _apply_rope(k, cos_sin)
        scores = jnp.einsum('bhqd,bhkd->bhqk', q, k) / np.sqrt(HEAD_DIM).astype(np.float32)
        causal = jnp.tril(jnp.ones((Tlen, Tlen), dtype=bool))
        scores = jnp.where(causal[None, None], scores, -jnp.inf)
        attn = jax.nn.softmax(scores, axis=-1)
        o = jnp.einsum('bhqk,bhkd->bhqd', attn, v)
        o = o.transpose(0, 2, 1, 3).reshape(Bsz, Tlen, D_MODEL)
        return jnp.einsum('bti,oi->bto', o, W_out)

    def _L0_ffn_ref(x, router_w, router_b, we_gate, we_up, we_down):
        import jax, jax.numpy as jnp
        import numpy as np
        EMBED = 512
        NUM_EXPERTS = 8
        TOP_K = 2
        x_shape = x.shape
        x_flat = x.reshape(-1, x_shape[-1])
        num_tokens = x_flat.shape[0]
        router_logits = x_flat @ router_w + router_b
        topk_weights, topk_indices = jax.lax.top_k(router_logits, k=TOP_K)
        topk_weights = jax.nn.softmax(topk_weights, axis=-1)
        token_idx_mesh = jnp.repeat(jnp.arange(num_tokens), TOP_K)
        expert_idx_mesh = topk_indices.reshape(-1)
        sort_permutation = jnp.argsort(expert_idx_mesh)
        sorted_expert_idx = expert_idx_mesh[sort_permutation]
        sorted_token_idx = token_idx_mesh[sort_permutation]
        group_sizes = jnp.bincount(sorted_expert_idx, length=NUM_EXPERTS)
        sorted_tokens = x_flat[sorted_token_idx]
        ff_gate = jax.lax.ragged_dot(sorted_tokens, we_gate, group_sizes)
        ff_up = jax.lax.ragged_dot(sorted_tokens, we_up, group_sizes)
        activated = jax.nn.silu(ff_gate) * ff_up
        ff_out = jax.lax.ragged_dot(activated, we_down, group_sizes)
        sorted_weights = topk_weights.reshape(-1)[sort_permutation]
        ff_out = ff_out * sorted_weights[:, None]
        output_flat = jnp.zeros_like(x_flat).at[sorted_token_idx].add(ff_out)
        return output_flat.reshape(x_shape)
    x = L0_attn_x
    xn = _layernorm(x, axis=-1)
    s = _L0_attn_ref(xn, L0_attn_W_qkv, L0_attn_W_out)
    g = _silu(_L0_ffn_ref(xn, L0_ffn_router_w, L0_ffn_router_b, L0_ffn_we_gate, L0_ffn_we_up, L0_ffn_we_down))
    x = x + s * g
    return x

_drawn_inputs = setup_inputs


def setup_inputs(seed=0):
    import zlib

    import numpy as np

    out = dict(_drawn_inputs(seed))
    spreads = {'L0_ffn_router_b': (0.0, 0.643)}
    factors = {}
    for name, (base, spread) in spreads.items():
        noise = np.random.default_rng([zlib.crc32(name.encode()), seed]).standard_normal(out[name].shape)
        drawn = base * np.exp(spread * noise) if base else spread * noise
        out[name] = jnp.asarray(drawn.astype(out[name].dtype))
    for name, factor in factors.items():
        out[name] = (out[name] * factor).astype(out[name].dtype)
    return out
```

```python
import concourse.bass as bass
from concourse import mybir
from contextlib import ExitStack

B, T, D = 4, 2048, 512
H, DH = 16, 32
E = 8
P = 128
NTOK = B * T
KD = D // P
CH = 512
TPC = CH // P
NCH = NTOK // CH
CPB = T // CH
NT = NTOK // P
QUAD = P // DH
NG = H // QUAD
NIT = B * NG
BLK = 256
NBLK = 2 * NTOK // BLK + E
NSLOT = NBLK * BLK
PADS = NSLOT - 2 * NTOK
RB = NTOK // BLK
NEG = -1.0e30
SCALE = 1.0 / float(DH) ** 0.5
EPS = 1e-5
UP = 1
PASSES = ((0, 0), (0, 1), (1, 0))


def build(nc, x, wqkvT, woutT, rwT, rb, wg, wu, wd, cos, sin, cmask, cmaskT, identb, ident, cst, out):
    f32, f32r, bf16 = mybir.dt.float32, mybir.dt.float32r, mybir.dt.bfloat16
    i32, u32 = mybir.dt.int32, mybir.dt.uint32
    ALU, ACT, AX = mybir.AluOpType, mybir.ActivationFunctionType, mybir.AxisListType.X

    def dram(name, shape, dt):
        return nc.dram_tensor(name, shape, dt, kind="Internal").ap()

    qk_d = [dram("qT_parts", (B * H, 2, DH, T), f32), dram("kT_parts", (B * H, 2, DH, T), f32)]
    v_d = dram("v_rows", (NTOK, D), f32)
    xn_d = dram("xn_rows", (NTOK, D), f32)
    attn_d = dram("attnT", (NIT, P, T), f32)
    xs_d = dram("sorted_rows", (NSLOT, D), f32)
    ys_d = dram("expert_rows", (NSLOT, D), f32)

    top = ExitStack()

    def scope(ctx, stage, sems=None):
        def sb(name, shape, dt):
            return ctx.enter_context(nc.sbuf_tensor(f"{stage}_{name}", shape, dt))

        def ps(name):
            return ctx.enter_context(nc.psum_tensor(f"{stage}_{name}", [P, 512], f32))

        def sem(name):
            s = ctx.enter_context(nc.semaphore(f"{stage}_{name}"))
            if sems is not None:
                sems.append(s)
            return s
        return sb, ps, sem

    with top:
        sb, _, _ = scope(top, "kept")
        ident_sb = sb("ident_sb", [P, P], f32)
        logits = sb("logits", [P, NT, E], f32)
        pos = sb("pos", [P, 2, NT], i32)
        wts = sb("wts", [P, 2, NT], f32)
        padpos = sb("padpos", [P, 2 * E], i32)
        blk_e = sb("blk_e", [1, NBLK], i32)

        project(nc, scope, x, wqkvT, rwT, rb, cos, sin, ident, ident_sb, logits, qk_d, v_d, xn_d)
        route(nc, scope, cst, ident_sb, logits, pos, wts, padpos, blk_e)
        attend(nc, scope, qk_d, v_d, xn_d, attn_d, xs_d, cmask, cmaskT, identb, cst, ident_sb, pos, padpos)
        experts(nc, scope, wg, wu, wd, xs_d, ys_d, ident_sb, blk_e)
        combine(nc, scope, x, woutT, attn_d, ys_d, pos, wts, out)


def project(nc, scope, x, wqkvT, rwT, rb, cos, sin, ident, ident_sb, logits, qk_d, v_d, xn_d):
    f32, f32r = mybir.dt.float32, mybir.dt.float32r
    ALU, ACT = mybir.AluOpType, mybir.ActivationFunctionType
    OC = 3 * D
    with ExitStack() as ctx:
        sems = []
        sb, ps, sem = scope(ctx, "project", sems)
        w = [sb(f"w_part{n}", [P, KD, OC], f32r) for n in range(2)]
        rw = [sb(f"rw_part{n}", [P, KD, E], f32r) for n in range(2)]
        rb_sb = sb("rb_sb", [E, 1], f32)
        cos_sb = sb("cos_sb", [P, T], f32)
        sin_sb = sb("sin_sb", [P, T], f32)
        with ExitStack() as c2:
            sb2, _, sem2 = scope(c2, "split")
            wraw = sb2("wraw", [P, KD, OC], f32)
            rwraw = sb2("rwraw", [P, KD, E], f32)
            loaded, high = sem2("weights_loaded"), sem2("weights_high")
            low = sem2("weights_low")
            block = c2.enter_context(nc.Block())

            @block.sync
            def _(sp):
                sp.dma_start(wraw[:, :, :], wqkvT.rearrange("(k p) o -> p k o", p=P)).then_inc(loaded, 16)
                sp.dma_start(rwraw[:, :, :], rwT.rearrange("(k p) e -> p k e", p=P)).then_inc(loaded, 16)
                sp.dma_start(rb_sb[:, :], rb).then_inc(loaded, 16)
                sp.dma_start(cos_sb[:, :], cos).then_inc(loaded, 16)
                sp.dma_start(sin_sb[:, :], sin).then_inc(loaded, 16)
                sp.dma_start(ident_sb[:, :], ident).then_inc(loaded, 16)

            @block.vector
            def _(dve):
                dve.wait_ge(loaded, 6 * 16)
                nc.vector.tensor_copy(rw[0][:, :, :], rwraw[:, :, :]).then_inc(high, 1)
                for k in range(KD):
                    nc.vector.tensor_copy(w[0][:, k, :], wraw[:, k, :]).then_inc(high, 1)
                dve.wait_ge(high, 1)
                nc.vector.tensor_tensor(rw[1][:, :, :], rwraw[:, :, :], rw[0][:, :, :].bitcast(f32),
                                        ALU.subtract).then_inc(low, 1)
                for k in range(KD):
                    dve.wait_ge(high, k + 2)
                    nc.vector.tensor_tensor(w[1][:, k, :], wraw[:, k, :], w[0][:, k, :].bitcast(f32),
                                            ALU.subtract).then_inc(low, 1)
                dve.wait_ge(low, KD + 1)

        xin = [sb(f"xin{n}", [P, TPC, D], f32) for n in range(2)]
        xn = [sb(f"xn{n}", [P, TPC, D], f32) for n in range(2)]
        stats = sb("stats", [P, 2, TPC, 6], f32)
        mv = sb("mv", [P, 2, TPC, 2], f32)
        std = sb("std", [P, 2, TPC], f32)
        rstd = sb("rstd", [P, 2, TPC], f32)
        eps = sb("eps", [P, 1], f32)
        xT = [[sb(f"xT{n}_part{m}", [P, KD, CH], f32r) for m in range(2)] for n in range(2)]
        prod = sb("rope_products", [P, 2, 2, CH], f32)
        rot = sb("rotated", [P, 2, CH], f32)
        rot_p = [sb(f"rotated_part{m}", [P, 2, 2, CH], f32r) for m in range(2)]
        v_sb = sb("v_sb", [P, TPC, D], f32)
        lt = sb("logitsT", [E, 2, CH], f32)

        tp = [ps(f"transposed{n}") for n in range(2)]
        qkp = [ps(f"qk_half{n}") for n in range(4)]
        vp = [ps(f"v_psum{n}") for n in range(2)]

        x_in, x_free = [sem(f"x_in{n}") for n in range(2)], sem("x_free")
        bn, agg, stdd, rs, normed = sem("bn"), sem("agg"), sem("stdd"), sem("rs"), sem("normed")
        eps_set = sem("eps_set")
        passed = sem("passed")
        xn_out = [sem(f"xn_out{n}") for n in range(2)]
        tr, t_hi, t_lo = sem("transposes"), sem("xT_high"), sem("xT_low")
        qk_full, v_full, rt_full = sem("qk_full"), sem("v_full"), sem("router_full")
        prods, rots, r_hi, r_lo = sem("products"), sem("rotations"), sem("rot_high"), sem("rot_low")
        qk_out = [sem(f"qk_out{n}") for n in range(2)]
        v_cp, v_out, lt_cp, lg_cp = sem("v_copied"), sem("v_out"), sem("lt_copied"), sem("logits_copied")
        moved_on = sem("moved_on")
        block = ctx.enter_context(nc.Block())

        NPAIR = 4

        @block.sync
        def _(sp):
            for s in sems:
                sp.sem_inc(s, UP)
            with sp.Fori(0, B) as b:
                for j in range(CPB):
                    c, n = b * CPB + j, j % 2
                    rows = x[bass.ds(c * CH, CH), :].rearrange("(t p) d -> p t d", p=P)
                    if j < 2:
                        sp.wait_ge(normed, c * TPC - (j) * TPC + UP)
                        sp.sem_inc(moved_on, 1)
                    else:
                        sp.wait_ge(normed, (c - 1) * TPC + UP)
                        sp.sem_inc(moved_on, 1)
                    sp.dma_start(xin[n][:, :, :], rows).then_inc(x_in[n], 16)

        @block.vector
        def _(dve):
            nc.vector.memset(eps[:, :], EPS).then_inc(eps_set, 1)
            with dve.Fori(0, B) as b:
                for j in range(CPB):
                    c, n = b * CPB + j, j % 2
                    dve.wait_ge(x_in[n], (b * 2 + j // 2 + 1) * 16 + UP)
                    for t in range(TPC):
                        nc.vector.bn_stats(stats[:, n, t, :], xin[n][:, t, :]).then_inc(bn, 1)
                    dve.wait_ge(bn, (c + 1) * TPC + UP)
                    dve.sem_inc(passed, 1)
                    for t in range(TPC):
                        nc.vector.bn_aggr(mv[:, n, t, :], stats[:, n, t, :]).then_inc(agg, 1)
                    dve.wait_ge(stdd, c + 1 + UP)
                    nc.vector.reciprocal(rstd[:, n, :], std[:, n, :]).then_inc(rs, 1)
                    dve.wait_ge(rs, c + 1 + UP)
                    dve.wait_ge(xn_out[n], (b * 2 + j // 2) * 16 + UP)
                    if j >= 2:
                        dve.wait_ge(tr, (c - 1) * KD + UP)
                    else:
                        dve.wait_ge(tr, (c - j) * KD + UP)
                    for t in range(TPC):
                        nc.vector.tensor_scalar(xn[n][:, t, :], xin[n][:, t, :], mv[:, n, t, 0:1],
                                                rstd[:, n, t:t + 1], ALU.subtract, ALU.mult).then_inc(normed, 1)
                    if j >= 2:
                        dve.wait_ge(qk_full, (c - 1) * 2 * NPAIR + UP)
                    else:
                        dve.wait_ge(qk_full, (c - j) * 2 * NPAIR + UP)
                    for k in range(KD):
                        dve.wait_ge(t_hi, c * KD + k + 1 + UP)
                        nc.vector.tensor_tensor(xT[n][1][:, k, :], tp[k % 2][:, :], xT[n][0][:, k, :].bitcast(f32),
                                                ALU.subtract).then_inc(t_lo, 1)
                    dve.wait_ge(rt_full, 2 * c + 2 + UP)
                    nc.vector.tensor_copy(logits[:, bass.ds(c * TPC, TPC), :],
                                          vp[0][:, 0:TPC * E].rearrange("p (t e) -> p t e", e=E)).then_inc(lg_cp, 1)
                    cs, sn = cos_sb[:, j * CH:(j + 1) * CH], sin_sb[:, j * CH:(j + 1) * CH]
                    for r in range(NPAIR):
                        a, bb = qkp[2 * (r % 2)], qkp[2 * (r % 2) + 1]
                        dve.wait_ge(rots, (c * NPAIR + r) * 2 + UP)
                        dve.wait_ge(qk_full, (c * NPAIR + r) * 2 + 1 + UP)
                        nc.vector.tensor_tensor(prod[:, 0, 0, :], a[:, :], cs, ALU.mult).then_inc(prods, 1)
                        nc.vector.tensor_tensor(prod[:, 0, 1, :], a[:, :], sn, ALU.mult).then_inc(prods, 1)
                        dve.wait_ge(qk_full, (c * NPAIR + r) * 2 + 2 + UP)
                        nc.vector.tensor_tensor(prod[:, 1, 0, :], bb[:, :], sn, ALU.mult).then_inc(prods, 1)
                        nc.vector.tensor_tensor(prod[:, 1, 1, :], bb[:, :], cs, ALU.mult).then_inc(prods, 1)

        @block.gpsimd
        def _(pool):
            with pool.Fori(0, B) as b:
                for j in range(CPB):
                    c = b * CPB + j
                    for r in range(NPAIR):
                        q, m = c * NPAIR + r, r % 2
                        pool.wait_ge(r_hi, q * 2 + UP)
                        pool.wait_ge(r_lo, q * 2 + UP)
                        pool.wait_ge(prods, q * 4 + 3 + UP)
                        nc.gpsimd.tensor_tensor(rot[:, 0, :], prod[:, 0, 0, :], prod[:, 1, 0, :],
                                                ALU.subtract).then_inc(rots, 1)
                        pool.wait_ge(prods, q * 4 + 4 + UP)
                        nc.gpsimd.tensor_tensor(rot[:, 1, :], prod[:, 0, 1, :], prod[:, 1, 1, :],
                                                ALU.add).then_inc(rots, 1)
                        for h in range(2):
                            pool.wait_ge(r_hi, q * 2 + h + 1 + UP)
                            nc.gpsimd.tensor_tensor(rot_p[1][:, m, h, :], rot[:, h, :],
                                                    rot_p[0][:, m, h, :].bitcast(f32), ALU.subtract).then_inc(r_lo, 1)

        @block.scalar
        def _(act):
            act.wait_ge(eps_set, 1 + UP)
            with act.Fori(0, B) as b:
                for j in range(CPB):
                    c, n = b * CPB + j, j % 2
                    act.wait_ge(agg, (c + 1) * TPC + UP)
                    nc.scalar.activation(std[:, n, :], mv[:, n, :, 1], ACT.Sqrt, bias=eps[:, 0:1]).then_inc(stdd, 1)
                    act.wait_ge(normed, (c + 1) * TPC + UP)
                    act.dma_start(xn_d[bass.ds(c * CH, CH), :].rearrange("(t p) d -> p t d", p=P),
                                  xn[n][:, :, :]).then_inc(xn_out[n], 16)
                    if j >= 2:
                        act.wait_ge(qk_full, (c - 1) * 2 * NPAIR + UP)
                    else:
                        act.wait_ge(qk_full, (c - j) * 2 * NPAIR + UP)
                    for k in range(KD):
                        act.wait_ge(tr, c * KD + k + 1 + UP)
                        nc.scalar.activation(xT[n][0][:, k, :], tp[k % 2][:, :], ACT.Copy).then_inc(t_hi, 1)
                    act.wait_ge(rt_full, 2 * c + 1 + UP)
                    nc.scalar.activation(lt[:, n, :], vp[0][0:E, :], ACT.Identity, bias=rb_sb[:, 0:1]).then_inc(lt_cp, 1)
                    act.wait_ge(v_out, c * 16 + UP)
                    for t in range(TPC):
                        act.wait_ge(v_full, c * TPC + t + 1 + UP)
                        nc.scalar.activation(v_sb[:, t, :], vp[(t + 1) % 2][:, :], ACT.Copy).then_inc(v_cp, 1)
                    act.wait_ge(v_cp, (c + 1) * TPC + UP)
                    act.dma_start(v_d[bass.ds(c * CH, CH), :].rearrange("(t p) d -> p t d", p=P),
                                  v_sb[:, :, :]).then_inc(v_out, 16)
                    for r in range(NPAIR):
                        q, m = c * NPAIR + r, r % 2
                        act.wait_ge(qk_out[m], (c * 2 + r // 2) * 64 + UP)
                        for h in range(2):
                            act.wait_ge(rots, q * 2 + h + 1 + UP)
                            nc.scalar.activation(rot_p[0][:, m, h, :], rot[:, h, :], ACT.Copy).then_inc(r_hi, 1)
                        act.wait_ge(r_hi, q * 2 + 2 + UP)
                        act.wait_ge(r_lo, q * 2 + 2 + UP)
                        z, g = r // 2, r % 2
                        for part in range(2):
                            for h in range(2):
                                dst = qk_d[z][bass.ds(b * H + g * (H // 2), H // 2), part,
                                              h * (DH // 2):(h + 1) * (DH // 2), j * CH:(j + 1) * CH]
                                act.dma_start(dst, rot_p[part][:, m, h, :].bitcast(f32)).then_inc(qk_out[m], 16)
            act.wait_ge(v_out, NCH * 16 + UP)
            for m in range(2):
                act.wait_ge(xn_out[m], NCH // 2 * 16 + UP)
                act.wait_ge(qk_out[m], NCH * 2 * 64 + UP)

        @block.tensor
        def _(pe):
            with pe.Fori(0, B) as b:
                for j in range(CPB):
                    c, n = b * CPB + j, j % 2
                    for k in range(KD):
                        if k == 0:
                            pe.wait_ge(normed, (c + 1) * TPC + UP)
                        if k < 2:
                            pe.wait_ge(t_lo, c * KD + UP)
                        else:
                            pe.wait_ge(t_lo, c * KD + k - 1 + UP)
                        for t in range(TPC):
                            last = nc.tensor.transpose(tp[k % 2][:, t * P:(t + 1) * P],
                                                       xn[n][:, t, k * P:(k + 1) * P], ident_sb[:, :])
                        last.then_inc(tr, 1)
                    pe.wait_ge(t_lo, (c + 1) * KD + UP)
                    pe.wait_ge(v_cp, c * TPC + UP)
                    for m, (k, (a, w2)) in enumerate([(k, p) for k in range(KD) for p in PASSES]):
                        last = nc.tensor.matmul(vp[0][0:E, :], rw[w2][:, k, :], xT[n][a][:, k, :],
                                                start=m == 0, stop=m == 3 * KD - 1)
                    last.then_inc(rt_full, 1)
                    for t in range(TPC):
                        bank = (t + 1) % 2
                        if t == 1:
                            pe.wait_ge(lt_cp, c + 1 + UP)
                            pe.sem_inc(passed, 1)
                            for u in range(TPC):
                                last = nc.tensor.transpose(vp[0][:, u * E:(u + 1) * E],
                                                           lt[:, n, u * P:(u + 1) * P], ident_sb[0:E, 0:E])
                            last.then_inc(rt_full, 1)
                            pe.wait_ge(lg_cp, c + 1 + UP)
                        if t >= 2:
                            pe.wait_ge(v_cp, c * TPC + t - 1 + UP)
                        for m, (k, (a, w2)) in enumerate([(k, p) for k in range(KD) for p in PASSES]):
                            last = nc.tensor.matmul(vp[bank][:, :], xT[n][a][:, k, t * P:(t + 1) * P],
                                                    w[w2][:, k, 2 * D:3 * D], start=m == 0, stop=m == 3 * KD - 1)
                        last.then_inc(v_full, 1)
                    for r in range(NPAIR):
                        for h in range(2):
                            pe.wait_ge(prods, (c * NPAIR + (r - 1 if r >= 2 else 0)) * 4 + UP)
                            col = (2 * r + h) * P
                            for m, (k, (a, w2)) in enumerate([(k, p) for k in range(KD) for p in PASSES]):
                                last = nc.tensor.matmul(qkp[2 * (r % 2) + h][:, :], w[w2][:, k, col:col + P],
                                                        xT[n][a][:, k, :], start=m == 0, stop=m == 3 * KD - 1)
                            last.then_inc(qk_full, 1)


C_IOTA = 0
C_RUN = C_IOTA + E
C_LESS = C_RUN + E * NT
C_ONE = C_LESS + P
C_THR = C_ONE + P
C_ROW = C_THR + RB
C_BLK = C_ROW + 2
C_SEL = C_BLK + NBLK
C_ALL = C_SEL + DH


def constants():
    import numpy as np
    c = np.zeros((P, C_ALL), np.float32)
    p = np.arange(P)
    c[:, C_IOTA:C_IOTA + E] = np.arange(E) - E
    run = np.ones((E, NT), np.float32)
    run[:, 0] = 0
    c[:, C_RUN:C_LESS] = run.reshape(-1)
    c[:, C_LESS:C_ONE] = p[:, None] < p[None, :]
    c[:, C_ONE:C_THR] = 1
    c[:, C_THR:C_ROW] = BLK * np.arange(RB)
    c[:, C_ROW:C_BLK] = p[:, None] + P * np.arange(2)
    c[:, C_BLK:C_SEL] = np.arange(NBLK)
    c[:, C_SEL:C_ALL] = (p[:, None] % DH) == np.arange(DH)
    return c


def route(nc, scope, cst, ident_sb, logits, pos, wts, padpos, blk_e):
    f32 = mybir.dt.float32
    ALU, ACT, AX = mybir.AluOpType, mybir.ActivationFunctionType, mybir.AxisListType.X
    with ExitStack() as ctx:
        sb, ps, sem = scope(ctx, "route")
        cs = sb("consts", [P, C_ALL], f32)
        t3 = sb("tmp3", [P, NT, E], f32)
        m3 = sb("masked_logits", [P, NT, E], f32)
        hot = [sb(f"onehot{n}", [P, NT, E], f32) for n in range(2)]
        best = sb("best", [P, 2, NT], f32)
        idx = sb("first_index", [P, NT], f32)
        ex = sb("exp_difference", [P, NT], f32)
        both = sb("chosen", [P, E, NT], f32)
        upto = sb("chosen_up_to", [P, E, NT], f32)
        row = sb("row_of_choice", [P, E, NT], f32)
        total = sb("partition_total", [P, E], f32)
        over = sb("blocks_over", [P, E, RB], f32)
        nb = sb("blocks", [P, E], f32)
        nbe = sb("blocks_up_to", [P, E], f32)
        start = sb("first_row", [P, E], f32)
        tot = sb("expert_total", [P, E], f32)
        pad = sb("pads", [P, E], f32)
        rest = sb("rest", [P, E], f32)
        rest_to = sb("rest_up_to", [P, E], f32)
        tail = sb("tail_base", [P, E], f32)
        inside = sb("pad_inside", [P, E, 2], f32)
        used = sb("pad_used", [P, E, 2], f32)
        outside = sb("pad_outside", [P, E, 2], f32)
        posf = sb("row_float", [P, 2, NT], f32)
        bc = sb("block_compare", [1, NBLK, E], f32)
        be = sb("block_expert", [1, NBLK], f32)
        cnt = ps("count_psum")
        got, step, counted, expd = sem("constants_in"), sem("dve_step"), sem("counted"), sem("exp_done")
        moved_on = sem("moved_on")
        block = ctx.enter_context(nc.Block())
        less, ones = cs[:, C_LESS:C_ONE], cs[:, C_ONE:C_THR]

        def per_expert(ap, n):
            return ap.rearrange("p (e o) -> p e o", o=1).to_broadcast([P, E, n])

        @block.sync
        def _(sp):
            sp.dma_start(cs[:, :], cst).then_inc(got, 16)

        marks = {}

        @block.vector
        def _(dve):
            done = [0]

            def link(ins):
                done[0] += 1
                ins.then_inc(step, 1)
                dve.wait_ge(step, done[0])

            v = nc.vector
            iota = cs[:, C_IOTA:C_RUN].rearrange("p (o e) -> p o e", o=1).to_broadcast([P, NT, E])
            dve.wait_ge(got, 16)
            for n, src in enumerate((logits, m3)):
                link(v.tensor_reduce(best[:, n, :], src[:, :, :], AX, ALU.max))
                top = best[:, n, :].rearrange("p (t o) -> p t o", o=1).to_broadcast([P, NT, E])
                link(v.tensor_tensor(t3[:, :, :], src[:, :, :], top, ALU.is_equal))
                link(v.scalar_tensor_tensor(out=t3[:, :, :], in0=t3[:, :, :], scalar=-float(E), in1=iota,
                                            op0=ALU.mult, op1=ALU.add))
                link(v.tensor_reduce(idx[:, :], t3[:, :, :], AX, ALU.min))
                link(v.tensor_scalar(idx[:, :], idx[:, :], float(E), None, ALU.add))
                first = idx[:, :].rearrange("p (t o) -> p t o", o=1).to_broadcast([P, NT, E])
                link(v.tensor_tensor(hot[n][:, :, :], iota, first, ALU.is_equal))
                if n == 0:
                    link(v.scalar_tensor_tensor(out=m3[:, :, :], in0=hot[0][:, :, :], scalar=-3.0e38,
                                                in1=logits[:, :, :], op0=ALU.mult, op1=ALU.add))
            link(v.tensor_tensor(ex[:, :], best[:, 1, :], best[:, 0, :], ALU.subtract))
            marks["diff"] = done[0]
            dve.wait_ge(expd, 1)
            link(v.tensor_scalar(wts[:, 1, :], ex[:, :], 1.0, None, ALU.add))
            link(v.reciprocal(wts[:, 0, :], wts[:, 1, :]))
            link(v.tensor_tensor(wts[:, 1, :], ex[:, :], wts[:, 0, :], ALU.mult))
            link(v.tensor_tensor(both[:, :, :].rearrange("p e t -> p t e"), hot[0][:, :, :], hot[1][:, :, :],
                                 ALU.add))
            link(v.tensor_tensor_scan(upto[:, :, :].rearrange("p e t -> p (e t)"), cs[:, C_RUN:C_LESS],
                                      both[:, :, :].rearrange("p e t -> p (e t)"), 0.0, ALU.mult, ALU.add))
            link(v.tensor_copy(total[:, :], upto[:, :, NT - 1]))
            marks["total"] = done[0]
            dve.wait_ge(counted, 1)
            link(v.tensor_copy(tot[:, :], cnt[:, E:2 * E]))
            thr = cs[:, C_THR:C_ROW].rearrange("p (o k) -> p o k", o=1).to_broadcast([P, E, RB])
            link(v.tensor_tensor(over[:, :, :], per_expert(tot[:, :], RB), thr, ALU.is_gt))
            link(v.tensor_reduce(nb[:, :], over[:, :, :], AX, ALU.add))
            link(v.tensor_tensor_scan(nbe[:, :], ones[:, 0:E], nb[:, :], 0.0, ALU.mult, ALU.add))
            link(v.tensor_tensor(start[:, :], nbe[:, :], nb[:, :], ALU.subtract))
            link(v.tensor_scalar(start[:, :], start[:, :], float(BLK), None, ALU.mult))
            link(v.tensor_tensor(row[:, :, :], upto[:, :, :], both[:, :, :], ALU.subtract))
            link(v.tensor_tensor(rest[:, :], start[:, :], cnt[:, 0:E], ALU.add))
            link(v.tensor_tensor(row[:, :, :], row[:, :, :], per_expert(rest[:, :], NT), ALU.add))
            for n in range(2):
                link(v.tensor_tensor(t3[:, :, :], hot[n][:, :, :], row[:, :, :].rearrange("p e t -> p t e"),
                                     ALU.mult))
                link(v.tensor_reduce(posf[:, n, :], t3[:, :, :], AX, ALU.add))
            link(v.tensor_copy(pos[:, :, :], posf[:, :, :]))
            link(v.tensor_scalar(pad[:, :], nb[:, :], float(BLK), None, ALU.mult))
            link(v.tensor_tensor(pad[:, :], pad[:, :], tot[:, :], ALU.subtract))
            link(v.tensor_scalar(rest[:, :], pad[:, :], -1.0, float(BLK), ALU.mult, ALU.add))
            link(v.tensor_tensor_scan(rest_to[:, :], ones[:, 0:E], rest[:, :], 0.0, ALU.mult, ALU.add))
            link(v.tensor_tensor(tail[:, :], rest_to[:, :], rest[:, :], ALU.subtract))
            link(v.tensor_tensor(tail[:, :], tail[:, :], pad[:, :], ALU.subtract))
            link(v.tensor_scalar(rest[:, :], nbe[:, :], float(BLK), None, ALU.mult))
            link(v.tensor_scalar(tail[:, :], tail[:, :], rest[:, E - 1:E], None, ALU.add))
            link(v.tensor_tensor(start[:, :], start[:, :], tot[:, :], ALU.add))
            r2 = cs[:, C_ROW:C_BLK].rearrange("p (o h) -> p o h", o=1).to_broadcast([P, E, 2])
            link(v.tensor_tensor(used[:, :, :], per_expert(pad[:, :], 2), r2, ALU.is_gt))
            link(v.tensor_tensor(inside[:, :, :], per_expert(start[:, :], 2), r2, ALU.add))
            link(v.tensor_tensor(outside[:, :, :], per_expert(tail[:, :], 2), r2, ALU.add))
            link(v.tensor_tensor(inside[:, :, :], inside[:, :, :], outside[:, :, :], ALU.subtract))
            link(v.tensor_tensor(inside[:, :, :], inside[:, :, :], used[:, :, :], ALU.mult))
            link(v.tensor_tensor(inside[:, :, :], inside[:, :, :], outside[:, :, :], ALU.add))
            link(v.tensor_copy(padpos[:, :], inside[:, :, :].rearrange("p e h -> p (e h)")))
            blk = cs[0:1, C_BLK:C_SEL].rearrange("p (i o) -> p i o", o=1).to_broadcast([1, NBLK, E])
            ends = nbe[0:1, :].rearrange("p (o e) -> p o e", o=1).to_broadcast([1, NBLK, E])
            link(v.tensor_tensor(bc[:, :, :], blk, ends, ALU.is_ge))
            link(v.tensor_reduce(be[:, :], bc[:, :, :], AX, ALU.add))
            link(v.tensor_scalar(be[:, :], be[:, :], float(E - 1), None, ALU.min))
            link(v.tensor_copy(blk_e[:, :], be[:, :]))

        @block.scalar
        def _(act):
            act.wait_ge(step, marks["diff"])
            nc.scalar.activation(ex[:, :], ex[:, :], ACT.Exp).then_inc(expd, 1)

        @block.tensor
        def _(pe):
            pe.wait_ge(step, marks["total"])
            nc.tensor.matmul(cnt[:, 0:E], less, total[:, :], start=True, stop=True)
            nc.tensor.matmul(cnt[:, E:2 * E], ones, total[:, :], start=True, stop=True).then_inc(counted, 1)


def attention_plan():
    units = [(c, h) for c in range(CPB) for h in range(QUAD)]
    plan, pending = [], []

    def scores(n):
        if n >= len(units):
            return []
        c, _ = units[n]
        return [("S", n, (t, k)) for t in range(TPC) for k in range(c + 1)]

    plan += scores(0) + scores(1) + [("M", 0, 0)]
    for n, (c, h) in enumerate(units):
        ahead = scores(n + 2)
        nkb = TPC * (c + 1)
        for kb in range(nkb):
            plan.append(("T", n, kb))
            a, z = kb * len(ahead) // nkb, (kb + 1) * len(ahead) // nkb
            plan += ahead[a:z]
            pending.append(("V", n, kb))
            if len(pending) > 3:
                plan.append(pending.pop(0))
            if kb == 2 and n + 1 < len(units):
                plan.append(("M", n + 1, 0))
            if kb == 5 and h == 0:
                plan.append(("F", c - 1, 0))
    plan += pending + [("F", CPB - 1, 0)]
    return units, plan


def attend(nc, scope, qk_d, v_d, xn_d, attn_d, xs_d, cmask, cmaskT, identb, cst, ident_sb, pos, padpos):
    f32, f32r, bf16 = mybir.dt.float32, mybir.dt.float32r, mybir.dt.bfloat16
    i32 = mybir.dt.int32
    ALU, ACT, AX = mybir.AluOpType, mybir.ActivationFunctionType, mybir.AxisListType.X
    units, plan = attention_plan()
    NU = len(units)
    NS = sum(k == "S" for k, _, _ in plan) + 2 * CPB
    NTS = sum(k in "TM" for k, _, _ in plan)
    NV = sum(k == "V" for k, _, _ in plan)
    SR, TR, PR = 3, 3, 6
    KQ = 3 * DH
    KM = KQ + 2
    with ExitStack() as ctx:
        sems = []
        sb, ps, sem = scope(ctx, "attend", sems)
        sem0 = scope(ctx, "attend_pool")[2]
        kt = [sb(f"k_rows{n}", [P, QUAD, T], f32r) for n in range(2)]
        qt = [sb(f"q_rows{n}", [P, QUAD, CH], f32r) for n in range(2)]
        vt = [sb(f"v_blocks{n}", [P, NT // B, P], f32) for n in range(2)]
        pt = sb("probsT", [P, PR, CH], f32)
        o_ev = sb("o_partial", [P, QUAD, CH], f32)
        z_ev = sb("z_partial", [P, QUAD, CH], f32)
        rz = sb("reciprocal_sums", [P, CH], f32)
        ot = sb("attn_out", [P, CPB, CH], f32)
        mx = sb("piece_max", [P, 2, TPC, CPB], f32)
        m4 = sb("row_max", [P, 2, TPC], f32)
        mneg = [sb(f"neg_max_parts{n}", [P, TPC, KM], f32r) for n in range(2)]
        mask, maskT, idb = sb("mask", [P, P], bf16), sb("maskT", [P, P], bf16), sb("identity_bf16", [P, P], bf16)
        idr = sb("identity_f32r", [P, P], f32r)
        ones = sb("ones", [P, DH], f32)
        zb = sb("zeros", [P, CH], bf16)
        sel = sb("selector", [P, DH], f32)
        xrow = [sb(f"xn_tile{n}", [P, D], f32) for n in range(2)]
        place = [sb(f"row_index{n}", [P, 2], i32) for n in range(2)]
        zero = sb("zero_rows", [P, D], f32)

        sp_ = [ps(f"s_psum{n}") for n in range(SR)]
        tp_ = [ps(f"t_psum{n}") for n in range(TR)]
        o_ps, z_ps = ps("o_psum"), ps("z_psum")

        cst_in, set_up = sem("constants_in"), sem("set_up")
        kv_in, q_in = [sem(f"kv_in{n}") for n in range(2)], [sem(f"q_in{n}") for n in range(2)]
        s_full, s_used = sem("s_full"), sem("s_used")
        t_full, t_used = sem("t_full"), sem("t_used")
        v_done = sem("v_done")
        mx_done, m4_done, mh_done, m_done = sem("piece_max_done"), sem("row_max_done"), sem("neg_high"), sem("neg_low")
        o_cp, z_cp, f_done, rz_done = sem("o_copied"), sem("z_copied"), sem("final_sums_read"), sem("reciprocal_done")
        ot_done, ot_out = sem("attn_out_done"), sem("attn_stored")
        q_used, kv_used = sem("q_used"), sem("kv_used")
        idx_in, zeroed = sem("index_in"), sem("zeroed")
        x_in, sc_out = [sem0(f"xn_tile_in{n}") for n in range(2)], [sem0(f"scattered{n}") for n in range(2)]
        pads_out = sem0("pads_out")
        passed = sem("passed")
        moved_on = sem("moved_on")
        block = ctx.enter_context(nc.Block())

        def first_kb(c):
            return TPC * c

        @block.sync
        def _(sp):
            for s in sems:
                sp.sem_inc(s, UP)
            for dst, src in ((mask, cmask), (maskT, cmaskT), (idb, identb)):
                sp.dma_start(dst[:, :], src).then_inc(cst_in, 16)
            sp.dma_start(sel[:, :], cst[:, C_SEL:C_ALL]).then_inc(cst_in, 16)

            def load_kv(it, n):
                heads = bass.ds(it * QUAD, QUAD)
                for rows, part in ((0, 0), (1, 1), (2, 0)):
                    sp.dma_start(kt[n][rows * DH:(rows + 1) * DH, :, :].bitcast(f32),
                                 qk_d[1][heads, part, :, :].rearrange("h d t -> d h t")).then_inc(kv_in[n], 16)
                sp.dma_start(vt[n][:, :, :], v_of(it)).then_inc(kv_in[n], 16)

            def v_of(it):
                base = v_d.rearrange("(k p) f -> p k f", p=P)
                return base[:, bass.ds((it // NG) * (T // P), T // P), bass.ds((it % NG) * P, P)]

            def load_q(it, c):
                heads = bass.ds(it * QUAD, QUAD)
                for rows, part in ((0, 0), (1, 0), (2, 1)):
                    sp.dma_start(qt[c % 2][rows * DH:(rows + 1) * DH, :, :].bitcast(f32),
                                 qk_d[0][heads, part, :, c * CH:(c + 1) * CH].rearrange("h d t -> d h t"))\
                      .then_inc(q_in[c % 2], 16)

            load_kv(0, 0)
            load_q(0, 0)
            load_q(0, 1)
            with sp.Fori(0, NIT // 2) as i:
                for n in range(2):
                    it = 2 * i + n
                    nxt = (it + 1) % NIT
                    for c in range(CPB):
                        sp.wait_ge(q_used, it * CPB + c + 1 + UP)
                        sp.sem_inc(moved_on, 1)
                        if c == 2:
                            sp.wait_ge(kv_used, it + UP)
                            sp.sem_inc(moved_on, 1)
                            load_kv(nxt, 1 - n)
                        load_q(it if c < 2 else nxt, (c + 2) % CPB)
                        sp.wait_ge(ot_done, it * CPB + c + 1 + UP)
                        sp.sem_inc(moved_on, 1)
                        sp.dma_start(attn_d[bass.ds(it, 1), :, c * CH:(c + 1) * CH].rearrange("o p t -> (o p) t"),
                                     ot[:, c, :]).then_inc(ot_out, 16)
            sp.wait_ge(ot_out, NIT * CPB * 16 + UP)
            for n in range(2):
                sp.wait_ge(kv_in[n], (NIT // 2 + (n == 0)) * 64 + UP)
                sp.wait_ge(q_in[n], (NIT * 2 + 1) * 48 + UP)

        @block.gpsimd
        def _(pool):
            nc.gpsimd.memset(zero[:, :], 0.0).then_inc(zeroed, 1)
            pool.wait_ge(zeroed, 1 + UP)
            for n in range(2 * E):
                nc.gpsimd.indirect_dma_start(xs_d[:, :], bass.IndirectOffsetOnAxis(ap=padpos[:, n:n + 1], axis=0),
                                             zero[:, :], None, bounds_check=NSLOT - 1).then_inc(pads_out, 16)
            with pool.Fori(0, NT // 2) as i:
                for n in range(2):
                    tile = 2 * i + n
                    pool.dma_start(xrow[n][:, :], xn_d[bass.ds(tile * P, P), :]).then_inc(x_in[n], 16)
                    nc.gpsimd.tensor_copy(place[n][:, :], pos[:, :, bass.ds(tile, 1)].rearrange("p c o -> p (c o)"))\
                        .then_inc(idx_in, 1)
                    pool.wait_ge(idx_in, tile + 1 + UP)
                    pool.wait_ge(x_in[n], (i + 1) * 16)
                    pool.sem_inc(passed, 1)
                    for m in range(2):
                        nc.gpsimd.indirect_dma_start(xs_d[:, :],
                                                     bass.IndirectOffsetOnAxis(ap=place[n][:, m:m + 1], axis=0),
                                                     xrow[n][:, :], None, bounds_check=NSLOT - 1)\
                            .then_inc(sc_out[n], 16)
                for n in range(2):
                    pool.wait_ge(sc_out[n], (i + 1) * 32)
                    pool.sem_inc(passed, 1)
            pool.wait_ge(pads_out, 2 * E * 16)

        @block.vector
        def _(dve):
            nc.vector.memset(ones[:, :], 1.0).then_inc(set_up, 1)
            nc.vector.memset(zb[:, :], 0.0).then_inc(set_up, 1)
            nc.vector.tensor_copy(idr[:, :], ident_sb[:, :]).then_inc(set_up, 1)
            for n in range(2):
                nc.vector.memset(mneg[n][:, :, :].bitcast(f32), 0.0).then_inc(set_up, 1)
                nc.vector.memset(kt[n][KQ:KM, :, :].bitcast(f32), 1.0).then_inc(set_up, 1)
            dve.wait_ge(set_up, 7 + UP)
            with dve.Fori(0, NIT // 2) as i:
                for half in range(2):
                    it = 2 * i + half
                    ns = nt = 0
                    m_slot = {}
                    for kind, n, k in plan:
                        if kind == "S":
                            c = units[n][0]
                            t, piece = k
                            w = CH if piece < c else (t + 1) * P
                            dve.wait_ge(s_full, it * NS + ns + 1 + UP)
                            nc.vector.tensor_reduce(mx[:, n % 2, t, piece:piece + 1], sp_[ns % SR][:, 0:w], AX, ALU.max)\
                                .then_inc(s_used, 1)
                            ns += 1
                            if (t, piece) == (TPC - 1, c):
                                dve.wait_ge(s_used, it * NS + ns + SR + UP)
                                nc.vector.tensor_reduce(m4[:, n % 2, :], mx[:, n % 2, :, 0:c + 1], AX, ALU.max)\
                                    .then_inc(m4_done, 1)
                                dve.wait_ge(m4_done, it * NU + n + 1 + UP)
                                if n >= 2:
                                    dve.wait_ge(t_full, it * NTS + m_slot[n - 2] + 1 + UP)
                                nc.vector.tensor_scalar(mneg[n % 2][:, :, KQ], m4[:, n % 2, :], -1.0, None, ALU.mult)\
                                    .then_inc(mh_done, 1)
                                dve.wait_ge(mh_done, it * NU + n + 1 + UP)
                                nc.vector.scalar_tensor_tensor(
                                    out=mneg[n % 2][:, :, KQ + 1], in0=m4[:, n % 2, :], scalar=-1.0,
                                    in1=mneg[n % 2][:, :, KQ].bitcast(f32), op0=ALU.mult, op1=ALU.subtract)\
                                    .then_inc(m_done, 1)
                        elif kind in "TM":
                            if kind == "M":
                                m_slot[n] = nt
                            nt += 1
                        elif kind == "V" and k == TPC * (units[n][0] + 1) - 1:
                            c, h = units[n]
                            dve.wait_ge(v_done, it * NV + sum(TPC * (u[0] + 1) for u in units[:n + 1]) + PR + UP)
                            if h == 0:
                                dve.wait_ge(f_done, it * CPB + c + UP)
                            nc.vector.tensor_copy(z_ev[:, h, :], z_ps[:, :]).then_inc(z_cp, 1)
                        elif kind == "F":
                            c = n
                            dve.wait_ge(s_full, it * NS + ns + 1 + UP)
                            nc.vector.reciprocal(rz[:, :], sp_[ns % SR][:, :]).then_inc(rz_done, 1)
                            dve.wait_ge(rz_done, it * CPB + c + 1 + UP)
                            dve.sem_inc(s_used, 1)
                            dve.wait_ge(ot_out, it * CPB * 16 + UP)
                            dve.wait_ge(s_full, it * NS + ns + 2 + UP)
                            nc.vector.tensor_tensor(ot[:, c, :], sp_[(ns + 1) % SR][:, :], rz[:, :], ALU.mult)\
                                .then_inc(ot_done, 1)
                            dve.wait_ge(ot_done, it * CPB + c + 1 + UP)
                            dve.sem_inc(s_used, 1)
                            ns += 2

        @block.scalar
        def _(act):
            with act.Fori(0, NIT // 2) as i:
                for half in range(2):
                    it = 2 * i + half
                    nt = nv = 0
                    for kind, n, k in plan:
                        if kind == "T":
                            c = units[n][0]
                            off = max(0, k - first_kb(c)) * P
                            act.wait_ge(v_done, it * NV + max(nv + 1, PR) + UP)
                            act.wait_ge(t_full, it * NTS + nt + 1 + UP)
                            nc.scalar.activation(pt[:, nv % PR, 0:CH - off], tp_[nt % TR][:, 0:CH - off], ACT.Exp,
                                                 scale=SCALE).then_inc(t_used, 1)
                            nt, nv = nt + 1, nv + 1
                        elif kind == "M":
                            c, h = units[n]
                            act.wait_ge(t_full, it * NTS + nt + 1 + UP)
                            nc.scalar.activation(qt[c % 2][KQ:KM, h, :], tp_[nt % TR][KQ:KM, :], ACT.Copy)\
                                .then_inc(t_used, 1)
                            nt += 1
                        elif kind == "V" and k == TPC * (units[n][0] + 1) - 1:
                            c, h = units[n]
                            act.wait_ge(v_done, it * NV + sum(TPC * (u[0] + 1) for u in units[:n + 1]) + PR + UP)
                            if h == 0:
                                act.wait_ge(f_done, it * CPB + c + UP)
                            nc.scalar.activation(o_ev[:, h, :], o_ps[:, :], ACT.Copy).then_inc(o_cp, 1)

        @block.tensor
        def _(pe):
            pe.sem_inc(s_used, SR)
            pe.sem_inc(t_used, TR)
            pe.sem_inc(v_done, PR)
            pe.wait_ge(cst_in, 4 * 16 + UP)
            pe.wait_ge(set_up, 7 + UP)
            with pe.Fori(0, NIT // 2) as i:
                for half in range(2):
                    it = 2 * i + half
                    ns = nt = nv = 0
                    slot = {}
                    seen_q = set()
                    pe.wait_ge(kv_in[half], (i + 1) * 64 + UP)
                    for kind, n, k in plan:
                        c, h = units[n] if kind != "F" else (n, 0)
                        kk, qq, vv = kt[half], qt[c % 2], vt[half]
                        if kind == "S":
                            t, piece = k
                            if c not in seen_q:
                                seen_q.add(c)
                                pe.wait_ge(q_in[c % 2], (it * 2 + c // 2 + 1) * 48 + UP)
                            w = CH if piece < c else (t + 1) * P
                            pe.wait_ge(s_used, it * NS + max(ns + 1, SR) + UP)
                            dst = sp_[ns % SR]
                            if piece == c:
                                nc.tensor.matmul(dst[:, w - P:w], idb[:, :], mask[:, :], start=True, stop=False,
                                                 skip_group_check=True)
                            nc.tensor.matmul(dst[:, 0:w], qq[0:KQ, h, t * P:(t + 1) * P],
                                             kk[0:KQ, h, piece * CH:piece * CH + w], start=piece < c, stop=True,
                                             skip_group_check=True).then_inc(s_full, 1)
                            ns += 1
                        elif kind == "M":
                            pe.wait_ge(m_done, it * NU + n + 1 + UP)
                            pe.wait_ge(t_used, it * NTS + max(nt + 1, TR) + UP)
                            for t in range(TPC):
                                last = nc.tensor.matmul(tp_[nt % TR][0:KM, t * P:(t + 1) * P], mneg[n % 2][:, t, :],
                                                        idr[:, :], start=True, stop=True)
                            last.then_inc(t_full, 1)
                            slot["M", n] = nt
                            nt += 1
                        elif kind == "T":
                            if k == 0:
                                pe.wait_ge(t_used, it * NTS + slot["M", n] + 1 + TR + UP)
                            pe.wait_ge(t_used, it * NTS + max(nt + 1, TR) + UP)
                            off = max(0, k - first_kb(c)) * P
                            dst = tp_[nt % TR]
                            diag = k >= first_kb(c)
                            if diag:
                                nc.tensor.matmul(dst[:, 0:P], idb[:, :], maskT[:, :], start=True, stop=False,
                                                 skip_group_check=True)
                            nc.tensor.matmul(dst[:, 0:CH - off], kk[0:KM, h, k * P:(k + 1) * P],
                                             qq[0:KM, h, off:CH], start=not diag, stop=True,
                                             skip_group_check=True).then_inc(t_full, 1)
                            slot["T", n, k] = (nt, nv)
                            nt, nv = nt + 1, nv + 1
                            if h == QUAD - 1 and k == TPC * (c + 1) - 1:
                                pe.wait_ge(t_full, it * NTS + nt + UP)
                                pe.sem_inc(q_used, 1)
                        elif kind == "V":
                            st, sv = slot["T", n, k]
                            pe.wait_ge(t_used, it * NTS + st + 1 + TR + UP)
                            if k == 0:
                                pe.wait_ge(o_cp, it * NU + n + UP)
                                pe.wait_ge(z_cp, it * NU + n + UP)
                            off = max(0, k - first_kb(c)) * P
                            g = k % QUAD
                            g2 = (g + 2) % QUAD
                            nkb = TPC * (c + 1)
                            if k == 0 and c == 0:
                                for dst in (o_ps, z_ps):
                                    nc.tensor.matmul(dst[:, :], zb[:, 0:P], zb[:, :], start=True, stop=False,
                                                     skip_group_check=True)
                            first = c > 0 and k < QUAD
                            nc.tensor.matmul(o_ps[g * DH:(g + 1) * DH, off:CH], vv[:, k, h * DH:(h + 1) * DH],
                                             pt[:, sv % PR, 0:CH - off], start=first, stop=k >= nkb - QUAD,
                                             skip_group_check=True)
                            nc.tensor.matmul(z_ps[g2 * DH:(g2 + 1) * DH, off:CH], ones[:, :],
                                             pt[:, sv % PR, 0:CH - off], start=first, stop=k >= nkb - QUAD,
                                             skip_group_check=True).then_inc(v_done, 1)
                        else:
                            pe.wait_ge(o_cp, it * NU + (c + 1) * QUAD + UP)
                            pe.wait_ge(z_cp, it * NU + (c + 1) * QUAD + UP)
                            for src in (z_ev, o_ev):
                                pe.wait_ge(s_used, it * NS + max(ns + 1, SR) + UP)
                                for hh in range(QUAD):
                                    last = nc.tensor.matmul(sp_[ns % SR][hh * DH:(hh + 1) * DH, :], sel[:, :],
                                                            src[:, hh, :], start=True, stop=True)
                                last.then_inc(s_full, 1)
                                ns += 1
                            pe.wait_ge(s_full, it * NS + ns + UP)
                            pe.sem_inc(f_done, 1)
                            if c == CPB - 1:
                                pe.sem_inc(kv_used, 1)


def experts(nc, scope, wg, wu, wd, xs_d, ys_d, ident_sb, blk_e):
    f32, f32r = mybir.dt.float32, mybir.dt.float32r
    ALU, ACT = mybir.AluOpType, mybir.ActivationFunctionType
    RT = BLK // P
    PARTS = 3 * KD
    PPF = PARTS // KD
    with ExitStack() as ctx:
        sems = []
        sb, ps, sem = scope(ctx, "experts", sems)
        raw = sb("raw", [P, 3, KD, D], f32)
        wp = [[sb(f"weights{n}_part{m}", [P, 3, KD, D], f32r) for m in range(2)] for n in range(2)]
        xr = [sb(f"x_rows{n}", [P, RT, D], f32) for n in range(2)]
        xT = [[sb(f"xT{n}_part{m}", [P, KD, BLK], f32r) for m in range(2)] for n in range(2)]
        gate = [sb(f"gate{n}", [P, BLK], f32) for n in range(2)]
        hid = sb("hidden", [P, KD, BLK], f32)
        hp = [[sb(f"hidden{n}_part{m}", [P, KD, BLK], f32r) for m in range(2)] for n in range(2)]
        y = [sb(f"y_rows{n}", [P, RT, D], f32) for n in range(2)]
        tps = [ps(f"x_psum{n}") for n in range(2)]
        gps, ups = [ps(f"gate_psum{n}") for n in range(2)], [ps(f"up_psum{n}") for n in range(2)]
        yps = [ps(f"y_psum{n}") for n in range(2)]

        w_in, x_in = [sem(f"w{m}_in") for m in range(3)], [sem(f"x_in{n}") for n in range(2)]
        w_hi, w_lo = sem("w_high"), sem("w_low")
        tr, x_hi, x_lo = sem("transposes"), sem("xT_high"), sem("xT_low")
        gu, g_act, h_mul = sem("gate_up_full"), sem("gate_done"), sem("hidden_done")
        h_hi, h_lo = sem("hidden_high"), sem("hidden_low")
        y_full, y_cp, y_out = sem("y_full"), sem("y_copied"), [sem(f"y_out{n}") for n in range(2)]
        moved_on = sem("moved_on")
        block = ctx.enter_context(nc.Block())
        weights = [w.rearrange("e (k p) f -> p e k f", p=P) for w in (wg, wu, wd)]

        @block.sync
        def _(sp):
            for s in sems:
                sp.sem_inc(s, UP)

            def load_weights(b, m):
                e = sp.value_load(blk_e[0:1, bass.ds(b, 1)], min_val=0, max_val=E - 1)
                sp.dma_start(raw[:, m, :, :], weights[m][:, bass.ds(e, 1), :, :].rearrange("p e k f -> p (e k) f"))\
                  .then_inc(w_in[m], 16)

            def load_rows(b, n):
                sp.dma_start(xr[n][:, :, :], xs_d[bass.ds(b * BLK, BLK), :].rearrange("(t p) d -> p t d", p=P))\
                  .then_inc(x_in[n], 16)

            for m in range(3):
                load_weights(0, m)
            load_rows(0, 0)
            with sp.Fori(0, NBLK // 2) as i:
                for n in range(2):
                    b = 2 * i + n
                    nxt = (b + 1) % NBLK
                    sp.wait_ge(tr, b * 2 + UP)
                    sp.sem_inc(moved_on, 1)
                    load_rows(nxt, 1 - n)
                    for m in range(3):
                        sp.wait_ge(w_lo, b * PARTS + (m + 1) * KD + UP)
                        sp.sem_inc(moved_on, 1)
                        load_weights(nxt, m)
            for m in range(3):
                sp.wait_ge(w_in[m], (NBLK + 1) * 16 + UP)
            sp.wait_ge(x_in[0], (NBLK // 2 + 1) * 16 + UP)

        def high_part(act, b, n, q):
            m, k = q // KD, q % KD
            if k == 0:
                act.wait_ge(w_in[m], (b + 1) * 16 + UP)
            nc.scalar.activation(wp[n][0][:, m, k, :], raw[:, m, k, :], ACT.Copy).then_inc(w_hi, 1)

        def low_part(dve, b, n, q):
            m, k = q // KD, q % KD
            dve.wait_ge(w_hi, b * PARTS + q + 1 + UP)
            nc.vector.tensor_tensor(wp[n][1][:, m, k, :], raw[:, m, k, :], wp[n][0][:, m, k, :].bitcast(f32),
                                    ALU.subtract).then_inc(w_lo, 1)

        def rows_high(act, b, n):
            for h in range(2):
                act.wait_ge(tr, b * 2 + h + 1 + UP)
                nc.scalar.activation(xT[n][0][:, 2 * h:2 * h + 2, :], tps[h][:, :], ACT.Copy).then_inc(x_hi, 1)

        def rows_low(dve, b, n):
            for h in range(2):
                dve.wait_ge(x_hi, b * 2 + h + 1 + UP)
                nc.vector.tensor_tensor(xT[n][1][:, 2 * h:2 * h + 2, :], tps[h][:, :],
                                        xT[n][0][:, 2 * h:2 * h + 2, :].bitcast(f32), ALU.subtract).then_inc(x_lo, 1)

        @block.gpsimd
        def _(pool):
            with pool.Fori(0, NBLK // 2) as i:
                for n in range(2):
                    b = 2 * i + n
                    for k in range(KD):
                        pool.wait_ge(h_hi, b * KD + k + 1 + UP)
                        nc.gpsimd.tensor_tensor(hp[n][1][:, k, :], hid[:, k, :], hp[n][0][:, k, :].bitcast(f32),
                                                ALU.subtract).then_inc(h_lo, 1)

        @block.vector
        def _(dve):
            for q in range(PARTS):
                low_part(dve, 0, 0, q)
            rows_low(dve, 0, 0)
            with dve.Fori(0, NBLK // 2) as i:
                for n in range(2):
                    b = 2 * i + n
                    dve.wait_ge(h_lo, b * KD + UP)
                    for f in range(KD):
                        dve.wait_ge(g_act, b * KD + f + 1 + UP)
                        nc.vector.tensor_tensor(hid[:, f, :], ups[f % 2][:, 0:BLK], gate[f % 2][:, :], ALU.mult)\
                            .then_inc(h_mul, 1)
                        if f < KD - 1:
                            for q in range(f * PPF, (f + 1) * PPF):
                                low_part(dve, b + 1, 1 - n, q)
                        if f == KD - 2:
                            rows_low(dve, b + 1, 1 - n)
                    for q in range(PARTS - PPF, PARTS):
                        low_part(dve, b + 1, 1 - n, q)

        @block.scalar
        def _(act):
            for q in range(PARTS):
                high_part(act, 0, 0, q)
            rows_high(act, 0, 0)
            with act.Fori(0, NBLK // 2) as i:
                for n in range(2):
                    b = 2 * i + n
                    act.wait_ge(y_full, b * RT + UP)
                    for f in range(KD):
                        act.wait_ge(gu, b * KD + f + 1 + UP)
                        nc.scalar.activation(gate[f % 2][:, :], gps[f % 2][:, 0:BLK], ACT.Silu).then_inc(g_act, 1)
                        if f < KD - 1:
                            high_part(act, b + 1, 1 - n, f * PPF)
                        act.wait_ge(h_mul, b * KD + f + 1 + UP)
                        nc.scalar.activation(hp[n][0][:, f, :], hid[:, f, :], ACT.Copy).then_inc(h_hi, 1)
                        if f < KD - 1:
                            for q in range(f * PPF + 1, (f + 1) * PPF):
                                high_part(act, b + 1, 1 - n, q)
                        if f == KD - 2:
                            rows_high(act, b + 1, 1 - n)
                    for q in range(PARTS - PPF, PARTS):
                        high_part(act, b + 1, 1 - n, q)
                    act.wait_ge(y_out[n], i * 16 + UP)
                    for t in range(RT):
                        act.wait_ge(y_full, b * RT + t + 1 + UP)
                        nc.scalar.activation(y[n][:, t, :], yps[t % 2][:, :], ACT.Copy).then_inc(y_cp, 1)
                    act.wait_ge(y_cp, (b + 1) * RT + UP)
                    act.dma_start(ys_d[bass.ds(b * BLK, BLK), :].rearrange("(t p) d -> p t d", p=P), y[n][:, :, :])\
                       .then_inc(y_out[n], 16)
            for n in range(2):
                act.wait_ge(y_out[n], NBLK // 2 * 16 + UP)

        @block.tensor
        def _(pe):
            def turn(b, n, count):
                pe.wait_ge(x_in[n], count * 16 + UP)
                pe.wait_ge(x_lo, b * 2 + UP)
                for k in range(KD):
                    for t in range(RT):
                        col = (k % 2) * BLK + t * P
                        last = nc.tensor.transpose(tps[k // 2][:, col:col + P],
                                                   xr[n][:, t, k * P:(k + 1) * P], ident_sb[:, :])
                    if k % 2:
                        last.then_inc(tr, 1)

            turn(0, 0, 1)
            with pe.Fori(0, NBLK // 2) as i:
                for n in range(2):
                    b = 2 * i + n
                    pe.wait_ge(x_lo, (b + 1) * 2 + UP)
                    pe.wait_ge(w_lo, b * PARTS + 2 * KD + UP)
                    for f in range(KD):
                        pe.wait_ge(h_mul, b * KD + (f - 1 if f >= 2 else 0) + UP)
                        for m, dst in ((0, gps[f % 2]), (1, ups[f % 2])):
                            for s, (k, (a, w2)) in enumerate([(k, p) for k in range(KD) for p in PASSES]):
                                last = nc.tensor.matmul(dst[:, 0:BLK], wp[n][w2][:, m, k, f * P:(f + 1) * P],
                                                        xT[n][a][:, k, :], start=s == 0, stop=s == 3 * KD - 1)
                        last.then_inc(gu, 1)
                        if f == KD - 2:
                            turn(b + 1, 1 - n, i + 1 + n)
                    pe.wait_ge(w_lo, (b + 1) * PARTS + UP)
                    pe.wait_ge(y_cp, b * RT + UP)
                    for ks in (range(KD - 1), range(KD - 1, KD)):
                        for t in range(RT):
                            for k in ks:
                                if t == 0:
                                    pe.wait_ge(h_lo, b * KD + k + 1 + UP)
                                for s, (a, w2) in enumerate(PASSES):
                                    last = nc.tensor.matmul(yps[t][:, :], hp[n][a][:, k, t * P:(t + 1) * P],
                                                            wp[n][w2][:, 2, k, :], start=k == 0 and s == 0,
                                                            stop=k == KD - 1 and s == len(PASSES) - 1)
                            if k == KD - 1:
                                last.then_inc(y_full, 1)


def combine(nc, scope, x, woutT, attn_d, ys_d, pos, wts, out):
    f32, i32 = mybir.dt.float32, mybir.dt.int32
    ALU, ACT = mybir.AluOpType, mybir.ActivationFunctionType
    with ExitStack() as ctx:
        sems = []
        sb, ps, sem = scope(ctx, "combine", sems)
        sem0 = scope(ctx, "combine_pool")[2]
        wo = sb("wo", [P, NG, D], f32)
        at = [sb(f"attn_chunk{n}", [P, NG, CH], f32) for n in range(2)]
        xr = [sb(f"x_chunk{n}", [P, TPC, D], f32) for n in range(2)]
        y1 = [sb(f"first_choice{n}", [P, TPC, D], f32) for n in range(2)]
        y2 = [sb(f"second_choice{n}", [P, TPC, D], f32) for n in range(2)]
        gate = [sb(f"moe_gate{n}", [P, TPC, D], f32) for n in range(2)]
        res = [sb(f"result{n}", [P, TPC, D], f32) for n in range(2)]
        ix = [sb(f"row_index{n}", [P, 2, TPC], i32) for n in range(2)]
        wt = [sb(f"weights{n}", [P, 2, TPC], f32) for n in range(2)]
        sps = [ps(f"s_psum{n}") for n in range(TPC)]
        w_in = sem("wo_in")
        in_ = [sem(f"chunk_in{n}") for n in range(2)]
        passed = sem("passed")
        idx, got = sem("index_copied"), [sem0(f"gathered{n}") for n in range(2)]
        wt_cp, y_w, mix, act_d, s_full, s_mul, add = (sem("weights_copied"), sem("weighted"), sem("mixed"), sem("gated"),
                                                      sem("s_full"), sem("s_times_gate"), sem("added"))
        o_out = [sem(f"out_stored{n}") for n in range(2)]
        moved_on = sem("moved_on")
        block = ctx.enter_context(nc.Block())

        @block.sync
        def _(sp):
            for s in sems:
                sp.sem_inc(s, UP)
            sp.dma_start(wo[:, :, :], woutT.rearrange("(k p) o -> p k o", p=P)).then_inc(w_in, 16)
            with sp.Fori(0, NCH // 2) as i:
                for n in range(2):
                    c = 2 * i + n
                    sp.wait_ge(s_full, (c - n if n == 0 else c - 1) * TPC + UP)
                    sp.wait_ge(add, (c - n if n == 0 else c - 1) * TPC + UP)
                    sp.sem_inc(moved_on, 1)
                    batch, at_t = c // CPB, (c % CPB) * CH
                    sp.dma_start(at[n][:, :, :], attn_d[bass.ds(batch * NG, NG), :, bass.ds(at_t, CH)]
                                 .rearrange("g p t -> p g t")).then_inc(in_[n], 16)
                    sp.dma_start(xr[n][:, :, :], x[bass.ds(c * CH, CH), :].rearrange("(t p) d -> p t d", p=P))\
                      .then_inc(in_[n], 16)

        @block.gpsimd
        def _(pool):
            with pool.Fori(0, NCH // 2) as i:
                for n in range(2):
                    c = 2 * i + n
                    pool.wait_ge(mix, (c - n if n == 0 else c - 1) * TPC + UP)
                    nc.gpsimd.tensor_copy(ix[n][:, :, :], pos[:, :, bass.ds(c * TPC, TPC)]).then_inc(idx, 1)
                    pool.wait_ge(idx, c + 1 + UP)
                    pool.sem_inc(passed, 1)
                    for t in range(TPC):
                        for m, y in ((0, y1), (1, y2)):
                            nc.gpsimd.indirect_dma_start(y[n][:, t, :], None, ys_d[:, :],
                                                         bass.IndirectOffsetOnAxis(ap=ix[n][:, m, t:t + 1], axis=0),
                                                         bounds_check=NSLOT - 1).then_inc(got[n], 16)

        @block.vector
        def _(dve):
            with dve.Fori(0, NCH // 2) as i:
                for n in range(2):
                    c = 2 * i + n
                    nc.vector.tensor_copy(wt[n][:, :, :], wts[:, :, bass.ds(c * TPC, TPC)]).then_inc(wt_cp, 1)
                    dve.wait_ge(wt_cp, c + 1 + UP)
                    dve.wait_ge(got[n], (i + 1) * 2 * TPC * 16)
                    for t in range(TPC):
                        nc.vector.tensor_scalar(y1[n][:, t, :], y1[n][:, t, :], wt[n][:, 0, t:t + 1], None,
                                                ALU.mult).then_inc(y_w, 1)
                    for t in range(TPC):
                        dve.wait_ge(y_w, c * TPC + t + 1 + UP)
                        nc.vector.scalar_tensor_tensor(out=gate[n][:, t, :], in0=y2[n][:, t, :],
                                                       scalar=wt[n][:, 1, t:t + 1], in1=y1[n][:, t, :],
                                                       op0=ALU.mult, op1=ALU.add).then_inc(mix, 1)
                    dve.wait_ge(in_[n], (i + 1) * 32 + UP)
                    dve.wait_ge(o_out[n], i * 16 + UP)
                    for t in range(TPC):
                        dve.wait_ge(act_d, c * TPC + t + 1 + UP)
                        dve.wait_ge(s_full, c * TPC + t + 1 + UP)
                        nc.vector.tensor_tensor(res[n][:, t, :], sps[t][:, :], gate[n][:, t, :], ALU.mult)\
                            .then_inc(s_mul, 1)
                    for t in range(TPC):
                        dve.wait_ge(s_mul, c * TPC + t + 1 + UP)
                        nc.vector.tensor_tensor(res[n][:, t, :], res[n][:, t, :], xr[n][:, t, :], ALU.add)\
                            .then_inc(add, 1)

        @block.scalar
        def _(act):
            with act.Fori(0, NCH // 2) as i:
                for n in range(2):
                    c = 2 * i + n
                    for t in range(TPC):
                        act.wait_ge(mix, c * TPC + t + 1 + UP)
                        nc.scalar.activation(gate[n][:, t, :], gate[n][:, t, :], ACT.Silu).then_inc(act_d, 1)
                    act.wait_ge(add, (c + 1) * TPC + UP)
                    act.dma_start(out[bass.ds(c * CH, CH), :].rearrange("(t p) d -> p t d", p=P), res[n][:, :, :])\
                       .then_inc(o_out[n], 16)
            for n in range(2):
                act.wait_ge(o_out[n], NCH // 2 * 16 + UP)

        @block.tensor
        def _(pe):
            pe.wait_ge(w_in, 16 + UP)
            with pe.Fori(0, NCH // 2) as i:
                for n in range(2):
                    c = 2 * i + n
                    pe.wait_ge(in_[n], (i + 1) * 32 + UP)
                    for t in range(TPC):
                        pe.wait_ge(s_mul, c * TPC + UP)
                        for k in range(NG):
                            last = nc.tensor.matmul(sps[t][:, :], at[n][:, k, t * P:(t + 1) * P], wo[:, k, :],
                                                    start=k == 0, stop=k == NG - 1)
                        last.then_inc(s_full, 1)


def kernel(L0_attn_x, L0_attn_W_qkv, L0_attn_W_out, L0_ffn_router_w, L0_ffn_router_b, L0_ffn_we_gate,
           L0_ffn_we_up, L0_ffn_we_down):
    import ml_dtypes
    import numpy as np
    from concourse import bacc
    from concourse.bass_utils import run_bass_kernel_spmd

    def arr(a):
        return np.asarray(a)

    wt = arr(L0_attn_W_qkv).T
    qk = wt[:, :2 * D].reshape(D, 2, 2, H // 2, DH // 2, 2).transpose(0, 1, 2, 5, 3, 4).reshape(D, 2 * D)
    wqkvT = np.ascontiguousarray(np.concatenate([qk, wt[:, 2 * D:]], axis=1))
    freqs = (1.0 / np.float32(10000.0) ** (np.arange(0, DH, 2, dtype=np.float32) / np.float32(DH))).astype(np.float32)
    angles = np.outer(np.arange(T, dtype=np.float32), freqs).astype(np.float32)
    cos = np.ascontiguousarray(np.tile(np.cos(angles).T, (H // 2, 1)))
    sin = np.ascontiguousarray(np.tile(np.sin(angles).T, (H // 2, 1)))
    r = np.arange(P)
    bf = ml_dtypes.bfloat16
    arrays = {
        "x": arr(L0_attn_x).reshape(NTOK, D),
        "wqkvT": wqkvT,
        "woutT": np.ascontiguousarray(arr(L0_attn_W_out).T),
        "rwT": arr(L0_ffn_router_w),
        "rb": arr(L0_ffn_router_b).reshape(E, 1),
        "wg": arr(L0_ffn_we_gate),
        "wu": arr(L0_ffn_we_up),
        "wd": arr(L0_ffn_we_down),
        "cos": cos,
        "sin": sin,
        "cmask": np.where(r[None, :] > r[:, None], NEG, 0).astype(bf),
        "cmaskT": np.where(r[:, None] > r[None, :], NEG, 0).astype(bf),
        "identb": np.eye(P).astype(bf),
        "ident": np.eye(P, dtype=np.float32),
        "cst": constants(),
    }
    nc = bacc.Bacc("TRN2", target_bir_lowering=False, num_devices=1)
    args, maps = [], {}
    for name, a in arrays.items():
        maps["in_" + name] = a
        args.append(nc.dram_tensor("in_" + name, a.shape, mybir.dt.from_np(a.dtype), kind="ExternalInput").ap())
    res = nc.dram_tensor("out_rows", (NTOK, D), mybir.dt.float32, kind="ExternalOutput").ap()
    build(nc, *args, res)
    r = run_bass_kernel_spmd(nc, [maps], core_ids=[0])
    return r.results[0]["out_rows"].reshape(B, T, D)
```

```python
import concourse.bass as bass
from concourse import mybir
from contextlib import ExitStack

B, T, D = 4, 2048, 512
H, DH = 16, 32
E = 8
P = 128
NTOK = B * T
KD = D // P
CH = 512
TPC = CH // P
NCH = NTOK // CH
CPB = T // CH
NT = NTOK // P
QUAD = P // DH
NG = H // QUAD
NIT = B * NG
BLK = 256
NBLK = 2 * NTOK // BLK + E
NSLOT = NBLK * BLK
PADS = NSLOT - 2 * NTOK
RB = NTOK // BLK
NEG = -1.0e30
SCALE = 1.0 / float(DH) ** 0.5
EPS = 1e-5
UP = 1
PASSES = ((0, 0), (0, 1), (1, 0))


def build(nc, x, wqkvT, woutT, rwT, rb, wg, wu, wd, cos, sin, cmask, cmaskT, identb, ident, cst, out):
    f32, f32r, bf16 = mybir.dt.float32, mybir.dt.float32r, mybir.dt.bfloat16
    i32, u32 = mybir.dt.int32, mybir.dt.uint32
    ALU, ACT, AX = mybir.AluOpType, mybir.ActivationFunctionType, mybir.AxisListType.X

    def dram(name, shape, dt):
        return nc.dram_tensor(name, shape, dt, kind="Internal").ap()

    qk_d = [dram("qT_parts", (B * H, 2, DH, T), f32), dram("kT_parts", (B * H, 2, DH, T), f32)]
    v_d = dram("v_rows", (NTOK, D), f32)
    xn_d = dram("xn_rows", (NTOK, D), f32)
    attn_d = dram("attnT", (NIT, P, T), f32)
    xs_d = dram("sorted_rows", (NSLOT, D), f32)
    ys_d = dram("expert_rows", (NSLOT, D), f32)

    top = ExitStack()

    def scope(ctx, stage, sems=None):
        def sb(name, shape, dt):
            return ctx.enter_context(nc.sbuf_tensor(f"{stage}_{name}", shape, dt))

        def ps(name):
            return ctx.enter_context(nc.psum_tensor(f"{stage}_{name}", [P, 512], f32))

        def sem(name):
            s = ctx.enter_context(nc.semaphore(f"{stage}_{name}"))
            if sems is not None:
                sems.append(s)
            return s
        return sb, ps, sem

    with top:
        sb, _, _ = scope(top, "kept")
        ident_sb = sb("ident_sb", [P, P], f32)
        logits = sb("logits", [P, NT, E], f32)
        pos = sb("pos", [P, 2, NT], i32)
        wts = sb("wts", [P, 2, NT], f32)
        padpos = sb("padpos", [P, 2 * E], i32)
        blk_e = sb("blk_e", [1, NBLK], i32)

        project(nc, scope, x, wqkvT, rwT, rb, cos, sin, ident, ident_sb, logits, qk_d, v_d, xn_d)
        route(nc, scope, cst, ident_sb, logits, pos, wts, padpos, blk_e)
        attend(nc, scope, qk_d, v_d, xn_d, attn_d, xs_d, cmask, cmaskT, identb, cst, ident_sb, pos, padpos)
        experts(nc, scope, wg, wu, wd, xs_d, ys_d, ident_sb, blk_e)
        combine(nc, scope, x, woutT, attn_d, ys_d, pos, wts, out)


def project(nc, scope, x, wqkvT, rwT, rb, cos, sin, ident, ident_sb, logits, qk_d, v_d, xn_d):
    f32, f32r = mybir.dt.float32, mybir.dt.float32r
    ALU, ACT = mybir.AluOpType, mybir.ActivationFunctionType
    OC = 3 * D
    with ExitStack() as ctx:
        sems = []
        sb, ps, sem = scope(ctx, "project", sems)
        w = [sb(f"w_part{n}", [P, KD, OC], f32r) for n in range(2)]
        rw = [sb(f"rw_part{n}", [P, KD, E], f32r) for n in range(2)]
        rb_sb = sb("rb_sb", [E, 1], f32)
        cos_sb = sb("cos_sb", [P, T], f32)
        sin_sb = sb("sin_sb", [P, T], f32)
        with ExitStack() as c2:
            sb2, _, sem2 = scope(c2, "split")
            wraw = sb2("wraw", [P, KD, OC], f32)
            rwraw = sb2("rwraw", [P, KD, E], f32)
            loaded, high = sem2("weights_loaded"), sem2("weights_high")
            low = sem2("weights_low")
            block = c2.enter_context(nc.Block())

            @block.sync
            def _(sp):
                sp.dma_start(wraw[:, :, :], wqkvT.rearrange("(k p) o -> p k o", p=P)).then_inc(loaded, 16)
                sp.dma_start(rwraw[:, :, :], rwT.rearrange("(k p) e -> p k e", p=P)).then_inc(loaded, 16)
                sp.dma_start(rb_sb[:, :], rb).then_inc(loaded, 16)
                sp.dma_start(cos_sb[:, :], cos).then_inc(loaded, 16)
                sp.dma_start(sin_sb[:, :], sin).then_inc(loaded, 16)
                sp.dma_start(ident_sb[:, :], ident).then_inc(loaded, 16)

            @block.vector
            def _(dve):
                dve.wait_ge(loaded, 6 * 16)
                nc.vector.tensor_copy(rw[0][:, :, :], rwraw[:, :, :]).then_inc(high, 1)
                for k in range(KD):
                    nc.vector.tensor_copy(w[0][:, k, :], wraw[:, k, :]).then_inc(high, 1)
                dve.wait_ge(high, 1)
                nc.vector.tensor_tensor(rw[1][:, :, :], rwraw[:, :, :], rw[0][:, :, :].bitcast(f32),
                                        ALU.subtract).then_inc(low, 1)
                for k in range(KD):
                    dve.wait_ge(high, k + 2)
                    nc.vector.tensor_tensor(w[1][:, k, :], wraw[:, k, :], w[0][:, k, :].bitcast(f32),
                                            ALU.subtract).then_inc(low, 1)
                dve.wait_ge(low, KD + 1)

        xin = [sb(f"xin{n}", [P, TPC, D], f32) for n in range(2)]
        xn = [sb(f"xn{n}", [P, TPC, D], f32) for n in range(2)]
        stats = sb("stats", [P, 2, TPC, 6], f32)
        mv = sb("mv", [P, 2, TPC, 2], f32)
        std = sb("std", [P, 2, TPC], f32)
        rstd = sb("rstd", [P, 2, TPC], f32)
        eps = sb("eps", [P, 1], f32)
        xT = [[sb(f"xT{n}_part{m}", [P, KD, CH], f32r) for m in range(2)] for n in range(2)]
        prod = sb("rope_products", [P, 2, 2, CH], f32)
        rot = sb("rotated", [P, 2, CH], f32)
        rot_p = [sb(f"rotated_part{m}", [P, 2, 2, CH], f32r) for m in range(2)]
        v_sb = sb("v_sb", [P, TPC, D], f32)
        lt = sb("logitsT", [E, 2, CH], f32)

        tp = [ps(f"transposed{n}") for n in range(2)]
        qkp = [ps(f"qk_half{n}") for n in range(4)]
        vp = [ps(f"v_psum{n}") for n in range(2)]

        x_in, x_free = [sem(f"x_in{n}") for n in range(2)], sem("x_free")
        bn, agg, stdd, rs, normed = sem("bn"), sem("agg"), sem("stdd"), sem("rs"), sem("normed")
        eps_set = sem("eps_set")
        passed = sem("passed")
        xn_out = [sem(f"xn_out{n}") for n in range(2)]
        tr, t_hi, t_lo = sem("transposes"), sem("xT_high"), sem("xT_low")
        qk_full, v_full, rt_full = sem("qk_full"), sem("v_full"), sem("router_full")
        prods, rots, r_hi, r_lo = sem("products"), sem("rotations"), sem("rot_high"), sem("rot_low")
        qk_out = [sem(f"qk_out{n}") for n in range(2)]
        v_cp, v_out, lt_cp, lg_cp = sem("v_copied"), sem("v_out"), sem("lt_copied"), sem("logits_copied")
        moved_on = sem("moved_on")
        block = ctx.enter_context(nc.Block())

        NPAIR = 4

        @block.sync
        def _(sp):
            for s in sems:
                sp.sem_inc(s, UP)
            with sp.Fori(0, B) as b:
                for j in range(CPB):
                    c, n = b * CPB + j, j % 2
                    rows = x[bass.ds(c * CH, CH), :].rearrange("(t p) d -> p t d", p=P)
                    if j < 2:
                        sp.wait_ge(normed, c * TPC - (j) * TPC + UP)
                        sp.sem_inc(moved_on, 1)
                    else:
                        sp.wait_ge(normed, (c - 1) * TPC + UP)
                        sp.sem_inc(moved_on, 1)
                    sp.dma_start(xin[n][:, :, :], rows).then_inc(x_in[n], 16)

        @block.vector
        def _(dve):
            nc.vector.memset(eps[:, :], EPS).then_inc(eps_set, 1)
            with dve.Fori(0, B) as b:
                for j in range(CPB):
                    c, n = b * CPB + j, j % 2
                    dve.wait_ge(x_in[n], (b * 2 + j // 2 + 1) * 16 + UP)
                    for t in range(TPC):
                        nc.vector.bn_stats(stats[:, n, t, :], xin[n][:, t, :]).then_inc(bn, 1)
                    dve.wait_ge(bn, (c + 1) * TPC + UP)
                    dve.sem_inc(passed, 1)
                    for t in range(TPC):
                        nc.vector.bn_aggr(mv[:, n, t, :], stats[:, n, t, :]).then_inc(agg, 1)
                    dve.wait_ge(stdd, c + 1 + UP)
                    nc.vector.reciprocal(rstd[:, n, :], std[:, n, :]).then_inc(rs, 1)
                    dve.wait_ge(rs, c + 1 + UP)
                    dve.wait_ge(xn_out[n], (b * 2 + j // 2) * 16 + UP)
                    if j >= 2:
                        dve.wait_ge(tr, (c - 1) * KD + UP)
                    else:
                        dve.wait_ge(tr, (c - j) * KD + UP)
                    for t in range(TPC):
                        nc.vector.tensor_scalar(xn[n][:, t, :], xin[n][:, t, :], mv[:, n, t, 0:1],
                                                rstd[:, n, t:t + 1], ALU.subtract, ALU.mult).then_inc(normed, 1)
                    if j >= 2:
                        dve.wait_ge(qk_full, (c - 1) * 2 * NPAIR + UP)
                    else:
                        dve.wait_ge(qk_full, (c - j) * 2 * NPAIR + UP)
                    for k in range(KD):
                        dve.wait_ge(t_hi, c * KD + k + 1 + UP)
                        nc.vector.tensor_tensor(xT[n][1][:, k, :], tp[k % 2][:, :], xT[n][0][:, k, :].bitcast(f32),
                                                ALU.subtract).then_inc(t_lo, 1)
                    dve.wait_ge(rt_full, 2 * c + 2 + UP)
                    nc.vector.tensor_copy(logits[:, bass.ds(c * TPC, TPC), :],
                                          vp[0][:, 0:TPC * E].rearrange("p (t e) -> p t e", e=E)).then_inc(lg_cp, 1)
                    cs, sn = cos_sb[:, j * CH:(j + 1) * CH], sin_sb[:, j * CH:(j + 1) * CH]
                    for r in range(NPAIR):
                        a, bb = qkp[2 * (r % 2)], qkp[2 * (r % 2) + 1]
                        dve.wait_ge(rots, (c * NPAIR + r) * 2 + UP)
                        dve.wait_ge(qk_full, (c * NPAIR + r) * 2 + 1 + UP)
                        nc.vector.tensor_tensor(prod[:, 0, 0, :], a[:, :], cs, ALU.mult).then_inc(prods, 1)
                        nc.vector.tensor_tensor(prod[:, 0, 1, :], a[:, :], sn, ALU.mult).then_inc(prods, 1)
                        dve.wait_ge(qk_full, (c * NPAIR + r) * 2 + 2 + UP)
                        nc.vector.tensor_tensor(prod[:, 1, 0, :], bb[:, :], sn, ALU.mult).then_inc(prods, 1)
                        nc.vector.tensor_tensor(prod[:, 1, 1, :], bb[:, :], cs, ALU.mult).then_inc(prods, 1)

        @block.gpsimd
        def _(pool):
            with pool.Fori(0, B) as b:
                for j in range(CPB):
                    c = b * CPB + j
                    for r in range(NPAIR):
                        q, m = c * NPAIR + r, r % 2
                        pool.wait_ge(r_hi, q * 2 + UP)
                        pool.wait_ge(r_lo, q * 2 + UP)
                        pool.wait_ge(prods, q * 4 + 3 + UP)
                        nc.gpsimd.tensor_tensor(rot[:, 0, :], prod[:, 0, 0, :], prod[:, 1, 0, :],
                                                ALU.subtract).then_inc(rots, 1)
                        pool.wait_ge(prods, q * 4 + 4 + UP)
                        nc.gpsimd.tensor_tensor(rot[:, 1, :], prod[:, 0, 1, :], prod[:, 1, 1, :],
                                                ALU.add).then_inc(rots, 1)
                        for h in range(2):
                            pool.wait_ge(r_hi, q * 2 + h + 1 + UP)
                            nc.gpsimd.tensor_tensor(rot_p[1][:, m, h, :], rot[:, h, :],
                                                    rot_p[0][:, m, h, :].bitcast(f32), ALU.subtract).then_inc(r_lo, 1)

        @block.scalar
        def _(act):
            act.wait_ge(eps_set, 1 + UP)
            with act.Fori(0, B) as b:
                for j in range(CPB):
                    c, n = b * CPB + j, j % 2
                    act.wait_ge(agg, (c + 1) * TPC + UP)
                    nc.scalar.activation(std[:, n, :], mv[:, n, :, 1], ACT.Sqrt, bias=eps[:, 0:1]).then_inc(stdd, 1)
                    act.wait_ge(normed, (c + 1) * TPC + UP)
                    act.dma_start(xn_d[bass.ds(c * CH, CH), :].rearrange("(t p) d -> p t d", p=P),
                                  xn[n][:, :, :]).then_inc(xn_out[n], 16)
                    if j >= 2:
                        act.wait_ge(qk_full, (c - 1) * 2 * NPAIR + UP)
                    else:
                        act.wait_ge(qk_full, (c - j) * 2 * NPAIR + UP)
                    for k in range(KD):
                        act.wait_ge(tr, c * KD + k + 1 + UP)
                        nc.scalar.activation(xT[n][0][:, k, :], tp[k % 2][:, :], ACT.Copy).then_inc(t_hi, 1)
                    act.wait_ge(rt_full, 2 * c + 1 + UP)
                    nc.scalar.activation(lt[:, n, :], vp[0][0:E, :], ACT.Identity, bias=rb_sb[:, 0:1]).then_inc(lt_cp, 1)
                    act.wait_ge(v_out, c * 16 + UP)
                    for t in range(TPC):
                        act.wait_ge(v_full, c * TPC + t + 1 + UP)
                        nc.scalar.activation(v_sb[:, t, :], vp[(t + 1) % 2][:, :], ACT.Copy).then_inc(v_cp, 1)
                    act.wait_ge(v_cp, (c + 1) * TPC + UP)
                    act.dma_start(v_d[bass.ds(c * CH, CH), :].rearrange("(t p) d -> p t d", p=P),
                                  v_sb[:, :, :]).then_inc(v_out, 16)
                    for r in range(NPAIR):
                        q, m = c * NPAIR + r, r % 2
                        act.wait_ge(qk_out[m], (c * 2 + r // 2) * 64 + UP)
                        for h in range(2):
                            act.wait_ge(rots, q * 2 + h + 1 + UP)
                            nc.scalar.activation(rot_p[0][:, m, h, :], rot[:, h, :], ACT.Copy).then_inc(r_hi, 1)
                        act.wait_ge(r_hi, q * 2 + 2 + UP)
                        act.wait_ge(r_lo, q * 2 + 2 + UP)
                        z, g = r // 2, r % 2
                        for part in range(2):
                            for h in range(2):
                                dst = qk_d[z][bass.ds(b * H + g * (H // 2), H // 2), part,
                                              h * (DH // 2):(h + 1) * (DH // 2), j * CH:(j + 1) * CH]
                                act.dma_start(dst, rot_p[part][:, m, h, :].bitcast(f32)).then_inc(qk_out[m], 16)
            act.wait_ge(v_out, NCH * 16 + UP)
            for m in range(2):
                act.wait_ge(xn_out[m], NCH // 2 * 16 + UP)
                act.wait_ge(qk_out[m], NCH * 2 * 64 + UP)

        @block.tensor
        def _(pe):
            with pe.Fori(0, B) as b:
                for j in range(CPB):
                    c, n = b * CPB + j, j % 2
                    for k in range(KD):
                        if k == 0:
                            pe.wait_ge(normed, (c + 1) * TPC + UP)
                        if k < 2:
                            pe.wait_ge(t_lo, c * KD + UP)
                        else:
                            pe.wait_ge(t_lo, c * KD + k - 1 + UP)
                        for t in range(TPC):
                            last = nc.tensor.transpose(tp[k % 2][:, t * P:(t + 1) * P],
                                                       xn[n][:, t, k * P:(k + 1) * P], ident_sb[:, :])
                        last.then_inc(tr, 1)
                    pe.wait_ge(t_lo, (c + 1) * KD + UP)
                    pe.wait_ge(v_cp, c * TPC + UP)
                    for m, (k, (a, w2)) in enumerate([(k, p) for k in range(KD) for p in PASSES]):
                        last = nc.tensor.matmul(vp[0][0:E, :], rw[w2][:, k, :], xT[n][a][:, k, :],
                                                start=m == 0, stop=m == 3 * KD - 1)
                    last.then_inc(rt_full, 1)
                    for t in range(TPC):
                        bank = (t + 1) % 2
                        if t == 1:
                            pe.wait_ge(lt_cp, c + 1 + UP)
                            pe.sem_inc(passed, 1)
                            for u in range(TPC):
                                last = nc.tensor.transpose(vp[0][:, u * E:(u + 1) * E],
                                                           lt[:, n, u * P:(u + 1) * P], ident_sb[0:E, 0:E])
                            last.then_inc(rt_full, 1)
                            pe.wait_ge(lg_cp, c + 1 + UP)
                        if t >= 2:
                            pe.wait_ge(v_cp, c * TPC + t - 1 + UP)
                        for m, (k, (a, w2)) in enumerate([(k, p) for k in range(KD) for p in PASSES]):
                            last = nc.tensor.matmul(vp[bank][:, :], xT[n][a][:, k, t * P:(t + 1) * P],
                                                    w[w2][:, k, 2 * D:3 * D], start=m == 0, stop=m == 3 * KD - 1)
                        last.then_inc(v_full, 1)
                    for r in range(NPAIR):
                        for h in range(2):
                            pe.wait_ge(prods, (c * NPAIR + (r - 1 if r >= 2 else 0)) * 4 + UP)
                            col = (2 * r + h) * P
                            for m, (k, (a, w2)) in enumerate([(k, p) for k in range(KD) for p in PASSES]):
                                last = nc.tensor.matmul(qkp[2 * (r % 2) + h][:, :], w[w2][:, k, col:col + P],
                                                        xT[n][a][:, k, :], start=m == 0, stop=m == 3 * KD - 1)
                            last.then_inc(qk_full, 1)


C_IOTA = 0
C_RUN = C_IOTA + E
C_LESS = C_RUN + E * NT
C_ONE = C_LESS + P
C_THR = C_ONE + P
C_ROW = C_THR + RB
C_BLK = C_ROW + 2
C_SEL = C_BLK + NBLK
C_ALL = C_SEL + DH


def constants():
    import numpy as np
    c = np.zeros((P, C_ALL), np.float32)
    p = np.arange(P)
    c[:, C_IOTA:C_IOTA + E] = np.arange(E) - E
    run = np.ones((E, NT), np.float32)
    run[:, 0] = 0
    c[:, C_RUN:C_LESS] = run.reshape(-1)
    c[:, C_LESS:C_ONE] = p[:, None] < p[None, :]
    c[:, C_ONE:C_THR] = 1
    c[:, C_THR:C_ROW] = BLK * np.arange(RB)
    c[:, C_ROW:C_BLK] = p[:, None] + P * np.arange(2)
    c[:, C_BLK:C_SEL] = np.arange(NBLK)
    c[:, C_SEL:C_ALL] = (p[:, None] % DH) == np.arange(DH)
    return c


def route(nc, scope, cst, ident_sb, logits, pos, wts, padpos, blk_e):
    f32 = mybir.dt.float32
    ALU, ACT, AX = mybir.AluOpType, mybir.ActivationFunctionType, mybir.AxisListType.X
    with ExitStack() as ctx:
        sb, ps, sem = scope(ctx, "route")
        cs = sb("consts", [P, C_ALL], f32)
        t3 = sb("tmp3", [P, NT, E], f32)
        m3 = sb("masked_logits", [P, NT, E], f32)
        hot = [sb(f"onehot{n}", [P, NT, E], f32) for n in range(2)]
        best = sb("best", [P, 2, NT], f32)
        idx = sb("first_index", [P, NT], f32)
        ex = sb("exp_difference", [P, NT], f32)
        both = sb("chosen", [P, E, NT], f32)
        upto = sb("chosen_up_to", [P, E, NT], f32)
        row = sb("row_of_choice", [P, E, NT], f32)
        total = sb("partition_total", [P, E], f32)
        over = sb("blocks_over", [P, E, RB], f32)
        nb = sb("blocks", [P, E], f32)
        nbe = sb("blocks_up_to", [P, E], f32)
        start = sb("first_row", [P, E], f32)
        tot = sb("expert_total", [P, E], f32)
        pad = sb("pads", [P, E], f32)
        rest = sb("rest", [P, E], f32)
        rest_to = sb("rest_up_to", [P, E], f32)
        tail = sb("tail_base", [P, E], f32)
        inside = sb("pad_inside", [P, E, 2], f32)
        used = sb("pad_used", [P, E, 2], f32)
        outside = sb("pad_outside", [P, E, 2], f32)
        posf = sb("row_float", [P, 2, NT], f32)
        bc = sb("block_compare", [1, NBLK, E], f32)
        be = sb("block_expert", [1, NBLK], f32)
        cnt = ps("count_psum")
        got, step, counted, expd = sem("constants_in"), sem("dve_step"), sem("counted"), sem("exp_done")
        moved_on = sem("moved_on")
        block = ctx.enter_context(nc.Block())
        less, ones = cs[:, C_LESS:C_ONE], cs[:, C_ONE:C_THR]

        def per_expert(ap, n):
            return ap.rearrange("p (e o) -> p e o", o=1).to_broadcast([P, E, n])

        @block.sync
        def _(sp):
            sp.dma_start(cs[:, :], cst).then_inc(got, 16)

        marks = {}

        @block.vector
        def _(dve):
            done = [0]

            def link(ins):
                done[0] += 1
                ins.then_inc(step, 1)
                dve.wait_ge(step, done[0])

            v = nc.vector
            iota = cs[:, C_IOTA:C_RUN].rearrange("p (o e) -> p o e", o=1).to_broadcast([P, NT, E])
            dve.wait_ge(got, 16)
            for n, src in enumerate((logits, m3)):
                link(v.tensor_reduce(best[:, n, :], src[:, :, :], AX, ALU.max))
                top = best[:, n, :].rearrange("p (t o) -> p t o", o=1).to_broadcast([P, NT, E])
                link(v.tensor_tensor(t3[:, :, :], src[:, :, :], top, ALU.is_equal))
                link(v.scalar_tensor_tensor(out=t3[:, :, :], in0=t3[:, :, :], scalar=-float(E), in1=iota,
                                            op0=ALU.mult, op1=ALU.add))
                link(v.tensor_reduce(idx[:, :], t3[:, :, :], AX, ALU.min))
                link(v.tensor_scalar(idx[:, :], idx[:, :], float(E), None, ALU.add))
                first = idx[:, :].rearrange("p (t o) -> p t o", o=1).to_broadcast([P, NT, E])
                link(v.tensor_tensor(hot[n][:, :, :], iota, first, ALU.is_equal))
                if n == 0:
                    link(v.scalar_tensor_tensor(out=m3[:, :, :], in0=hot[0][:, :, :], scalar=-3.0e38,
                                                in1=logits[:, :, :], op0=ALU.mult, op1=ALU.add))
            link(v.tensor_tensor(ex[:, :], best[:, 1, :], best[:, 0, :], ALU.subtract))
            marks["diff"] = done[0]
            dve.wait_ge(expd, 1)
            link(v.tensor_scalar(wts[:, 1, :], ex[:, :], 1.0, None, ALU.add))
            link(v.reciprocal(wts[:, 0, :], wts[:, 1, :]))
            link(v.tensor_tensor(wts[:, 1, :], ex[:, :], wts[:, 0, :], ALU.mult))
            link(v.tensor_tensor(both[:, :, :].rearrange("p e t -> p t e"), hot[0][:, :, :], hot[1][:, :, :],
                                 ALU.add))
            link(v.tensor_tensor_scan(upto[:, :, :].rearrange("p e t -> p (e t)"), cs[:, C_RUN:C_LESS],
                                      both[:, :, :].rearrange("p e t -> p (e t)"), 0.0, ALU.mult, ALU.add))
            link(v.tensor_copy(total[:, :], upto[:, :, NT - 1]))
            marks["total"] = done[0]
            dve.wait_ge(counted, 1)
            link(v.tensor_copy(tot[:, :], cnt[:, E:2 * E]))
            thr = cs[:, C_THR:C_ROW].rearrange("p (o k) -> p o k", o=1).to_broadcast([P, E, RB])
            link(v.tensor_tensor(over[:, :, :], per_expert(tot[:, :], RB), thr, ALU.is_gt))
            link(v.tensor_reduce(nb[:, :], over[:, :, :], AX, ALU.add))
            link(v.tensor_tensor_scan(nbe[:, :], ones[:, 0:E], nb[:, :], 0.0, ALU.mult, ALU.add))
            link(v.tensor_tensor(start[:, :], nbe[:, :], nb[:, :], ALU.subtract))
            link(v.tensor_scalar(start[:, :], start[:, :], float(BLK), None, ALU.mult))
            link(v.tensor_tensor(row[:, :, :], upto[:, :, :], both[:, :, :], ALU.subtract))
            link(v.tensor_tensor(rest[:, :], start[:, :], cnt[:, 0:E], ALU.add))
            link(v.tensor_tensor(row[:, :, :], row[:, :, :], per_expert(rest[:, :], NT), ALU.add))
            for n in range(2):
                link(v.tensor_tensor(t3[:, :, :], hot[n][:, :, :], row[:, :, :].rearrange("p e t -> p t e"),
                                     ALU.mult))
                link(v.tensor_reduce(posf[:, n, :], t3[:, :, :], AX, ALU.add))
            link(v.tensor_copy(pos[:, :, :], posf[:, :, :]))
            link(v.tensor_scalar(pad[:, :], nb[:, :], float(BLK), None, ALU.mult))
            link(v.tensor_tensor(pad[:, :], pad[:, :], tot[:, :], ALU.subtract))
            link(v.tensor_scalar(rest[:, :], pad[:, :], -1.0, float(BLK), ALU.mult, ALU.add))
            link(v.tensor_tensor_scan(rest_to[:, :], ones[:, 0:E], rest[:, :], 0.0, ALU.mult, ALU.add))
            link(v.tensor_tensor(tail[:, :], rest_to[:, :], rest[:, :], ALU.subtract))
            link(v.tensor_tensor(tail[:, :], tail[:, :], pad[:, :], ALU.subtract))
            link(v.tensor_scalar(rest[:, :], nbe[:, :], float(BLK), None, ALU.mult))
            link(v.tensor_scalar(tail[:, :], tail[:, :], rest[:, E - 1:E], None, ALU.add))
            link(v.tensor_tensor(start[:, :], start[:, :], tot[:, :], ALU.add))
            r2 = cs[:, C_ROW:C_BLK].rearrange("p (o h) -> p o h", o=1).to_broadcast([P, E, 2])
            link(v.tensor_tensor(used[:, :, :], per_expert(pad[:, :], 2), r2, ALU.is_gt))
            link(v.tensor_tensor(inside[:, :, :], per_expert(start[:, :], 2), r2, ALU.add))
            link(v.tensor_tensor(outside[:, :, :], per_expert(tail[:, :], 2), r2, ALU.add))
            link(v.tensor_tensor(inside[:, :, :], inside[:, :, :], outside[:, :, :], ALU.subtract))
            link(v.tensor_tensor(inside[:, :, :], inside[:, :, :], used[:, :, :], ALU.mult))
            link(v.tensor_tensor(inside[:, :, :], inside[:, :, :], outside[:, :, :], ALU.add))
            link(v.tensor_copy(padpos[:, :], inside[:, :, :].rearrange("p e h -> p (e h)")))
            blk = cs[0:1, C_BLK:C_SEL].rearrange("p (i o) -> p i o", o=1).to_broadcast([1, NBLK, E])
            ends = nbe[0:1, :].rearrange("p (o e) -> p o e", o=1).to_broadcast([1, NBLK, E])
            link(v.tensor_tensor(bc[:, :, :], blk, ends, ALU.is_ge))
            link(v.tensor_reduce(be[:, :], bc[:, :, :], AX, ALU.add))
            link(v.tensor_scalar(be[:, :], be[:, :], float(E - 1), None, ALU.min))
            link(v.tensor_copy(blk_e[:, :], be[:, :]))

        @block.scalar
        def _(act):
            act.wait_ge(step, marks["diff"])
            nc.scalar.activation(ex[:, :], ex[:, :], ACT.Exp).then_inc(expd, 1)

        @block.tensor
        def _(pe):
            pe.wait_ge(step, marks["total"])
            nc.tensor.matmul(cnt[:, 0:E], less, total[:, :], start=True, stop=True)
            nc.tensor.matmul(cnt[:, E:2 * E], ones, total[:, :], start=True, stop=True).then_inc(counted, 1)


def attention_plan():
    units = [(c, h) for c in range(CPB) for h in range(QUAD)]
    NU = len(units)
    plan, waiting = [], []
    clock = 0

    def scores(n):
        return [("S", n, (t, k)) for t in range(TPC) for k in range(units[n % NU][0] + 1)]

    def release(upto):
        for entry in sorted((w for w in waiting if w[0] <= upto), key=lambda w: w[0]):
            plan.extend(entry[1])
            waiting.remove(entry)

    for n, (c, h) in enumerate(units):
        ahead = scores(n + 2) if n + 1 < NU else []
        nkb = TPC * (c + 1)
        plan.append(("X", n, 0))
        for kb in range(nkb):
            plan.append(("T", n, kb))
            plan += ahead[kb * len(ahead) // nkb:(kb + 1) * len(ahead) // nkb]
            full = kb < TPC * c
            if full and kb % 2:
                plan.append(("A", n, kb // 2))
            if kb % 4 == 3:
                burst = [("V", n, k) for k in range(kb - 3, kb + 1)]
                if full:
                    waiting.append((clock + V_LAG, burst))
                    for m in range(2):
                        waiting.append((clock + Z_LAG + m, [("Z", n, kb // 2 - 1 + m)]))
                else:
                    burst += [("Z", n, 2 * c + d) for d in range(TPC)]
                    waiting.append((clock + V_LAG, burst))
                    waiting.append((clock + V_LAG + C_LAG, [("C", n, "o"), ("C", n, "z")]))
            release(clock)
            if kb == 2 and n + 1 < NU:
                plan.append(("M", n + 1, 0))
            if h == 0 and c and kb == 7:
                plan.append(("F", c - 1, 0))
            if h == 1 and c and kb < 4:
                plan.append(("R", c - 1, kb))
                if kb == 3:
                    plan.append(("O", c - 1, 0))
            clock += 1
    rest = scores(NU + 1)
    release(clock)
    plan += rest[:len(rest) // 2]
    release(clock + V_LAG)
    plan += rest[len(rest) // 2:]
    release(clock + 100)
    plan += [("R", CPB - 1, k) for k in range(4)] + [("F", CPB - 1, 0), ("M", NU, 0), ("O", CPB - 1, 0)]
    return units, scores(0) + scores(1) + [("M", 0, 0)], plan


V_LAG, Z_LAG, C_LAG = 2, 4, 0
def attend(nc, scope, qk_d, v_d, xn_d, attn_d, xs_d, cmask, cmaskT, identb, cst, ident_sb, pos, padpos):
    f32, f32r, bf16 = mybir.dt.float32, mybir.dt.float32r, mybir.dt.bfloat16
    i32 = mybir.dt.int32
    ALU, ACT, AX = mybir.AluOpType, mybir.ActivationFunctionType, mybir.AxisListType.X
    units, first, plan = attention_plan()
    SR, TR, PR, AR = 3, 3, 12, 4
    KQ = 3 * DH
    KM = KQ + 3
    FT = NT // NIT

    at, count = {}, {}
    for step in first + [step for step in plan if step[1] < len(units)]:
        ring = {"S": "s", "M": "t", "T": "t", "F": "t"}.get(step[0])
        for key in (step[0], ring):
            if key:
                at[key, step] = count.get(key, 0)
                count[key] = at[key, step] + 1
    NS, NTS, NV, NA, NZ, NU = count["s"], count["t"], count["T"], count["A"], count["Z"], len(units)

    def sums_of(n):
        return 2 * units[n][0] + TPC

    def steps(it, part):
        for kind, n, k in part:
            yield it + n // NU, (kind, n % NU, k)

    with ExitStack() as ctx:
        sems = []
        sb, ps, sem = scope(ctx, "attend", sems)
        sem0 = scope(ctx, "attend_pool")[2]
        kt = [sb(f"k_rows{n}", [P, QUAD, T], f32r) for n in range(2)]
        qt = [sb(f"q_rows{n}", [P, QUAD, CH], f32r) for n in range(2)]
        vt = [sb(f"v_blocks{n}", [P, NT // B, P], f32) for n in range(2)]
        pt = sb("probsT", [P, PR, CH], f32)
        pair = sb("prob_pairs", [P, AR, CH], f32)
        o_ev = sb("o_partial", [P, QUAD, CH], f32)
        of = sb("o_sum", [P, CH], f32)
        zf = sb("z_sum", [P, CPB, CH], f32)
        ot = sb("attn_out", [P, CPB, CH], f32)
        mx = sb("piece_max", [P, 2, TPC, CPB], f32)
        m4 = sb("row_max", [P, 2, TPC], f32)
        rest = sb("max_rest", [P, 2, TPC], f32)
        mneg = [sb(f"neg_max_parts{n}", [P, TPC, P], bf16) for n in range(2)]
        mask, maskT, idb = sb("mask", [P, P], bf16), sb("maskT", [P, P], bf16), sb("identity_bf16", [P, P], bf16)
        ones = sb("ones", [P, DH], f32)
        zb = sb("zeros", [P, CH], bf16)
        sel = sb("selector", [P, DH], f32)
        xrow = sb("xn_tile", [P, D], f32)
        place = sb("row_index", [P, 2], i32)
        pad_place = sb("pad_index", [P, 1], i32)
        zero = sb("zero_rows", [P, D], f32)

        sp_ = [ps(f"s_psum{n}") for n in range(SR)]
        tp_ = [ps(f"t_psum{n}") for n in range(TR)]
        o_ps, z_ps = ps("o_psum"), ps("z_psum")

        cst_in, set_up = sem("constants_in"), sem("set_up")
        kv_in, q_in = [sem(f"kv_in{n}") for n in range(2)], [sem(f"q_in{n}") for n in range(2)]
        s_full, s_used = sem("s_full"), sem("s_used")
        t_full, t_used = sem("t_full"), sem("t_used")
        v_done, z_done, paired = sem("v_done"), sem("z_done"), sem("paired")
        m4_done, m_hi, m_rest, m_mid, m_done = (sem("row_max_done"), sem("neg_max_high"), sem("neg_max_rest"),
                                                sem("neg_max_middle"), sem("neg_max_low"))
        o_cp, z_cp, inverted = sem("o_copied"), sem("z_copied"), sem("sums_inverted")
        ot_done, ot_out = sem("attn_out_done"), sem("attn_stored")
        idx_in, zeroed = sem("index_in"), sem("zeroed")
        x_in, sc_out, pads_out = sem0("xn_tile_in"), sem0("scattered"), sem0("pads_out")
        moved_on, passed = sem("moved_on"), sem("passed")
        block = ctx.enter_context(nc.Block())

        def after(it, per, step, key):
            return it * per + at[key, step] + 1 + UP

        def ring_free(it, per, index, size):
            return it * per + max(0, index - size + 1) + UP

        @block.sync
        def _(sp):
            for s in sems:
                sp.sem_inc(s, UP)
            sp.sem_inc(ot_done, CPB)
            for dst, src in ((mask, cmask), (maskT, cmaskT), (idb, identb)):
                sp.dma_start(dst[:, :], src).then_inc(cst_in, 16)
            sp.dma_start(sel[:, :], cst[:, C_SEL:C_ALL]).then_inc(cst_in, 16)

            def load_kv(it, n):
                heads = bass.ds(it * QUAD, QUAD)
                for rows, part in ((0, 0), (1, 1), (2, 0)):
                    sp.dma_start(kt[n][rows * DH:(rows + 1) * DH, :, :].bitcast(f32),
                                 qk_d[1][heads, part, :, :].rearrange("h d t -> d h t")).then_inc(kv_in[n], 16)
                rows_v = v_d.rearrange("(k p) f -> p k f", p=P)
                sp.dma_start(vt[n][:, :, :], rows_v[:, bass.ds((it // NG) * (T // P), T // P),
                                                    bass.ds((it % NG) * P, P)]).then_inc(kv_in[n], 16)

            def load_q(it, c):
                heads = bass.ds(it * QUAD, QUAD)
                for rows, part in ((0, 0), (1, 0), (2, 1)):
                    sp.dma_start(qt[c % 2][rows * DH:(rows + 1) * DH, :, :].bitcast(f32),
                                 qk_d[0][heads, part, :, c * CH:(c + 1) * CH].rearrange("h d t -> d h t"))\
                      .then_inc(q_in[c % 2], 16)

            load_kv(0, 0)
            load_q(0, 0)
            load_q(0, 1)
            with sp.Fori(0, NIT // 2) as i:
                for n in range(2):
                    it = 2 * i + n
                    nxt = (it + 1) % NIT
                    for c in range(CPB):
                        last = ("T", units.index((c, QUAD - 1)), TPC * (c + 1) - 1)
                        sp.wait_ge(t_full, after(it, NTS, last, "t"))
                        sp.sem_inc(moved_on, 1)
                        if c == 1:
                            sp.wait_ge(v_done, it * NV + UP)
                            sp.sem_inc(moved_on, 1)
                            load_kv(nxt, 1 - n)
                        load_q(it if c < 2 else nxt, (c + 2) % CPB)
                        sp.wait_ge(ot_done, (it + 1) * CPB + c + 1 + UP)
                        sp.sem_inc(moved_on, 1)
                        sp.dma_start(attn_d[bass.ds(it, 1), :, c * CH:(c + 1) * CH].rearrange("o p t -> (o p) t"),
                                     ot[:, c, :]).then_inc(ot_out, 16)
            sp.wait_ge(ot_out, NIT * CPB * 16 + UP)
            for n in range(2):
                sp.wait_ge(kv_in[n], (NIT // 2 + (n == 0)) * 64 + UP)
                sp.wait_ge(q_in[n], (NIT * 2 + 1) * 48 + UP)

        def sum_of_pair(index):
            _, n, k = next(s for s in plan if s[0] == "A" and at["A", s] == index)
            return "Z", n, k

        @block.gpsimd
        def _(pool):
            nc.gpsimd.memset(zero[:, :], 0.0).then_inc(zeroed, 1)
            pool.wait_ge(zeroed, 1 + UP)
            with pool.Fori(0, NIT) as it:
                for step in plan:
                    kind, n, k = step
                    if kind == "A":
                        a, b = at["T", ("T", n, 2 * k)], at["T", ("T", n, 2 * k + 1)]
                        mine = at["A", step]
                        pool.wait_ge(t_used, after(it, NTS, ("T", n, 2 * k + 1), "t"))
                        before = mine - AR
                        if before >= 0:
                            pool.wait_ge(z_done, after(it, NZ, sum_of_pair(before), "Z"))
                        else:
                            pool.wait_ge(z_done, it * NZ + UP)
                        nc.gpsimd.tensor_tensor(pair[:, mine % AR, :], pt[:, a % PR, :], pt[:, b % PR, :], ALU.add)\
                            .then_inc(paired, 1)
                    elif kind == "O":
                        pool.wait_ge(t_used, after(it, NTS, ("F", n, 0), "t"))
                        pool.wait_ge(inverted, (it * CPB + n + 1) * 4 + UP)
                        pool.wait_ge(ot_out, it * CPB * 16 + UP)
                        nc.gpsimd.tensor_tensor(ot[:, n, :], of[:, :], zf[:, n, :], ALU.mult).then_inc(ot_done, 1)
                    elif kind == "X":
                        tile, phase = it * FT + n // 4, n % 4
                        if phase == 0:
                            pool.dma_start(xrow[:, :], xn_d[bass.ds(tile * P, P), :]).then_inc(x_in, 16)
                            nc.gpsimd.tensor_copy(place[:, :],
                                                  pos[:, :, bass.ds(tile, 1)].rearrange("p c o -> p (c o)"))\
                                .then_inc(idx_in, 1)
                            if n == 0:
                                nc.gpsimd.tensor_copy(pad_place[:, :], padpos[:, bass.ds(it, 1)]).then_inc(idx_in, 1)
                        elif phase == 1:
                            pool.wait_ge(idx_in, it * (FT + 1) + n // 4 + 2 + UP)
                            pool.wait_ge(x_in, (tile + 1) * 16)
                            pool.sem_inc(passed, 1)
                            for m in range(2):
                                nc.gpsimd.indirect_dma_start(
                                    xs_d[:, :], bass.IndirectOffsetOnAxis(ap=place[:, m:m + 1], axis=0),
                                    xrow[:, :], None, bounds_check=NSLOT - 1).then_inc(sc_out, 16)
                            if n == 1:
                                nc.gpsimd.indirect_dma_start(
                                    xs_d[:, :], bass.IndirectOffsetOnAxis(ap=pad_place[:, 0:1], axis=0),
                                    zero[:, :], None, bounds_check=NSLOT - 1).then_inc(pads_out, 16)
                        elif phase == 3:
                            pool.wait_ge(sc_out, (tile + 1) * 32)
                            pool.sem_inc(passed, 1)
                            if n == 3:
                                pool.wait_ge(pads_out, (it + 1) * 16)
                                pool.sem_inc(passed, 1)

        @block.vector
        def _(dve):
            nc.vector.memset(ones[:, :], 1.0).then_inc(set_up, 1)
            nc.vector.memset(zb[:, :], 0.0).then_inc(set_up, 1)
            for n in range(2):
                nc.vector.memset(mneg[n][:, :, :], 0.0).then_inc(set_up, 1)
                nc.vector.memset(kt[n][KQ:KM, :, :].bitcast(f32), 1.0).then_inc(set_up, 1)
            dve.wait_ge(set_up, 6 + UP)

            def run(base, part):
                for it, step in steps(base, part):
                    kind, n, k = step
                    if kind == "S":
                        c = units[n][0]
                        t, piece = k
                        w = CH if piece < c else (t + 1) * P
                        dve.wait_ge(s_full, after(it, NS, step, "s"))
                        nc.vector.tensor_reduce(mx[:, n % 2, t, piece:piece + 1], sp_[at["s", step] % SR][:, 0:w],
                                                AX, ALU.max).then_inc(s_used, 1)
                        if (t, piece) != (TPC - 1, c):
                            continue
                        done = it * NU + n + 1 + UP
                        parts = mneg[n % 2]
                        dve.wait_ge(s_used, after(it, NS, step, "s"))
                        nc.vector.tensor_reduce(m4[:, n % 2, :], mx[:, n % 2, :, 0:c + 1], AX, ALU.max)\
                            .then_inc(m4_done, 1)
                        if n >= 2:
                            dve.wait_ge(t_full, after(it, NTS, ("M", n - 2, 0), "t"))
                        elif part is plan:
                            dve.wait_ge(t_full, after(it - 1, NTS, ("M", n - 2 + NU, 0), "t"))
                        dve.wait_ge(m4_done, done)
                        nc.vector.tensor_scalar(parts[:, :, KQ], m4[:, n % 2, :], -1.0, None, ALU.mult)\
                            .then_inc(m_hi, 1)
                        dve.wait_ge(m_hi, done)
                        nc.vector.scalar_tensor_tensor(out=rest[:, n % 2, :], in0=m4[:, n % 2, :], scalar=-1.0,
                                                       in1=parts[:, :, KQ], op0=ALU.mult, op1=ALU.subtract)\
                            .then_inc(m_rest, 1)
                        dve.wait_ge(m_rest, done)
                        nc.vector.tensor_copy(parts[:, :, KQ + 1], rest[:, n % 2, :]).then_inc(m_mid, 1)
                        dve.wait_ge(m_mid, done)
                        nc.vector.tensor_tensor(parts[:, :, KQ + 2], rest[:, n % 2, :], parts[:, :, KQ + 1],
                                                ALU.subtract).then_inc(m_done, 1)
                    elif kind == "R":
                        dve.wait_ge(z_cp, it * NU + (n + 1) * QUAD + UP)
                        cols = slice(k * P, (k + 1) * P)
                        nc.vector.reciprocal(zf[:, n, cols], zf[:, n, cols]).then_inc(inverted, 1)

            run(0, first)
            with dve.Fori(0, NIT) as i:
                run(i, plan)

        @block.scalar
        def _(act):
            def run(base, part):
                for it, step in steps(base, part):
                    kind, n, k = step
                    c = units[n][0]
                    if kind == "T":
                        nv = at["T", step]
                        off = max(0, k - TPC * c) * P
                        before = next((s for s in plan if s[0] == "T" and at["T", s] == nv - PR), None)
                        if before is None:
                            act.wait_ge(z_done, it * NZ + UP)
                        else:
                            _, bn, bk = before
                            full = TPC * units[bn][0]
                            act.wait_ge(v_done, after(it, NV, ("V", bn, bk), "V"))
                            if bk < full:
                                act.wait_ge(paired, after(it, NA, ("A", bn, bk // 2), "A"))
                            else:
                                act.wait_ge(z_done, after(it, NZ, ("Z", bn, full // 2 + bk - full), "Z"))
                        act.wait_ge(t_full, after(it, NTS, step, "t"))
                        nc.scalar.activation(pt[:, nv % PR, 0:CH - off], tp_[at["t", step] % TR][:, 0:CH - off],
                                             ACT.Exp, scale=SCALE).then_inc(t_used, 1)
                    elif kind == "M":
                        c, h = units[n]
                        act.wait_ge(t_full, after(it, NTS, step, "t"))
                        nc.scalar.activation(qt[c % 2][KQ:KM, h, :], tp_[at["t", step] % TR][KQ:KM, :], ACT.Copy)\
                            .then_inc(t_used, 1)
                    elif kind == "F":
                        act.wait_ge(ot_done, (it + 1) * CPB + n + UP)
                        act.wait_ge(t_full, after(it, NTS, step, "t"))
                        nc.scalar.activation(of[:, :], tp_[at["t", step] % TR][:, :], ACT.Copy).then_inc(t_used, 1)
                    elif kind == "C" and k == "o":
                        h = units[n][1]
                        if h == 0:
                            if c:
                                act.wait_ge(t_full, after(it, NTS, ("F", c - 1, 0), "t"))
                            else:
                                act.wait_ge(t_full, it * NTS + UP)
                        act.wait_ge(v_done, after(it, NV, ("V", n, TPC * (c + 1) - 1), "V"))
                        nc.scalar.activation(o_ev[:, h, :], o_ps[:, :], ACT.Copy).then_inc(o_cp, 1)
                    elif kind == "C":
                        h = units[n][1]
                        if h == 0:
                            act.wait_ge(ot_done, it * CPB + c + 1 + UP)
                        act.wait_ge(z_done, after(it, NZ, ("Z", n, sums_of(n) - 1), "Z"))
                        for t in range(TPC):
                            cols = slice(t * P, (t + 1) * P)
                            last = nc.scalar.activation(zf[h * DH:(h + 1) * DH, c, cols],
                                                        z_ps[t * DH:(t + 1) * DH, cols], ACT.Copy)
                        last.then_inc(z_cp, 1)

            run(0, first)
            with act.Fori(0, NIT) as i:
                run(i, plan)

        @block.tensor
        def _(pe):
            pe.wait_ge(cst_in, 4 * 16 + UP)
            pe.wait_ge(set_up, 6 + UP)
            def run(turns, half, part):
                for kind, n, k in part:
                    ahead, n = divmod(n, NU)
                    it, mine = 2 * turns + half + ahead, (half + ahead) % 2
                    kk, vv = kt[mine], vt[mine]
                    step = (kind, n, k)
                    c, h = units[n]
                    if kind == "S":
                        t, piece = k
                        if (t, piece, n) == (0, 0, 0):
                            pe.wait_ge(kv_in[mine], (turns + (half + ahead) // 2 + 1) * 64 + UP)
                        if (t, piece, h) == (0, 0, 0):
                            pe.wait_ge(q_in[c % 2], (it * 2 + c // 2 + 1) * 48 + UP)
                        w = CH if piece < c else (t + 1) * P
                        pe.wait_ge(s_used, ring_free(it, NS, at["s", step], SR))
                        dst = sp_[at["s", step] % SR]
                        if piece == c:
                            nc.tensor.matmul(dst[:, w - P:w], idb[:, :], mask[:, :], start=True, stop=False,
                                             skip_group_check=True)
                        nc.tensor.matmul(dst[:, 0:w], qt[c % 2][0:KQ, h, t * P:(t + 1) * P],
                                         kk[0:KQ, h, piece * CH:piece * CH + w], start=piece < c, stop=True,
                                         skip_group_check=True).then_inc(s_full, 1)
                    elif kind == "M":
                        pe.wait_ge(m_done, it * NU + n + 1 + UP)
                        pe.wait_ge(t_used, ring_free(it, NTS, at["t", step], TR))
                        for t in range(TPC):
                            last = nc.tensor.matmul(tp_[at["t", step] % TR][:, t * P:(t + 1) * P],
                                                    mneg[n % 2][:, t, :], idb[:, :], start=True, stop=True)
                        last.then_inc(t_full, 1)
                    elif kind == "T":
                        if k == 0:
                            pe.wait_ge(t_used, after(it, NTS, ("M", n, 0), "t"))
                        pe.wait_ge(t_used, ring_free(it, NTS, at["t", step], TR))
                        off = max(0, k - TPC * c) * P
                        dst = tp_[at["t", step] % TR]
                        diag = k >= TPC * c
                        if diag:
                            nc.tensor.matmul(dst[:, 0:P], idb[:, :], maskT[:, :], start=True, stop=False,
                                             skip_group_check=True)
                        nc.tensor.matmul(dst[:, 0:CH - off], kk[0:KM, h, k * P:(k + 1) * P],
                                         qt[c % 2][0:KM, h, off:CH], start=not diag, stop=True,
                                         skip_group_check=True).then_inc(t_full, 1)
                    elif kind == "V":
                        pe.wait_ge(t_used, after(it, NTS, ("T", n, k), "t"))
                        off = max(0, k - TPC * c) * P
                        g = k % QUAD
                        dst = o_ps
                        if k == 0:
                            pe.wait_ge(o_cp, it * NU + n + UP)
                            if c == 0:
                                nc.tensor.matmul(dst[:, :], zb[:, 0:P], zb[:, :], start=True, stop=False,
                                                 skip_group_check=True)
                        nc.tensor.matmul(dst[g * DH:(g + 1) * DH, off:CH], vv[:, k, h * DH:(h + 1) * DH],
                                         pt[:, at["T", ("T", n, k)] % PR, 0:CH - off], start=c > 0 and k < QUAD,
                                         stop=k >= TPC * (c + 1) - QUAD, skip_group_check=True)\
                            .then_inc(v_done, 1)
                    elif kind == "Z":
                        dst = z_ps
                        npair = 2 * c
                        if k < npair:
                            pe.wait_ge(paired, after(it, NA, ("A", n, k), "A"))
                            off, src = 0, pair[:, at["A", ("A", n, k)] % AR, :]
                        else:
                            kb = k - npair + TPC * c
                            off = (k - npair) * P
                            src = pt[:, at["T", ("T", n, kb)] % PR, :]
                        if k == 0:
                            pe.wait_ge(z_cp, it * NU + n + UP)
                        for t in range(off // P, TPC):
                            g, cols = slice(t * DH, (t + 1) * DH), slice(t * P, (t + 1) * P)
                            last = nc.tensor.matmul(dst[g, cols], ones[:, :], src[:, t * P - off:(t + 1) * P - off],
                                                    start=k == 0, stop=k == sums_of(n) - TPC + t,
                                                    skip_group_check=True)
                        last.then_inc(z_done, 1)
                    elif kind == "F":
                        pe.wait_ge(o_cp, it * NU + (n + 1) * QUAD + UP)
                        pe.wait_ge(t_used, ring_free(it, NTS, at["t", step], TR))
                        for hh in range(QUAD):
                            last = nc.tensor.matmul(tp_[at["t", step] % TR][hh * DH:(hh + 1) * DH, :], sel[:, :],
                                                    o_ev[:, hh, :], start=True, stop=True)
                        last.then_inc(t_full, 1)


            run(0, 0, first)
            with pe.Fori(0, NIT // 2) as i:
                for half in range(2):
                    run(i, half, plan)


def experts(nc, scope, wg, wu, wd, xs_d, ys_d, ident_sb, blk_e):
    f32, f32r = mybir.dt.float32, mybir.dt.float32r
    ALU, ACT = mybir.AluOpType, mybir.ActivationFunctionType
    RT = BLK // P
    PARTS = 3 * KD
    PPF = PARTS // KD
    with ExitStack() as ctx:
        sems = []
        sb, ps, sem = scope(ctx, "experts", sems)
        raw = sb("raw", [P, 3, KD, D], f32)
        wp = [[sb(f"weights{n}_part{m}", [P, 3, KD, D], f32r) for m in range(2)] for n in range(2)]
        xr = [sb(f"x_rows{n}", [P, RT, D], f32) for n in range(2)]
        xT = [[sb(f"xT{n}_part{m}", [P, KD, BLK], f32r) for m in range(2)] for n in range(2)]
        gate = [sb(f"gate{n}", [P, BLK], f32) for n in range(2)]
        hid = sb("hidden", [P, KD, BLK], f32)
        hp = [[sb(f"hidden{n}_part{m}", [P, KD, BLK], f32r) for m in range(2)] for n in range(2)]
        y = [sb(f"y_rows{n}", [P, RT, D], f32) for n in range(2)]
        tps = [ps(f"x_psum{n}") for n in range(2)]
        gps, ups = [ps(f"gate_psum{n}") for n in range(2)], [ps(f"up_psum{n}") for n in range(2)]
        yps = [ps(f"y_psum{n}") for n in range(2)]

        w_in, x_in = [sem(f"w{m}_in") for m in range(3)], [sem(f"x_in{n}") for n in range(2)]
        w_hi, w_lo = sem("w_high"), sem("w_low")
        tr, x_hi, x_lo = sem("transposes"), sem("xT_high"), sem("xT_low")
        gu, g_act, h_mul = sem("gate_up_full"), sem("gate_done"), sem("hidden_done")
        h_hi, h_lo = sem("hidden_high"), sem("hidden_low")
        y_full, y_cp, y_out = sem("y_full"), sem("y_copied"), [sem(f"y_out{n}") for n in range(2)]
        moved_on = sem("moved_on")
        block = ctx.enter_context(nc.Block())
        weights = [w.rearrange("e (k p) f -> p e k f", p=P) for w in (wg, wu, wd)]

        @block.sync
        def _(sp):
            for s in sems:
                sp.sem_inc(s, UP)

            def load_weights(b, m):
                e = sp.value_load(blk_e[0:1, bass.ds(b, 1)], min_val=0, max_val=E - 1)
                sp.dma_start(raw[:, m, :, :], weights[m][:, bass.ds(e, 1), :, :].rearrange("p e k f -> p (e k) f"))\
                  .then_inc(w_in[m], 16)

            def load_rows(b, n):
                sp.dma_start(xr[n][:, :, :], xs_d[bass.ds(b * BLK, BLK), :].rearrange("(t p) d -> p t d", p=P))\
                  .then_inc(x_in[n], 16)

            for m in range(3):
                load_weights(0, m)
            load_rows(0, 0)
            with sp.Fori(0, NBLK // 2) as i:
                for n in range(2):
                    b = 2 * i + n
                    nxt = (b + 1) % NBLK
                    sp.wait_ge(tr, b * 2 + UP)
                    sp.sem_inc(moved_on, 1)
                    load_rows(nxt, 1 - n)
                    for m in range(3):
                        sp.wait_ge(w_lo, b * PARTS + (m + 1) * KD + UP)
                        sp.sem_inc(moved_on, 1)
                        load_weights(nxt, m)
            for m in range(3):
                sp.wait_ge(w_in[m], (NBLK + 1) * 16 + UP)
            sp.wait_ge(x_in[0], (NBLK // 2 + 1) * 16 + UP)

        def high_part(act, b, n, q):
            m, k = q // KD, q % KD
            if k == 0:
                act.wait_ge(w_in[m], (b + 1) * 16 + UP)
            nc.scalar.activation(wp[n][0][:, m, k, :], raw[:, m, k, :], ACT.Copy).then_inc(w_hi, 1)

        def low_part(dve, b, n, q):
            m, k = q // KD, q % KD
            dve.wait_ge(w_hi, b * PARTS + q + 1 + UP)
            nc.vector.tensor_tensor(wp[n][1][:, m, k, :], raw[:, m, k, :], wp[n][0][:, m, k, :].bitcast(f32),
                                    ALU.subtract).then_inc(w_lo, 1)

        def rows_high(act, b, n):
            for h in range(2):
                act.wait_ge(tr, b * 2 + h + 1 + UP)
                nc.scalar.activation(xT[n][0][:, 2 * h:2 * h + 2, :], tps[h][:, :], ACT.Copy).then_inc(x_hi, 1)

        def rows_low(dve, b, n):
            for h in range(2):
                dve.wait_ge(x_hi, b * 2 + h + 1 + UP)
                nc.vector.tensor_tensor(xT[n][1][:, 2 * h:2 * h + 2, :], tps[h][:, :],
                                        xT[n][0][:, 2 * h:2 * h + 2, :].bitcast(f32), ALU.subtract).then_inc(x_lo, 1)

        @block.gpsimd
        def _(pool):
            with pool.Fori(0, NBLK // 2) as i:
                for n in range(2):
                    b = 2 * i + n
                    for k in range(KD):
                        pool.wait_ge(h_hi, b * KD + k + 1 + UP)
                        nc.gpsimd.tensor_tensor(hp[n][1][:, k, :], hid[:, k, :], hp[n][0][:, k, :].bitcast(f32),
                                                ALU.subtract).then_inc(h_lo, 1)

        @block.vector
        def _(dve):
            for q in range(PARTS):
                low_part(dve, 0, 0, q)
            rows_low(dve, 0, 0)
            with dve.Fori(0, NBLK // 2) as i:
                for n in range(2):
                    b = 2 * i + n
                    dve.wait_ge(h_lo, b * KD + UP)
                    for f in range(KD):
                        dve.wait_ge(g_act, b * KD + f + 1 + UP)
                        nc.vector.tensor_tensor(hid[:, f, :], ups[f % 2][:, 0:BLK], gate[f % 2][:, :], ALU.mult)\
                            .then_inc(h_mul, 1)
                        if f < KD - 1:
                            for q in range(f * PPF, (f + 1) * PPF):
                                low_part(dve, b + 1, 1 - n, q)
                        if f == KD - 2:
                            rows_low(dve, b + 1, 1 - n)
                    for q in range(PARTS - PPF, PARTS):
                        low_part(dve, b + 1, 1 - n, q)

        @block.scalar
        def _(act):
            for q in range(PARTS):
                high_part(act, 0, 0, q)
            rows_high(act, 0, 0)
            with act.Fori(0, NBLK // 2) as i:
                for n in range(2):
                    b = 2 * i + n
                    act.wait_ge(y_full, b * RT + UP)
                    for f in range(KD):
                        act.wait_ge(gu, b * KD + f + 1 + UP)
                        nc.scalar.activation(gate[f % 2][:, :], gps[f % 2][:, 0:BLK], ACT.Silu).then_inc(g_act, 1)
                        if f < KD - 1:
                            high_part(act, b + 1, 1 - n, f * PPF)
                        act.wait_ge(h_mul, b * KD + f + 1 + UP)
                        nc.scalar.activation(hp[n][0][:, f, :], hid[:, f, :], ACT.Copy).then_inc(h_hi, 1)
                        if f < KD - 1:
                            for q in range(f * PPF + 1, (f + 1) * PPF):
                                high_part(act, b + 1, 1 - n, q)
                        if f == KD - 2:
                            rows_high(act, b + 1, 1 - n)
                    for q in range(PARTS - PPF, PARTS):
                        high_part(act, b + 1, 1 - n, q)
                    act.wait_ge(y_out[n], i * 16 + UP)
                    for t in range(RT):
                        act.wait_ge(y_full, b * RT + t + 1 + UP)
                        nc.scalar.activation(y[n][:, t, :], yps[t % 2][:, :], ACT.Copy).then_inc(y_cp, 1)
                    act.wait_ge(y_cp, (b + 1) * RT + UP)
                    act.dma_start(ys_d[bass.ds(b * BLK, BLK), :].rearrange("(t p) d -> p t d", p=P), y[n][:, :, :])\
                       .then_inc(y_out[n], 16)
            for n in range(2):
                act.wait_ge(y_out[n], NBLK // 2 * 16 + UP)

        @block.tensor
        def _(pe):
            def turn(b, n, count):
                pe.wait_ge(x_in[n], count * 16 + UP)
                pe.wait_ge(x_lo, b * 2 + UP)
                for k in range(KD):
                    for t in range(RT):
                        col = (k % 2) * BLK + t * P
                        last = nc.tensor.transpose(tps[k // 2][:, col:col + P],
                                                   xr[n][:, t, k * P:(k + 1) * P], ident_sb[:, :])
                    if k % 2:
                        last.then_inc(tr, 1)

            turn(0, 0, 1)
            with pe.Fori(0, NBLK // 2) as i:
                for n in range(2):
                    b = 2 * i + n
                    pe.wait_ge(x_lo, (b + 1) * 2 + UP)
                    pe.wait_ge(w_lo, b * PARTS + 2 * KD + UP)
                    for f in range(KD):
                        pe.wait_ge(h_mul, b * KD + (f - 1 if f >= 2 else 0) + UP)
                        for m, dst in ((0, gps[f % 2]), (1, ups[f % 2])):
                            for s, (k, (a, w2)) in enumerate([(k, p) for k in range(KD) for p in PASSES]):
                                last = nc.tensor.matmul(dst[:, 0:BLK], wp[n][w2][:, m, k, f * P:(f + 1) * P],
                                                        xT[n][a][:, k, :], start=s == 0, stop=s == 3 * KD - 1)
                        last.then_inc(gu, 1)
                        if f == KD - 2:
                            turn(b + 1, 1 - n, i + 1 + n)
                    pe.wait_ge(w_lo, (b + 1) * PARTS + UP)
                    pe.wait_ge(y_cp, b * RT + UP)
                    for ks in (range(KD - 1), range(KD - 1, KD)):
                        for t in range(RT):
                            for k in ks:
                                if t == 0:
                                    pe.wait_ge(h_lo, b * KD + k + 1 + UP)
                                for s, (a, w2) in enumerate(PASSES):
                                    last = nc.tensor.matmul(yps[t][:, :], hp[n][a][:, k, t * P:(t + 1) * P],
                                                            wp[n][w2][:, 2, k, :], start=k == 0 and s == 0,
                                                            stop=k == KD - 1 and s == len(PASSES) - 1)
                            if k == KD - 1:
                                last.then_inc(y_full, 1)


def combine(nc, scope, x, woutT, attn_d, ys_d, pos, wts, out):
    f32, i32 = mybir.dt.float32, mybir.dt.int32
    ALU, ACT = mybir.AluOpType, mybir.ActivationFunctionType
    with ExitStack() as ctx:
        sems = []
        sb, ps, sem = scope(ctx, "combine", sems)
        sem0 = scope(ctx, "combine_pool")[2]
        wo = sb("wo", [P, NG, D], f32)
        at = [sb(f"attn_chunk{n}", [P, NG, CH], f32) for n in range(2)]
        xr = [sb(f"x_chunk{n}", [P, TPC, D], f32) for n in range(2)]
        y1 = [sb(f"first_choice{n}", [P, TPC, D], f32) for n in range(2)]
        y2 = [sb(f"second_choice{n}", [P, TPC, D], f32) for n in range(2)]
        gate = [sb(f"moe_gate{n}", [P, TPC, D], f32) for n in range(2)]
        res = [sb(f"result{n}", [P, TPC, D], f32) for n in range(2)]
        ix = [sb(f"row_index{n}", [P, 2, TPC], i32) for n in range(2)]
        wt = [sb(f"weights{n}", [P, 2, TPC], f32) for n in range(2)]
        sps = [ps(f"s_psum{n}") for n in range(TPC)]
        w_in = sem("wo_in")
        in_ = [sem(f"chunk_in{n}") for n in range(2)]
        passed = sem("passed")
        idx, got = sem("index_copied"), [sem0(f"gathered{n}") for n in range(2)]
        wt_cp, y_w, mix, act_d, s_full, s_mul, add = (sem("weights_copied"), sem("weighted"), sem("mixed"), sem("gated"),
                                                      sem("s_full"), sem("s_times_gate"), sem("added"))
        o_out = [sem(f"out_stored{n}") for n in range(2)]
        moved_on = sem("moved_on")
        block = ctx.enter_context(nc.Block())

        @block.sync
        def _(sp):
            for s in sems:
                sp.sem_inc(s, UP)
            sp.dma_start(wo[:, :, :], woutT.rearrange("(k p) o -> p k o", p=P)).then_inc(w_in, 16)
            with sp.Fori(0, NCH // 2) as i:
                for n in range(2):
                    c = 2 * i + n
                    sp.wait_ge(s_full, (c - n if n == 0 else c - 1) * TPC + UP)
                    sp.wait_ge(add, (c - n if n == 0 else c - 1) * TPC + UP)
                    sp.sem_inc(moved_on, 1)
                    batch, at_t = c // CPB, (c % CPB) * CH
                    sp.dma_start(at[n][:, :, :], attn_d[bass.ds(batch * NG, NG), :, bass.ds(at_t, CH)]
                                 .rearrange("g p t -> p g t")).then_inc(in_[n], 16)
                    sp.dma_start(xr[n][:, :, :], x[bass.ds(c * CH, CH), :].rearrange("(t p) d -> p t d", p=P))\
                      .then_inc(in_[n], 16)

        @block.gpsimd
        def _(pool):
            with pool.Fori(0, NCH // 2) as i:
                for n in range(2):
                    c = 2 * i + n
                    pool.wait_ge(mix, (c - n if n == 0 else c - 1) * TPC + UP)
                    nc.gpsimd.tensor_copy(ix[n][:, :, :], pos[:, :, bass.ds(c * TPC, TPC)]).then_inc(idx, 1)
                    pool.wait_ge(idx, c + 1 + UP)
                    pool.sem_inc(passed, 1)
                    for t in range(TPC):
                        for m, y in ((0, y1), (1, y2)):
                            nc.gpsimd.indirect_dma_start(y[n][:, t, :], None, ys_d[:, :],
                                                         bass.IndirectOffsetOnAxis(ap=ix[n][:, m, t:t + 1], axis=0),
                                                         bounds_check=NSLOT - 1).then_inc(got[n], 16)

        @block.vector
        def _(dve):
            with dve.Fori(0, NCH // 2) as i:
                for n in range(2):
                    c = 2 * i + n
                    nc.vector.tensor_copy(wt[n][:, :, :], wts[:, :, bass.ds(c * TPC, TPC)]).then_inc(wt_cp, 1)
                    dve.wait_ge(wt_cp, c + 1 + UP)
                    dve.wait_ge(got[n], (i + 1) * 2 * TPC * 16)
                    for t in range(TPC):
                        nc.vector.tensor_scalar(y1[n][:, t, :], y1[n][:, t, :], wt[n][:, 0, t:t + 1], None,
                                                ALU.mult).then_inc(y_w, 1)
                    for t in range(TPC):
                        dve.wait_ge(y_w, c * TPC + t + 1 + UP)
                        nc.vector.scalar_tensor_tensor(out=gate[n][:, t, :], in0=y2[n][:, t, :],
                                                       scalar=wt[n][:, 1, t:t + 1], in1=y1[n][:, t, :],
                                                       op0=ALU.mult, op1=ALU.add).then_inc(mix, 1)
                    dve.wait_ge(in_[n], (i + 1) * 32 + UP)
                    dve.wait_ge(o_out[n], i * 16 + UP)
                    for t in range(TPC):
                        dve.wait_ge(act_d, c * TPC + t + 1 + UP)
                        dve.wait_ge(s_full, c * TPC + t + 1 + UP)
                        nc.vector.tensor_tensor(res[n][:, t, :], sps[t][:, :], gate[n][:, t, :], ALU.mult)\
                            .then_inc(s_mul, 1)
                    for t in range(TPC):
                        dve.wait_ge(s_mul, c * TPC + t + 1 + UP)
                        nc.vector.tensor_tensor(res[n][:, t, :], res[n][:, t, :], xr[n][:, t, :], ALU.add)\
                            .then_inc(add, 1)

        @block.scalar
        def _(act):
            with act.Fori(0, NCH // 2) as i:
                for n in range(2):
                    c = 2 * i + n
                    for t in range(TPC):
                        act.wait_ge(mix, c * TPC + t + 1 + UP)
                        nc.scalar.activation(gate[n][:, t, :], gate[n][:, t, :], ACT.Silu).then_inc(act_d, 1)
                    act.wait_ge(add, (c + 1) * TPC + UP)
                    act.dma_start(out[bass.ds(c * CH, CH), :].rearrange("(t p) d -> p t d", p=P), res[n][:, :, :])\
                       .then_inc(o_out[n], 16)
            for n in range(2):
                act.wait_ge(o_out[n], NCH // 2 * 16 + UP)

        @block.tensor
        def _(pe):
            pe.wait_ge(w_in, 16 + UP)
            with pe.Fori(0, NCH // 2) as i:
                for n in range(2):
                    c = 2 * i + n
                    pe.wait_ge(in_[n], (i + 1) * 32 + UP)
                    for t in range(TPC):
                        pe.wait_ge(s_mul, c * TPC + UP)
                        for k in range(NG):
                            last = nc.tensor.matmul(sps[t][:, :], at[n][:, k, t * P:(t + 1) * P], wo[:, k, :],
                                                    start=k == 0, stop=k == NG - 1)
                        last.then_inc(s_full, 1)


def kernel(L0_attn_x, L0_attn_W_qkv, L0_attn_W_out, L0_ffn_router_w, L0_ffn_router_b, L0_ffn_we_gate,
           L0_ffn_we_up, L0_ffn_we_down):
    import ml_dtypes
    import numpy as np
    from concourse import bacc
    from concourse.bass_utils import run_bass_kernel_spmd

    def arr(a):
        return np.asarray(a)

    wt = arr(L0_attn_W_qkv).T
    qk = wt[:, :2 * D].reshape(D, 2, 2, H // 2, DH // 2, 2).transpose(0, 1, 2, 5, 3, 4).reshape(D, 2 * D)
    wqkvT = np.ascontiguousarray(np.concatenate([qk, wt[:, 2 * D:]], axis=1))
    freqs = (1.0 / np.float32(10000.0) ** (np.arange(0, DH, 2, dtype=np.float32) / np.float32(DH))).astype(np.float32)
    angles = np.outer(np.arange(T, dtype=np.float32), freqs).astype(np.float32)
    cos = np.ascontiguousarray(np.tile(np.cos(angles).T, (H // 2, 1)))
    sin = np.ascontiguousarray(np.tile(np.sin(angles).T, (H // 2, 1)))
    r = np.arange(P)
    bf = ml_dtypes.bfloat16
    arrays = {
        "x": arr(L0_attn_x).reshape(NTOK, D),
        "wqkvT": wqkvT,
        "woutT": np.ascontiguousarray(arr(L0_attn_W_out).T),
        "rwT": arr(L0_ffn_router_w),
        "rb": arr(L0_ffn_router_b).reshape(E, 1),
        "wg": arr(L0_ffn_we_gate),
        "wu": arr(L0_ffn_we_up),
        "wd": arr(L0_ffn_we_down),
        "cos": cos,
        "sin": sin,
        "cmask": np.where(r[None, :] > r[:, None], NEG, 0).astype(bf),
        "cmaskT": np.where(r[:, None] > r[None, :], NEG, 0).astype(bf),
        "identb": np.eye(P).astype(bf),
        "ident": np.eye(P, dtype=np.float32),
        "cst": constants(),
    }
    nc = bacc.Bacc("TRN2", target_bir_lowering=False, num_devices=1)
    args, maps = [], {}
    for name, a in arrays.items():
        maps["in_" + name] = a
        args.append(nc.dram_tensor("in_" + name, a.shape, mybir.dt.from_np(a.dtype), kind="ExternalInput").ap())
    res = nc.dram_tensor("out_rows", (NTOK, D), mybir.dt.float32, kind="ExternalOutput").ap()
    build(nc, *args, res)
    r = run_bass_kernel_spmd(nc, [maps], core_ids=[0])
    return r.results[0]["out_rows"].reshape(B, T, D)
```

```python
import concourse.bass as bass
from concourse import mybir
from contextlib import ExitStack

B, T, D = 4, 2048, 512
H, DH = 16, 32
E = 8
P = 128
NTOK = B * T
KD = D // P
CH = 512
TPC = CH // P
NCH = NTOK // CH
CPB = T // CH
NT = NTOK // P
QUAD = P // DH
NG = H // QUAD
NIT = B * NG
BLK = 256
NBLK = 2 * NTOK // BLK + E
NSLOT = NBLK * BLK
RB = NTOK // BLK
NEG = -1.0e30
SCALE = 1.0 / float(DH) ** 0.5
EPS = 1e-5
UP = 1
PASSES = ((0, 0), (0, 1), (1, 0))


def build(nc, x, wqkvT, woutT, rwT, rb, wg, wu, wd, cos, sin, cmask, cmaskT, identb, ident, cst, out):
    f32, f32r, bf16 = mybir.dt.float32, mybir.dt.float32r, mybir.dt.bfloat16
    i32, u32 = mybir.dt.int32, mybir.dt.uint32
    ALU, ACT, AX = mybir.AluOpType, mybir.ActivationFunctionType, mybir.AxisListType.X

    def dram(name, shape, dt):
        return nc.dram_tensor(name, shape, dt, kind="Internal").ap()

    qk_d = [dram("qT_parts", (B * H, 2, DH, T), f32), dram("kT_parts", (B * H, 2, DH, T), f32)]
    v_d = dram("v_rows", (NTOK, D), f32)
    xn_d = dram("xn_rows", (NTOK, D), f32)
    attn_d = dram("attnT", (NIT, P, T), f32)
    xs_d = dram("sorted_rows", (NSLOT, D), f32)
    ys_d = dram("expert_rows", (NSLOT, D), f32)

    top = ExitStack()

    def scope(ctx, stage, sems=None):
        def sb(name, shape, dt):
            return ctx.enter_context(nc.sbuf_tensor(f"{stage}_{name}", shape, dt))

        def ps(name):
            return ctx.enter_context(nc.psum_tensor(f"{stage}_{name}", [P, 512], f32))

        def sem(name):
            s = ctx.enter_context(nc.semaphore(f"{stage}_{name}"))
            if sems is not None:
                sems.append(s)
            return s
        return sb, ps, sem

    with top:
        sb, _, _ = scope(top, "kept")
        ident_sb = sb("ident_sb", [P, P], f32)
        logits = sb("logits", [P, NT, E], f32)
        pos = sb("pos", [P, 2, NT], i32)
        wts = sb("wts", [P, 2, NT], f32)
        padpos = sb("padpos", [P, 2 * E], i32)
        blk_e = sb("blk_e", [1, NBLK], i32)

        project(nc, scope, x, wqkvT, rwT, rb, cos, sin, ident, ident_sb, logits, qk_d, v_d, xn_d)
        with ExitStack() as ctx:
            operands = AttentionOperands(nc, scope, ctx, qk_d, v_d, cmask, cmaskT, identb, cst)
            route(nc, scope, cst, logits, pos, wts, padpos, blk_e, operands)
            attend(nc, scope, operands, xn_d, attn_d, xs_d, pos, padpos)
        experts(nc, scope, wg, wu, wd, xs_d, ys_d, ident_sb, blk_e)
        combine(nc, scope, x, woutT, attn_d, ys_d, pos, wts, out)


def project(nc, scope, x, wqkvT, rwT, rb, cos, sin, ident, ident_sb, logits, qk_d, v_d, xn_d):
    f32, f32r = mybir.dt.float32, mybir.dt.float32r
    ALU, ACT = mybir.AluOpType, mybir.ActivationFunctionType
    OC = 3 * D
    with ExitStack() as ctx:
        sems = []
        sb, ps, sem = scope(ctx, "project", sems)
        w = [sb(f"w_part{n}", [P, KD, OC], f32r) for n in range(2)]
        rw = [sb(f"rw_part{n}", [P, KD, E], f32r) for n in range(2)]
        rb_sb = sb("rb_sb", [E, 1], f32)
        cos_sb = sb("cos_sb", [P, T], f32)
        sin_sb = sb("sin_sb", [P, T], f32)
        xin = [sb(f"xin{n}", [P, TPC, D], f32) for n in range(2)]
        x_in = [sem(f"x_in{n}") for n in range(2)]

        def rows(array, c):
            return array[bass.ds((c % NCH) * CH, CH), :].rearrange("(t p) d -> p t d", p=P)

        with ExitStack() as c2:
            sb2, _, sem2 = scope(c2, "split")
            wraw = sb2("wraw", [P, KD, OC], f32)
            rwraw = sb2("rwraw", [P, KD, E], f32)
            loaded, rw_high, rw_low = sem2("small_loaded"), sem2("router_high"), sem2("router_low")
            w_in = [sem2(f"weights_in{k}") for k in range(KD)]
            high, low = sem2("weights_high"), sem2("weights_low")
            block = c2.enter_context(nc.Block())

            @block.sync
            def _(sp):
                rows_w = wqkvT.rearrange("(k p) o -> p k o", p=P)
                for k in range(KD):
                    sp.dma_start(wraw[:, k, :], rows_w[:, k, :]).then_inc(w_in[k], 16)
                sp.dma_start(xin[0][:, :, :], rows(x, 0)).then_inc(x_in[0], 16)
                sp.dma_start(rwraw[:, :, :], rwT.rearrange("(k p) e -> p k e", p=P)).then_inc(loaded, 16)
                sp.dma_start(rb_sb[:, :], rb).then_inc(loaded, 16)
                sp.dma_start(cos_sb[:, :], cos).then_inc(loaded, 16)
                sp.dma_start(sin_sb[:, :], sin).then_inc(loaded, 16)
                sp.dma_start(ident_sb[:, :], ident).then_inc(loaded, 16)
                sp.wait_ge(loaded, 5 * 16)

            @block.scalar
            def _(act):
                for k in range(KD):
                    act.wait_ge(w_in[k], 16)
                    nc.scalar.activation(w[0][:, k, :], wraw[:, k, :], ACT.Copy).then_inc(high, 1)

            @block.vector
            def _(dve):
                for k in range(KD):
                    dve.wait_ge(high, k + 1)
                    nc.vector.tensor_tensor(w[1][:, k, :], wraw[:, k, :], w[0][:, k, :].bitcast(f32),
                                            ALU.subtract).then_inc(low, 1)
                dve.wait_ge(loaded, 5 * 16)
                nc.vector.tensor_copy(rw[0][:, :, :], rwraw[:, :, :]).then_inc(rw_high, 1)
                dve.wait_ge(rw_high, 1)
                nc.vector.tensor_tensor(rw[1][:, :, :], rwraw[:, :, :], rw[0][:, :, :].bitcast(f32),
                                        ALU.subtract).then_inc(rw_low, 1)
                dve.wait_ge(rw_low, 1)
                dve.wait_ge(low, KD)

        xn = [sb(f"xn{n}", [P, TPC, D], f32) for n in range(2)]
        stats = sb("stats", [P, 2, TPC, 6], f32)
        mv = sb("mv", [P, 2, TPC, 2], f32)
        std = sb("std", [P, 2, TPC], f32)
        rstd = sb("rstd", [P, 2, TPC], f32)
        eps = sb("eps", [P, 1], f32)
        xT = [[sb(f"xT{n}_part{m}", [P, KD, CH], f32r) for m in range(2)] for n in range(2)]
        prod = sb("rope_products", [P, 2, 2, 2, CH], f32)
        rot = sb("rotated", [P, 2, CH], f32)
        rot_p = [sb(f"rotated_part{m}", [P, 2, 2, CH], f32r) for m in range(2)]
        v_sb = sb("v_sb", [P, TPC, D], f32)
        lt = sb("logitsT", [E, 2, CH], f32)

        tp = [ps(f"transposed{n}") for n in range(2)]
        qkp = [ps(f"qk_half{n}") for n in range(4)]
        vp = [ps(f"v_psum{n}") for n in range(2)]

        bn, agg, stdd, rs, normed = sem("bn"), sem("agg"), sem("stdd"), sem("rs"), sem("normed")
        eps_set = sem("eps_set")
        passed = sem("passed")
        xn_out = [sem(f"xn_out{n}") for n in range(2)]
        tr, t_hi, t_lo = sem("transposes"), sem("xT_high"), sem("xT_low")
        qk_full, v_full, rt_full = sem("qk_full"), sem("v_full"), sem("router_full")
        prods, rots, r_hi = sem("products"), sem("rotations"), sem("rot_high")
        r_lo = [sem("rot_low_by_pool"), sem("rot_low_by_vector")]
        qk_out = [sem(f"qk_out{n}") for n in range(2)]
        v_cp, v_out, lt_cp, lg_cp = sem("v_copied"), sem("v_out"), sem("lt_copied"), sem("logits_copied")
        moved_on = sem("moved_on")
        block = ctx.enter_context(nc.Block())

        NPAIR = 4

        def chunks(b):
            for j in range(CPB):
                yield b * CPB + j, j, b + (j + 1) // CPB, (j + 1) % CPB

        @block.sync
        def _(sp):
            for s in sems:
                sp.sem_inc(s, UP)
            sp.dma_start(xin[1][:, :, :], rows(x, 1)).then_inc(x_in[1], 16)
            with sp.Fori(0, B) as b:
                for c, j, _, _ in chunks(b):
                    sp.wait_ge(normed, (c + 1) * TPC + UP)
                    sp.sem_inc(moved_on, 1)
                    sp.dma_start(xin[j % 2][:, :, :], rows(x, c + 2)).then_inc(x_in[j % 2], 16)
                    for r in range(NPAIR):
                        q, m = c * NPAIR + r, r % 2
                        sp.wait_ge(r_hi, q * 2 + 2 + UP)
                        sp.sem_inc(moved_on, 1)
                        sp.wait_ge(r_lo[0], q + 1 + UP)
                        sp.sem_inc(moved_on, 1)
                        sp.wait_ge(r_lo[1], q + 1 + UP)
                        sp.sem_inc(moved_on, 1)
                        z, g = r // 2, r % 2
                        for part in range(2):
                            for h in range(2):
                                dst = qk_d[z][bass.ds(b * H + g * (H // 2), H // 2), part,
                                              h * (DH // 2):(h + 1) * (DH // 2), j * CH:(j + 1) * CH]
                                sp.dma_start(dst, rot_p[part][:, m, h, :].bitcast(f32)).then_inc(qk_out[m], 16)
            for n in range(2):
                sp.wait_ge(x_in[n], (NCH // 2 + 1) * 16 + UP)
                sp.wait_ge(qk_out[n], NCH * 2 * 64 + UP)

        @block.vector
        def _(dve):
            nc.vector.memset(eps[:, :], EPS).then_inc(eps_set, 1)

            def statistics(c, b, j):
                n = j % 2
                dve.wait_ge(x_in[n], (b * 2 + j // 2 + 1) * 16 + UP)
                for t in range(TPC):
                    nc.vector.bn_stats(stats[:, n, t, :], xin[n][:, t, :]).then_inc(bn, 1)
                dve.wait_ge(bn, (c + 1) * TPC + UP)
                dve.sem_inc(passed, 1)
                for t in range(TPC):
                    nc.vector.bn_aggr(mv[:, n, t, :], stats[:, n, t, :]).then_inc(agg, 1)

            def normalise(c, b, j, first=False):
                n = j % 2
                dve.wait_ge(stdd, c + 1 + UP)
                nc.vector.reciprocal(rstd[:, n, :], std[:, n, :]).then_inc(rs, 1)
                dve.wait_ge(rs, c + 1 + UP)
                if not first:
                    dve.wait_ge(xn_out[n], (b * 2 + j // 2) * 16 + UP)
                    dve.wait_ge(tr, (c - 1) * KD + UP)
                for t in range(TPC):
                    nc.vector.tensor_scalar(xn[n][:, t, :], xin[n][:, t, :], mv[:, n, t, 0:1],
                                            rstd[:, n, t:t + 1], ALU.subtract, ALU.mult).then_inc(normed, 1)

            def low_part(c, j, k):
                n = j % 2
                dve.wait_ge(t_hi, c * KD + k + 1 + UP)
                nc.vector.tensor_tensor(xT[n][1][:, k, :], tp[k % 2][:, :], xT[n][0][:, k, :].bitcast(f32),
                                        ALU.subtract).then_inc(t_lo, 1)

            def rotated_low(c, r):
                q = c * NPAIR + r
                dve.wait_ge(r_hi, q * 2 + 2 + UP)
                nc.vector.tensor_tensor(rot_p[1][:, r % 2, 1, :], rot[:, 1, :],
                                        rot_p[0][:, r % 2, 1, :].bitcast(f32), ALU.subtract).then_inc(r_lo[1], 1)

            statistics(0, 0, 0)
            normalise(0, 0, 0, first=True)
            for k in range(KD):
                low_part(0, 0, k)
            with dve.Fori(0, B) as b:
                for c, j, b1, j1 in chunks(b):
                    statistics(c + 1, b1, j1)
                    normalise(c + 1, b1, j1)
                    dve.wait_ge(qk_full, c * 2 * NPAIR + UP)
                    cs, sn = cos_sb[:, j * CH:(j + 1) * CH], sin_sb[:, j * CH:(j + 1) * CH]
                    for r in range(NPAIR):
                        q, m = c * NPAIR + r, r % 2
                        dve.wait_ge(rots, (q - 1 if r else q) * 2 + UP)
                        for h, factors in ((0, (cs, sn)), (1, (sn, cs))):
                            dve.wait_ge(qk_full, q * 2 + h + 1 + UP)
                            for half in range(2):
                                nc.vector.tensor_tensor(prod[:, m, h, half, :], qkp[2 * m + h][:, :],
                                                        factors[half], ALU.mult).then_inc(prods, 1)
                            if 2 * r + h < KD:
                                low_part(c + 1, j1, 2 * r + h)
                        if r:
                            rotated_low(c, r - 1)
                        if r == 1:
                            dve.wait_ge(rt_full, 2 * c + 2 + UP)
                            nc.vector.tensor_copy(logits[:, bass.ds(c * TPC, TPC), :],
                                                  vp[0][:, 0:TPC * E].rearrange("p (t e) -> p t e", e=E)).then_inc(lg_cp, 1)
                    rotated_low(c, NPAIR - 1)

        @block.gpsimd
        def _(pool):
            with pool.Fori(0, B) as b:
                for c, j, _, _ in chunks(b):
                    for r in range(NPAIR):
                        q, m = c * NPAIR + r, r % 2
                        pool.wait_ge(r_hi, q * 2 + UP)
                        pool.wait_ge(r_lo[0], q + UP)
                        pool.wait_ge(r_lo[1], q + UP)
                        pool.wait_ge(prods, q * 4 + 3 + UP)
                        nc.gpsimd.tensor_tensor(rot[:, 0, :], prod[:, m, 0, 0, :], prod[:, m, 1, 0, :],
                                                ALU.subtract).then_inc(rots, 1)
                        pool.wait_ge(prods, q * 4 + 4 + UP)
                        nc.gpsimd.tensor_tensor(rot[:, 1, :], prod[:, m, 0, 1, :], prod[:, m, 1, 1, :],
                                                ALU.add).then_inc(rots, 1)
                        pool.wait_ge(r_hi, q * 2 + 1 + UP)
                        nc.gpsimd.tensor_tensor(rot_p[1][:, m, 0, :], rot[:, 0, :],
                                                rot_p[0][:, m, 0, :].bitcast(f32), ALU.subtract).then_inc(r_lo[0], 1)

        @block.scalar
        def _(act):
            def deviation(c, j):
                act.wait_ge(agg, (c + 1) * TPC + UP)
                nc.scalar.activation(std[:, j % 2, :], mv[:, j % 2, :, 1], ACT.Sqrt, bias=eps[:, 0:1])\
                    .then_inc(stdd, 1)

            def store_rows(c, j):
                act.wait_ge(normed, (c + 1) * TPC + UP)
                act.dma_start(rows(xn_d, c), xn[j % 2][:, :, :]).then_inc(xn_out[j % 2], 16)

            def high_part(c, j, k):
                act.wait_ge(tr, c * KD + k + 1 + UP)
                nc.scalar.activation(xT[j % 2][0][:, k, :], tp[k % 2][:, :], ACT.Copy).then_inc(t_hi, 1)

            def rotated(c, r, h):
                act.wait_ge(rots, (c * NPAIR + r) * 2 + h + 1 + UP)
                nc.scalar.activation(rot_p[0][:, r % 2, h, :], rot[:, h, :], ACT.Copy).then_inc(r_hi, 1)

            act.wait_ge(eps_set, 1 + UP)
            deviation(0, 0)
            store_rows(0, 0)
            for k in range(KD):
                high_part(0, 0, k)
            with act.Fori(0, B) as b:
                for c, j, b1, j1 in chunks(b):
                    act.wait_ge(v_out, c * 16 + UP)
                    for t in range(TPC):
                        act.wait_ge(v_full, c * TPC + t + 1 + UP)
                        nc.scalar.activation(v_sb[:, t, :], vp[t % 2][:, :], ACT.Copy).then_inc(v_cp, 1)
                        if t == 1:
                            deviation(c + 1, j1)
                    act.wait_ge(v_cp, (c + 1) * TPC + UP)
                    act.dma_start(rows(v_d, c), v_sb[:, :, :]).then_inc(v_out, 16)
                    act.wait_ge(rt_full, 2 * c + 1 + UP)
                    nc.scalar.activation(lt[:, j % 2, :], vp[0][0:E, :], ACT.Identity, bias=rb_sb[:, 0:1])\
                        .then_inc(lt_cp, 1)
                    store_rows(c + 1, j1)
                    act.wait_ge(qk_full, c * 2 * NPAIR + UP)
                    for k in range(KD - 1):
                        high_part(c + 1, j1, k)
                    for r in range(NPAIR):
                        q, m = c * NPAIR + r, r % 2
                        act.wait_ge(qk_out[m], (c * 2 + r // 2) * 64 + UP)
                        for h in range(2):
                            rotated(c, r, h)
                        if r == 0:
                            high_part(c + 1, j1, KD - 1)
            act.wait_ge(v_out, NCH * 16 + UP)
            for m in range(2):
                act.wait_ge(xn_out[m], (NCH // 2 + (m == 0)) * 16 + UP)

        @block.tensor
        def _(pe):
            def turn(c, j, k):
                if k == 0:
                    pe.wait_ge(normed, (c + 1) * TPC + UP)
                if k < 2:
                    pe.wait_ge(t_lo, c * KD + UP)
                else:
                    pe.wait_ge(t_lo, c * KD + k - 1 + UP)
                for t in range(TPC):
                    last = nc.tensor.transpose(tp[k % 2][:, t * P:(t + 1) * P],
                                               xn[j % 2][:, t, k * P:(k + 1) * P], ident_sb[:, :])
                last.then_inc(tr, 1)

            for k in range(KD):
                turn(0, 0, k)
            with pe.Fori(0, B) as b:
                for c, j, b1, j1 in chunks(b):
                    n = j % 2
                    pe.wait_ge(t_lo, (c + 1) * KD + UP)
                    pe.wait_ge(lg_cp, c + UP)
                    for t in range(TPC):
                        pe.wait_ge(v_cp, c * TPC + max(0, t - 1) + UP)
                        for m, (k, (a, w2)) in enumerate([(k, p) for k in range(KD) for p in PASSES]):
                            last = nc.tensor.matmul(vp[t % 2][:, :], xT[n][a][:, k, t * P:(t + 1) * P],
                                                    w[w2][:, k, 2 * D:3 * D], start=m == 0, stop=m == 3 * KD - 1)
                        last.then_inc(v_full, 1)
                    pe.wait_ge(v_cp, c * TPC + TPC - 1 + UP)
                    for m, (k, (a, w2)) in enumerate([(k, p) for k in range(KD) for p in PASSES]):
                        last = nc.tensor.matmul(vp[0][0:E, :], rw[w2][:, k, :], xT[n][a][:, k, :],
                                                start=m == 0, stop=m == 3 * KD - 1)
                    last.then_inc(rt_full, 1)
                    for r in range(NPAIR):
                        for h in range(2):
                            pe.wait_ge(prods, (c * NPAIR + (r - 1 if r >= 2 else 0)) * 4 + UP)
                            col = (2 * r + h) * P
                            for m, (k, (a, w2)) in enumerate([(k, p) for k in range(KD) for p in PASSES]):
                                last = nc.tensor.matmul(qkp[2 * (r % 2) + h][:, :], w[w2][:, k, col:col + P],
                                                        xT[n][a][:, k, :], start=m == 0, stop=m == 3 * KD - 1)
                            last.then_inc(qk_full, 1)
                            if (r, h) == (0, 1):
                                pe.wait_ge(lt_cp, c + 1 + UP)
                                pe.sem_inc(passed, 1)
                                for u in range(TPC):
                                    last = nc.tensor.transpose(vp[0][:, u * E:(u + 1) * E],
                                                               lt[:, n, u * P:(u + 1) * P], ident_sb[0:E, 0:E])
                                last.then_inc(rt_full, 1)
                            if 2 * r + h < KD:
                                turn(c + 1, j1, 2 * r + h)


C_IOTA = 0
C_RUN = C_IOTA + E
C_LESS = C_RUN + E * NT
C_ONE = C_LESS + P
C_THR = C_ONE + P
C_ROW = C_THR + RB
C_BLK = C_ROW + 2
C_SEL = C_BLK + NBLK
C_ALL = C_SEL + DH


def constants():
    import numpy as np
    c = np.zeros((P, C_ALL), np.float32)
    p = np.arange(P)
    c[:, C_IOTA:C_IOTA + E] = np.arange(E) - E
    run = np.ones((E, NT), np.float32)
    run[:, 0] = 0
    c[:, C_RUN:C_LESS] = run.reshape(-1)
    c[:, C_LESS:C_ONE] = p[:, None] < p[None, :]
    c[:, C_ONE:C_THR] = 1
    c[:, C_THR:C_ROW] = BLK * np.arange(RB)
    c[:, C_ROW:C_BLK] = p[:, None] + P * np.arange(2)
    c[:, C_BLK:C_SEL] = np.arange(NBLK)
    c[:, C_SEL:C_ALL] = (p[:, None] % DH) == np.arange(DH)
    return c


def route(nc, scope, cst, logits, pos, wts, padpos, blk_e, attention):
    f32 = mybir.dt.float32
    ALU, ACT, AX = mybir.AluOpType, mybir.ActivationFunctionType, mybir.AxisListType.X
    with ExitStack() as ctx:
        sb, ps, sem = scope(ctx, "route")
        cs = sb("consts", [P, C_ALL], f32)
        t3 = sb("tmp3", [P, NT, E], f32)
        m3 = sb("masked_logits", [P, NT, E], f32)
        hot = [sb(f"onehot{n}", [P, NT, E], f32) for n in range(2)]
        best = sb("best", [P, 2, NT], f32)
        idx = sb("first_index", [P, NT], f32)
        ex = sb("exp_difference", [P, NT], f32)
        both = sb("chosen", [P, E, NT], f32)
        upto = sb("chosen_up_to", [P, E, NT], f32)
        row = sb("row_of_choice", [P, E, NT], f32)
        total = sb("partition_total", [P, E], f32)
        over = sb("blocks_over", [P, E, RB], f32)
        nb = sb("blocks", [P, E], f32)
        nbe = sb("blocks_up_to", [P, E], f32)
        start = sb("first_row", [P, E], f32)
        tot = sb("expert_total", [P, E], f32)
        pad = sb("pads", [P, E], f32)
        rest = sb("rest", [P, E], f32)
        rest_to = sb("rest_up_to", [P, E], f32)
        tail = sb("tail_base", [P, E], f32)
        inside = sb("pad_inside", [P, E, 2], f32)
        used = sb("pad_used", [P, E, 2], f32)
        outside = sb("pad_outside", [P, E, 2], f32)
        posf = sb("row_float", [P, 2, NT], f32)
        bc = sb("block_compare", [1, NBLK, E], f32)
        be = sb("block_expert", [1, NBLK], f32)
        cnt = ps("count_psum")
        got, step, counted, expd = sem("constants_in"), sem("dve_step"), sem("counted"), sem("exp_done")
        moved_on = sem("moved_on")
        block = ctx.enter_context(nc.Block())
        less, ones = cs[:, C_LESS:C_ONE], cs[:, C_ONE:C_THR]

        def per_expert(ap, n):
            return ap.rearrange("p (e o) -> p e o", o=1).to_broadcast([P, E, n])

        @block.sync
        def _(sp):
            sp.dma_start(cs[:, :], cst).then_inc(got, 16)
            attention.first_loads(sp)

        @block.gpsimd
        def _(pool):
            attention.fill(pool)

        marks = {}

        @block.vector
        def _(dve):
            done = [0]

            def link(ins):
                done[0] += 1
                ins.then_inc(step, 1)
                dve.wait_ge(step, done[0])

            v = nc.vector
            iota = cs[:, C_IOTA:C_RUN].rearrange("p (o e) -> p o e", o=1).to_broadcast([P, NT, E])
            dve.wait_ge(got, 16)
            for n, src in enumerate((logits, m3)):
                link(v.tensor_reduce(best[:, n, :], src[:, :, :], AX, ALU.max))
                top = best[:, n, :].rearrange("p (t o) -> p t o", o=1).to_broadcast([P, NT, E])
                link(v.tensor_tensor(t3[:, :, :], src[:, :, :], top, ALU.is_equal))
                link(v.scalar_tensor_tensor(out=t3[:, :, :], in0=t3[:, :, :], scalar=-float(E), in1=iota,
                                            op0=ALU.mult, op1=ALU.add))
                link(v.tensor_reduce(idx[:, :], t3[:, :, :], AX, ALU.min))
                link(v.tensor_scalar(idx[:, :], idx[:, :], float(E), None, ALU.add))
                first = idx[:, :].rearrange("p (t o) -> p t o", o=1).to_broadcast([P, NT, E])
                link(v.tensor_tensor(hot[n][:, :, :], iota, first, ALU.is_equal))
                if n == 0:
                    link(v.scalar_tensor_tensor(out=m3[:, :, :], in0=hot[0][:, :, :], scalar=-3.0e38,
                                                in1=logits[:, :, :], op0=ALU.mult, op1=ALU.add))
            link(v.tensor_tensor(ex[:, :], best[:, 1, :], best[:, 0, :], ALU.subtract))
            marks["diff"] = done[0]
            dve.wait_ge(expd, 1)
            link(v.tensor_scalar(wts[:, 1, :], ex[:, :], 1.0, None, ALU.add))
            link(v.reciprocal(wts[:, 0, :], wts[:, 1, :]))
            link(v.tensor_tensor(wts[:, 1, :], ex[:, :], wts[:, 0, :], ALU.mult))
            link(v.tensor_tensor(both[:, :, :].rearrange("p e t -> p t e"), hot[0][:, :, :], hot[1][:, :, :],
                                 ALU.add))
            link(v.tensor_tensor_scan(upto[:, :, :].rearrange("p e t -> p (e t)"), cs[:, C_RUN:C_LESS],
                                      both[:, :, :].rearrange("p e t -> p (e t)"), 0.0, ALU.mult, ALU.add))
            link(v.tensor_copy(total[:, :], upto[:, :, NT - 1]))
            marks["total"] = done[0]
            dve.wait_ge(counted, 1)
            link(v.tensor_copy(tot[:, :], cnt[:, E:2 * E]))
            thr = cs[:, C_THR:C_ROW].rearrange("p (o k) -> p o k", o=1).to_broadcast([P, E, RB])
            link(v.tensor_tensor(over[:, :, :], per_expert(tot[:, :], RB), thr, ALU.is_gt))
            link(v.tensor_reduce(nb[:, :], over[:, :, :], AX, ALU.add))
            link(v.tensor_tensor_scan(nbe[:, :], ones[:, 0:E], nb[:, :], 0.0, ALU.mult, ALU.add))
            link(v.tensor_tensor(start[:, :], nbe[:, :], nb[:, :], ALU.subtract))
            link(v.tensor_scalar(start[:, :], start[:, :], float(BLK), None, ALU.mult))
            link(v.tensor_tensor(row[:, :, :], upto[:, :, :], both[:, :, :], ALU.subtract))
            link(v.tensor_tensor(rest[:, :], start[:, :], cnt[:, 0:E], ALU.add))
            link(v.tensor_tensor(row[:, :, :], row[:, :, :], per_expert(rest[:, :], NT), ALU.add))
            for n in range(2):
                link(v.tensor_tensor(t3[:, :, :], hot[n][:, :, :], row[:, :, :].rearrange("p e t -> p t e"),
                                     ALU.mult))
                link(v.tensor_reduce(posf[:, n, :], t3[:, :, :], AX, ALU.add))
            link(v.tensor_copy(pos[:, :, :], posf[:, :, :]))
            link(v.tensor_scalar(pad[:, :], nb[:, :], float(BLK), None, ALU.mult))
            link(v.tensor_tensor(pad[:, :], pad[:, :], tot[:, :], ALU.subtract))
            link(v.tensor_scalar(rest[:, :], pad[:, :], -1.0, float(BLK), ALU.mult, ALU.add))
            link(v.tensor_tensor_scan(rest_to[:, :], ones[:, 0:E], rest[:, :], 0.0, ALU.mult, ALU.add))
            link(v.tensor_tensor(tail[:, :], rest_to[:, :], rest[:, :], ALU.subtract))
            link(v.tensor_tensor(tail[:, :], tail[:, :], pad[:, :], ALU.subtract))
            link(v.tensor_scalar(rest[:, :], nbe[:, :], float(BLK), None, ALU.mult))
            link(v.tensor_scalar(tail[:, :], tail[:, :], rest[:, E - 1:E], None, ALU.add))
            link(v.tensor_tensor(start[:, :], start[:, :], tot[:, :], ALU.add))
            r2 = cs[:, C_ROW:C_BLK].rearrange("p (o h) -> p o h", o=1).to_broadcast([P, E, 2])
            link(v.tensor_tensor(used[:, :, :], per_expert(pad[:, :], 2), r2, ALU.is_gt))
            link(v.tensor_tensor(inside[:, :, :], per_expert(start[:, :], 2), r2, ALU.add))
            link(v.tensor_tensor(outside[:, :, :], per_expert(tail[:, :], 2), r2, ALU.add))
            link(v.tensor_tensor(inside[:, :, :], inside[:, :, :], outside[:, :, :], ALU.subtract))
            link(v.tensor_tensor(inside[:, :, :], inside[:, :, :], used[:, :, :], ALU.mult))
            link(v.tensor_tensor(inside[:, :, :], inside[:, :, :], outside[:, :, :], ALU.add))
            link(v.tensor_copy(padpos[:, :], inside[:, :, :].rearrange("p e h -> p (e h)")))
            blk = cs[0:1, C_BLK:C_SEL].rearrange("p (i o) -> p i o", o=1).to_broadcast([1, NBLK, E])
            ends = nbe[0:1, :].rearrange("p (o e) -> p o e", o=1).to_broadcast([1, NBLK, E])
            link(v.tensor_tensor(bc[:, :, :], blk, ends, ALU.is_ge))
            link(v.tensor_reduce(be[:, :], bc[:, :, :], AX, ALU.add))
            link(v.tensor_scalar(be[:, :], be[:, :], float(E - 1), None, ALU.min))
            link(v.tensor_copy(blk_e[:, :], be[:, :]))

        @block.scalar
        def _(act):
            act.wait_ge(step, marks["diff"])
            nc.scalar.activation(ex[:, :], ex[:, :], ACT.Exp).then_inc(expd, 1)

        @block.tensor
        def _(pe):
            pe.wait_ge(step, marks["total"])
            nc.tensor.matmul(cnt[:, 0:E], less, total[:, :], start=True, stop=True)
            nc.tensor.matmul(cnt[:, E:2 * E], ones, total[:, :], start=True, stop=True).then_inc(counted, 1)


def attention_plan():
    units = [(c, h) for c in range(CPB) for h in range(QUAD)]
    NU = len(units)
    plan, waiting = [], []
    clock = 0

    def scores(n):
        return [("S", n, (t, k)) for t in range(TPC) for k in range(units[n % NU][0] + 1)]

    def release(upto):
        for entry in sorted((w for w in waiting if w[0] <= upto), key=lambda w: w[0]):
            plan.extend(entry[1])
            waiting.remove(entry)

    for n, (c, h) in enumerate(units):
        ahead = scores(n + 2)
        nkb = TPC * (c + 1)
        plan.append(("X", n, 0))
        for kb in range(nkb):
            plan.append(("T", n, kb))
            plan += ahead[kb * len(ahead) // nkb:(kb + 1) * len(ahead) // nkb]
            full = kb < TPC * c
            if full and kb % 2:
                plan.append(("A", n, kb // 2))
            if kb % 4 == 3:
                burst = [("V", n, k) for k in range(kb - 3, kb + 1)]
                if full:
                    waiting.append((clock + V_LAG, burst))
                    for m in range(2):
                        waiting.append((clock + Z_LAG + m, [("Z", n, kb // 2 - 1 + m)]))
                else:
                    burst += [("Z", n, 2 * c + d) for d in range(TPC)]
                    waiting.append((clock + V_LAG, burst))
                    waiting.append((clock + V_LAG + O_LAG, [("C", n, "o")]))
                    waiting.append((clock + V_LAG + S_LAG, [("C", n, "z")]))
            release(clock)
            if kb == (M_AT if c else M_FIRST) and n + 1 < NU:
                plan.append(("M", n + 1, 0))
            if h == 0 and c and kb == 7:
                plan.append(("F", c - 1, 0))
            if h == 1 and c and kb % 2:
                if kb < 8:
                    plan.append(("R", c - 1, kb // 2))
                if kb == 7:
                    plan.append(("O", c - 1, 0))
            clock += 1
    plan.append(("M", NU, 0))
    release(clock + 100)
    plan += [("R", CPB - 1, k) for k in range(4)] + [("G", CPB - 1, 0), ("O", CPB - 1, 0)]
    return units, scores(0) + scores(1) + [("M", 0, 0)], plan


V_LAG, Z_LAG, O_LAG, S_LAG = 1, 3, 0, 1
M_AT, M_FIRST = 4, 1


KQ = 3 * DH
KM = KQ + 3


class AttentionOperands:

    def __init__(self, nc, scope, ctx, qk_d, v_d, cmask, cmaskT, identb, cst):
        f32, f32r, bf16 = mybir.dt.float32, mybir.dt.float32r, mybir.dt.bfloat16
        self.nc, self.qk_d = nc, qk_d
        self.rows_v = v_d.rearrange("(k p) f -> p k f", p=P)
        self.sems = []
        sb, _, sem = scope(ctx, "attend_operands", self.sems)
        self.kt = [sb(f"k_rows{n}", [P, QUAD, T], f32r) for n in range(2)]
        self.qt = [sb(f"q_rows{n}", [P, QUAD, CH], f32r) for n in range(2)]
        self.vt = [sb(f"v_blocks{n}", [P, NT // B, P], f32) for n in range(2)]
        self.mask, self.maskT = sb("mask", [P, P], bf16), sb("maskT", [P, P], bf16)
        self.idb = sb("identity_bf16", [P, P], bf16)
        self.ones = sb("ones", [P, DH], f32)
        self.zb = sb("zeros", [P, CH], bf16)
        self.sel = sb("selector", [P, DH], f32)
        self.constants = ((self.mask, cmask), (self.maskT, cmaskT), (self.idb, identb),
                          (self.sel, cst[:, C_SEL:C_ALL]))
        self.kv_in, self.q_in = [sem(f"kv_in{n}") for n in range(2)], [sem(f"q_in{n}") for n in range(2)]
        self.cst_in, self.filled = sem("constants_in"), sem("filled")

    def load_kv(self, sp, it, n):
        f32, heads = mybir.dt.float32, bass.ds(it * QUAD, QUAD)
        for rows, part in ((0, 0), (1, 1), (2, 0)):
            sp.dma_start(self.kt[n][rows * DH:(rows + 1) * DH, :, :].bitcast(f32),
                         self.qk_d[1][heads, part, :, :].rearrange("h d t -> d h t")).then_inc(self.kv_in[n], 16)
        sp.dma_start(self.vt[n][:, :, :], self.rows_v[:, bass.ds((it // NG) * (T // P), T // P),
                                                      bass.ds((it % NG) * P, P)]).then_inc(self.kv_in[n], 16)

    def load_q(self, sp, it, c):
        f32, heads = mybir.dt.float32, bass.ds(it * QUAD, QUAD)
        for rows, part in ((0, 0), (1, 0), (2, 1)):
            sp.dma_start(self.qt[c % 2][rows * DH:(rows + 1) * DH, :, :].bitcast(f32),
                         self.qk_d[0][heads, part, :, c * CH:(c + 1) * CH].rearrange("h d t -> d h t"))\
              .then_inc(self.q_in[c % 2], 16)

    def first_loads(self, sp):
        for s in self.sems:
            sp.sem_inc(s, UP)
        self.load_kv(sp, 0, 0)
        self.load_q(sp, 0, 0)
        self.load_q(sp, 0, 1)
        for dst, src in self.constants:
            sp.dma_start(dst[:, :], src).then_inc(self.cst_in, 16)

    def fill(self, pool):
        nc = self.nc
        fills = [(self.ones[:, :], 1.0), (self.zb[:, :], 0.0)]
        fills += [(self.kt[n][KQ:KM, :, :].bitcast(mybir.dt.float32), 1.0) for n in range(2)]
        for n, (rows, value) in enumerate(fills):
            nc.gpsimd.memset(rows, value).then_inc(self.filled, 1)
            pool.wait_ge(self.filled, n + 1 + UP)


def attend(nc, scope, operands, xn_d, attn_d, xs_d, pos, padpos):
    f32, f32r, bf16 = mybir.dt.float32, mybir.dt.float32r, mybir.dt.bfloat16
    i32 = mybir.dt.int32
    ALU, ACT, AX = mybir.AluOpType, mybir.ActivationFunctionType, mybir.AxisListType.X
    units, first, plan = attention_plan()
    SR, TR, PR, AR = 3, 3, 12, 4
    o = operands
    kt, qt, vt, ones, zb = o.kt, o.qt, o.vt, o.ones, o.zb
    mask, maskT, idb, sel = o.mask, o.maskT, o.idb, o.sel
    kv_in, q_in, load_kv, load_q = o.kv_in, o.q_in, o.load_kv, o.load_q
    FT = NT // NIT

    at, count = {}, {}
    for step in first + [step for step in plan if step[1] < len(units)]:
        ring = {"S": "s", "M": "t", "T": "t", "F": "t"}.get(step[0])
        for key in (step[0], ring):
            if key:
                at[key, step] = count.get(key, 0)
                count[key] = at[key, step] + 1
    NS, NTS, NV, NA, NZ, NU = count["s"], count["t"], count["T"], count["A"], count["Z"], len(units)

    def sums_of(n):
        return 2 * units[n][0] + TPC

    def steps(it, part):
        for kind, n, k in part:
            yield it + n // NU, (kind, n % NU, k)

    with ExitStack() as ctx:
        sems = []
        sb, ps, sem = scope(ctx, "attend", sems)
        sem0 = scope(ctx, "attend_pool")[2]
        started = sem0("counts_started")
        pt = sb("probsT", [P, PR, CH], f32)
        pair = sb("prob_pairs", [P, AR, CH], f32)
        o_ev = sb("o_partial", [P, QUAD, CH], f32)
        of = sb("o_sum", [P, CH], f32)
        zf = sb("z_sum", [P, CPB, CH], f32)
        ot = sb("attn_out", [P, CPB, CH], f32)
        mx = sb("piece_max", [P, 2, TPC, CPB], f32)
        m4 = sb("row_max", [P, 2, TPC], f32)
        rest = sb("max_rest", [P, 2, TPC], f32)
        mneg = [sb(f"neg_max_parts{n}", [P, TPC, P], bf16) for n in range(2)]
        xrow = sb("xn_tile", [P, D], f32)
        place = sb("row_index", [P, 2], i32)
        pad_place = sb("pad_index", [P, 1], i32)
        zero = sb("zero_rows", [P, D], f32)

        sp_ = [ps(f"s_psum{n}") for n in range(SR)]
        tp_ = [ps(f"t_psum{n}") for n in range(TR)]
        o_ps, z_ps = ps("o_psum"), ps("z_psum")

        set_up = sem("set_up")
        s_full, s_used = sem("s_full"), sem("s_used")
        t_full, t_used = sem("t_full"), sem("t_used")
        v_done, z_done, paired = sem("v_done"), sem("z_done"), sem("paired")
        m4_done, m_hi, m_rest, m_mid, m_done = (sem("row_max_done"), sem("neg_max_high"), sem("neg_max_rest"),
                                                sem("neg_max_middle"), sem("neg_max_low"))
        f_full, f_used = sem("last_sum_full"), sem("last_sum_copied")
        o_cp, z_cp, inverted = sem("o_copied"), sem("z_copied"), sem("sums_inverted")
        ot_done, ot_out = sem("attn_out_done"), sem("attn_stored")
        idx_in, zeroed = sem("index_in"), sem("zeroed")
        x_in, sc_out, pads_out = sem0("xn_tile_in"), sem0("scattered"), sem0("pads_out")
        moved_on, passed = sem("moved_on"), sem("passed")
        block = ctx.enter_context(nc.Block())

        def after(it, per, step, key):
            return it * per + at[key, step] + 1 + UP

        def ring_free(it, per, index, size):
            return it * per + max(0, index - size + 1) + UP

        @block.sync
        def _(sp):
            for s in sems:
                sp.sem_inc(s, UP)
            sp.sem_inc(ot_done, CPB)
            sp.sem_inc(started, 1)

            with sp.Fori(0, NIT // 2) as i:
                for n in range(2):
                    it = 2 * i + n
                    nxt = (it + 1) % NIT
                    for c in range(CPB):
                        last = ("T", units.index((c, QUAD - 1)), TPC * (c + 1) - 1)
                        sp.wait_ge(t_full, after(it, NTS, last, "t"))
                        sp.sem_inc(moved_on, 1)
                        if c == 1:
                            sp.wait_ge(v_done, it * NV + UP)
                            sp.sem_inc(moved_on, 1)
                            load_kv(sp, nxt, 1 - n)
                        load_q(sp, it if c < 2 else nxt, (c + 2) % CPB)
                        sp.wait_ge(ot_done, (it + 1) * CPB + c + 1 + UP)
                        sp.sem_inc(moved_on, 1)
                        sp.dma_start(attn_d[bass.ds(it, 1), :, c * CH:(c + 1) * CH].rearrange("o p t -> (o p) t"),
                                     ot[:, c, :]).then_inc(ot_out, 16)
            sp.wait_ge(ot_out, NIT * CPB * 16 + UP)
            for n in range(2):
                sp.wait_ge(kv_in[n], (NIT // 2 + (n == 0)) * 64 + UP)
                sp.wait_ge(q_in[n], (NIT * 2 + 1) * 48 + UP)

        def sum_of_pair(index):
            _, n, k = next(s for s in plan if s[0] == "A" and at["A", s] == index)
            return "Z", n, k

        @block.gpsimd
        def _(pool):
            pool.wait_ge(started, 1)
            nc.gpsimd.memset(zero[:, :], 0.0).then_inc(zeroed, 1)
            pool.wait_ge(zeroed, 1 + UP)
            with pool.Fori(0, NIT) as it:
                for step in plan:
                    kind, n, k = step
                    if kind == "A":
                        a, b = at["T", ("T", n, 2 * k)], at["T", ("T", n, 2 * k + 1)]
                        mine = at["A", step]
                        pool.wait_ge(t_used, after(it, NTS, ("T", n, 2 * k + 1), "t"))
                        before = mine - AR
                        if before >= 0:
                            pool.wait_ge(z_done, after(it, NZ, sum_of_pair(before), "Z"))
                        else:
                            pool.wait_ge(z_done, it * NZ + UP)
                        nc.gpsimd.tensor_tensor(pair[:, mine % AR, :], pt[:, a % PR, :], pt[:, b % PR, :], ALU.add)\
                            .then_inc(paired, 1)
                    elif kind == "O":
                        if n < CPB - 1:
                            pool.wait_ge(t_used, after(it, NTS, ("F", n, 0), "t"))
                        else:
                            pool.wait_ge(f_used, it + 1 + UP)
                        pool.wait_ge(inverted, (it * CPB + n + 1) * 4 + UP)
                        pool.wait_ge(ot_out, it * CPB * 16 + UP)
                        nc.gpsimd.tensor_tensor(ot[:, n, :], of[:, :], zf[:, n, :], ALU.mult).then_inc(ot_done, 1)
                    elif kind == "X":
                        tile, phase = it * FT + n // 4, n % 4
                        if phase == 0:
                            pool.dma_start(xrow[:, :], xn_d[bass.ds(tile * P, P), :]).then_inc(x_in, 16)
                            nc.gpsimd.tensor_copy(place[:, :],
                                                  pos[:, :, bass.ds(tile, 1)].rearrange("p c o -> p (c o)"))\
                                .then_inc(idx_in, 1)
                            if n == 0:
                                nc.gpsimd.tensor_copy(pad_place[:, :], padpos[:, bass.ds(it, 1)]).then_inc(idx_in, 1)
                        elif phase == 1:
                            pool.wait_ge(idx_in, it * (FT + 1) + n // 4 + 2 + UP)
                            pool.wait_ge(x_in, (tile + 1) * 16)
                            pool.sem_inc(passed, 1)
                            for m in range(2):
                                nc.gpsimd.indirect_dma_start(
                                    xs_d[:, :], bass.IndirectOffsetOnAxis(ap=place[:, m:m + 1], axis=0),
                                    xrow[:, :], None, bounds_check=NSLOT - 1).then_inc(sc_out, 16)
                            if n == 1:
                                nc.gpsimd.indirect_dma_start(
                                    xs_d[:, :], bass.IndirectOffsetOnAxis(ap=pad_place[:, 0:1], axis=0),
                                    zero[:, :], None, bounds_check=NSLOT - 1).then_inc(pads_out, 16)
                        elif phase == 3:
                            pool.wait_ge(sc_out, (tile + 1) * 32)
                            pool.sem_inc(passed, 1)
                            if n == 3:
                                pool.wait_ge(pads_out, (it + 1) * 16)
                                pool.sem_inc(passed, 1)

        @block.vector
        def _(dve):
            dve.wait_ge(started, 1)
            for n in range(2):
                nc.vector.memset(mneg[n][:, :, :], 0.0).then_inc(set_up, 1)
            dve.wait_ge(set_up, 2 + UP)

            def run(base, part):
                for it, step in steps(base, part):
                    kind, n, k = step
                    if kind == "S":
                        c = units[n][0]
                        t, piece = k
                        w = CH if piece < c else (t + 1) * P
                        dve.wait_ge(s_full, after(it, NS, step, "s"))
                        nc.vector.tensor_reduce(mx[:, n % 2, t, piece:piece + 1], sp_[at["s", step] % SR][:, 0:w],
                                                AX, ALU.max).then_inc(s_used, 1)
                        if (t, piece) != (TPC - 1, c):
                            continue
                        done = it * NU + n + 1 + UP
                        parts = mneg[n % 2]
                        dve.wait_ge(s_used, after(it, NS, step, "s"))
                        nc.vector.tensor_reduce(m4[:, n % 2, :], mx[:, n % 2, :, 0:c + 1], AX, ALU.max)\
                            .then_inc(m4_done, 1)
                        if n >= 2:
                            dve.wait_ge(t_full, after(it, NTS, ("M", n - 2, 0), "t"))
                        elif part is plan:
                            dve.wait_ge(t_full, after(it - 1, NTS, ("M", n - 2 + NU, 0), "t"))
                        dve.wait_ge(m4_done, done)
                        nc.vector.tensor_scalar(parts[:, :, KQ], m4[:, n % 2, :], -1.0, None, ALU.mult)\
                            .then_inc(m_hi, 1)
                        dve.wait_ge(m_hi, done)
                        nc.vector.scalar_tensor_tensor(out=rest[:, n % 2, :], in0=m4[:, n % 2, :], scalar=-1.0,
                                                       in1=parts[:, :, KQ], op0=ALU.mult, op1=ALU.subtract)\
                            .then_inc(m_rest, 1)
                        dve.wait_ge(m_rest, done)
                        nc.vector.tensor_copy(parts[:, :, KQ + 1], rest[:, n % 2, :]).then_inc(m_mid, 1)
                        dve.wait_ge(m_mid, done)
                        nc.vector.tensor_tensor(parts[:, :, KQ + 2], rest[:, n % 2, :], parts[:, :, KQ + 1],
                                                ALU.subtract).then_inc(m_done, 1)
                    elif kind == "R":
                        dve.wait_ge(z_cp, it * NU + (n + 1) * QUAD + UP)
                        cols = slice(k * P, (k + 1) * P)
                        nc.vector.reciprocal(zf[:, n, cols], zf[:, n, cols]).then_inc(inverted, 1)

            run(0, first)
            with dve.Fori(0, NIT) as i:
                run(i, plan)

        @block.scalar
        def _(act):
            act.wait_ge(started, 1)
            def run(base, part):
                for it, step in steps(base, part):
                    kind, n, k = step
                    c = units[n][0]
                    if kind == "T":
                        nv = at["T", step]
                        off = max(0, k - TPC * c) * P
                        before = next((s for s in plan if s[0] == "T" and at["T", s] == nv - PR), None)
                        if before is None:
                            act.wait_ge(z_done, it * NZ + UP)
                        else:
                            _, bn, bk = before
                            full = TPC * units[bn][0]
                            act.wait_ge(v_done, after(it, NV, ("V", bn, bk), "V"))
                            if bk < full:
                                act.wait_ge(paired, after(it, NA, ("A", bn, bk // 2), "A"))
                            else:
                                act.wait_ge(z_done, after(it, NZ, ("Z", bn, full // 2 + bk - full), "Z"))
                        act.wait_ge(t_full, after(it, NTS, step, "t"))
                        nc.scalar.activation(pt[:, nv % PR, 0:CH - off], tp_[at["t", step] % TR][:, 0:CH - off],
                                             ACT.Exp, scale=SCALE).then_inc(t_used, 1)
                    elif kind == "M":
                        c, h = units[n]
                        act.wait_ge(t_full, after(it, NTS, step, "t"))
                        nc.scalar.activation(qt[c % 2][KQ:KM, h, :], tp_[at["t", step] % TR][KQ:KM, :], ACT.Copy)\
                            .then_inc(t_used, 1)
                    elif kind in ("F", "G"):
                        act.wait_ge(ot_done, (it + 1) * CPB + n + UP)
                        if kind == "G":
                            act.wait_ge(f_full, it + 1 + UP)
                            nc.scalar.activation(of[:, :], z_ps[:, :], ACT.Copy).then_inc(f_used, 1)
                            continue
                        act.wait_ge(t_full, after(it, NTS, step, "t"))
                        nc.scalar.activation(of[:, :], tp_[at["t", step] % TR][:, :], ACT.Copy).then_inc(t_used, 1)
                    elif kind == "C" and k == "o":
                        h = units[n][1]
                        if h == 0:
                            if c:
                                act.wait_ge(t_full, after(it, NTS, ("F", c - 1, 0), "t"))
                            else:
                                act.wait_ge(f_full, it + UP)
                        act.wait_ge(v_done, after(it, NV, ("V", n, TPC * (c + 1) - 1), "V"))
                        nc.scalar.activation(o_ev[:, h, :], o_ps[:, :], ACT.Copy).then_inc(o_cp, 1)
                    elif kind == "C":
                        h = units[n][1]
                        if h == 0:
                            act.wait_ge(ot_done, it * CPB + c + 1 + UP)
                        act.wait_ge(z_done, after(it, NZ, ("Z", n, sums_of(n) - 1), "Z"))
                        for t in range(TPC):
                            cols = slice(t * P, (t + 1) * P)
                            last = nc.scalar.activation(zf[h * DH:(h + 1) * DH, c, cols],
                                                        z_ps[t * DH:(t + 1) * DH, cols], ACT.Copy)
                        last.then_inc(z_cp, 1)

            run(0, first)
            with act.Fori(0, NIT) as i:
                run(i, plan)

        @block.tensor
        def _(pe):
            pe.wait_ge(started, 1)
            pe.wait_ge(o.cst_in, 4 * 16 + UP)
            pe.wait_ge(set_up, 2 + UP)
            def run(turns, half, part):
                for kind, n, k in part:
                    ahead, n = divmod(n, NU)
                    it, mine = 2 * turns + half + ahead, (half + ahead) % 2
                    kk, vv = kt[mine], vt[mine]
                    step = (kind, n, k)
                    c, h = units[n]
                    if kind == "S":
                        t, piece = k
                        if (t, piece, n) == (0, 0, 0):
                            pe.wait_ge(kv_in[mine], (turns + (half + ahead) // 2 + 1) * 64 + UP)
                        if (t, piece, h) == (0, 0, 0):
                            pe.wait_ge(q_in[c % 2], (it * 2 + c // 2 + 1) * 48 + UP)
                        w = CH if piece < c else (t + 1) * P
                        pe.wait_ge(s_used, ring_free(it, NS, at["s", step], SR))
                        dst = sp_[at["s", step] % SR]
                        if piece == c:
                            nc.tensor.matmul(dst[:, w - P:w], idb[:, :], mask[:, :], start=True, stop=False,
                                             skip_group_check=True)
                        nc.tensor.matmul(dst[:, 0:w], qt[c % 2][0:KQ, h, t * P:(t + 1) * P],
                                         kk[0:KQ, h, piece * CH:piece * CH + w], start=piece < c, stop=True,
                                         skip_group_check=True).then_inc(s_full, 1)
                    elif kind == "M":
                        pe.wait_ge(m_done, it * NU + n + 1 + UP)
                        pe.wait_ge(t_used, ring_free(it, NTS, at["t", step], TR))
                        for t in range(TPC):
                            last = nc.tensor.matmul(tp_[at["t", step] % TR][:, t * P:(t + 1) * P],
                                                    mneg[n % 2][:, t, :], idb[:, :], start=True, stop=True)
                        last.then_inc(t_full, 1)
                    elif kind == "T":
                        if k == 0:
                            pe.wait_ge(t_used, after(it, NTS, ("M", n, 0), "t"))
                        pe.wait_ge(t_used, ring_free(it, NTS, at["t", step], TR))
                        off = max(0, k - TPC * c) * P
                        dst = tp_[at["t", step] % TR]
                        diag = k >= TPC * c
                        if diag:
                            nc.tensor.matmul(dst[:, 0:P], idb[:, :], maskT[:, :], start=True, stop=False,
                                             skip_group_check=True)
                        nc.tensor.matmul(dst[:, 0:CH - off], kk[0:KM, h, k * P:(k + 1) * P],
                                         qt[c % 2][0:KM, h, off:CH], start=not diag, stop=True,
                                         skip_group_check=True).then_inc(t_full, 1)
                    elif kind == "V":
                        pe.wait_ge(t_used, after(it, NTS, ("T", n, k), "t"))
                        off = max(0, k - TPC * c) * P
                        g = k % QUAD
                        dst = o_ps
                        if k == 0:
                            pe.wait_ge(o_cp, it * NU + n + UP)
                            if c == 0:
                                nc.tensor.matmul(dst[:, :], zb[:, 0:P], zb[:, :], start=True, stop=False,
                                                 skip_group_check=True)
                        nc.tensor.matmul(dst[g * DH:(g + 1) * DH, off:CH], vv[:, k, h * DH:(h + 1) * DH],
                                         pt[:, at["T", ("T", n, k)] % PR, 0:CH - off], start=c > 0 and k < QUAD,
                                         stop=k >= TPC * (c + 1) - QUAD, skip_group_check=True)\
                            .then_inc(v_done, 1)
                    elif kind == "Z":
                        dst = z_ps
                        npair = 2 * c
                        if k < npair:
                            pe.wait_ge(paired, after(it, NA, ("A", n, k), "A"))
                            off, src = 0, pair[:, at["A", ("A", n, k)] % AR, :]
                        else:
                            kb = k - npair + TPC * c
                            off = (k - npair) * P
                            src = pt[:, at["T", ("T", n, kb)] % PR, :]
                        if k == 0:
                            pe.wait_ge(z_cp, it * NU + n + UP)
                            if n == 0:
                                pe.wait_ge(f_used, it + UP)
                        for t in range(off // P, TPC):
                            g, cols = slice(t * DH, (t + 1) * DH), slice(t * P, (t + 1) * P)
                            last = nc.tensor.matmul(dst[g, cols], ones[:, :], src[:, t * P - off:(t + 1) * P - off],
                                                    start=k == 0, stop=k == sums_of(n) - TPC + t,
                                                    skip_group_check=True)
                        last.then_inc(z_done, 1)
                    elif kind in ("F", "G"):
                        pe.wait_ge(o_cp, it * NU + (n + 1) * QUAD + UP)
                        if kind == "F":
                            pe.wait_ge(t_used, ring_free(it, NTS, at["t", step], TR))
                            dst, full = tp_[at["t", step] % TR], t_full
                        else:
                            pe.wait_ge(z_cp, it * NU + (n + 1) * QUAD + UP)
                            dst, full = z_ps, f_full
                        for hh in range(QUAD):
                            last = nc.tensor.matmul(dst[hh * DH:(hh + 1) * DH, :], sel[:, :], o_ev[:, hh, :],
                                                    start=True, stop=True)
                        last.then_inc(full, 1)


            run(0, 0, first)
            with pe.Fori(0, NIT // 2) as i:
                for half in range(2):
                    run(i, half, plan)


def experts(nc, scope, wg, wu, wd, xs_d, ys_d, ident_sb, blk_e):
    f32, f32r = mybir.dt.float32, mybir.dt.float32r
    ALU, ACT = mybir.AluOpType, mybir.ActivationFunctionType
    RT = BLK // P
    PARTS = 3 * KD
    PPF = PARTS // KD
    with ExitStack() as ctx:
        sems = []
        sb, ps, sem = scope(ctx, "experts", sems)
        raw = sb("raw", [P, 3, KD, D], f32)
        wp = [[sb(f"weights{n}_part{m}", [P, 3, KD, D], f32r) for m in range(2)] for n in range(2)]
        xr = [sb(f"x_rows{n}", [P, RT, D], f32) for n in range(2)]
        xT = [[sb(f"xT{n}_part{m}", [P, KD, BLK], f32r) for m in range(2)] for n in range(2)]
        gate = [sb(f"gate{n}", [P, BLK], f32) for n in range(2)]
        hid = sb("hidden", [P, KD, BLK], f32)
        hp = [[sb(f"hidden{n}_part{m}", [P, KD, BLK], f32r) for m in range(2)] for n in range(2)]
        y = [sb(f"y_rows{n}", [P, RT, D], f32) for n in range(2)]
        tps = [ps(f"x_psum{n}") for n in range(2)]
        gps, ups = [ps(f"gate_psum{n}") for n in range(2)], [ps(f"up_psum{n}") for n in range(2)]
        yps = [ps(f"y_psum{n}") for n in range(2)]

        w_in, x_in = [sem(f"w{m}_in") for m in range(3)], [sem(f"x_in{n}") for n in range(2)]
        w_hi, w_lo = sem("w_high"), sem("w_low")
        tr, x_hi, x_lo = sem("transposes"), sem("xT_high"), sem("xT_low")
        gu, g_act, h_mul = sem("gate_up_full"), sem("gate_done"), sem("hidden_done")
        h_hi, h_lo = sem("hidden_high"), sem("hidden_low")
        y_full, y_cp, y_out = sem("y_full"), sem("y_copied"), [sem(f"y_out{n}") for n in range(2)]
        moved_on = sem("moved_on")
        block = ctx.enter_context(nc.Block())
        weights = [w.rearrange("e (k p) f -> p e k f", p=P) for w in (wg, wu, wd)]

        @block.sync
        def _(sp):
            for s in sems:
                sp.sem_inc(s, UP)

            def load_weights(b, m):
                e = sp.value_load(blk_e[0:1, bass.ds(b, 1)], min_val=0, max_val=E - 1)
                sp.dma_start(raw[:, m, :, :], weights[m][:, bass.ds(e, 1), :, :].rearrange("p e k f -> p (e k) f"))\
                  .then_inc(w_in[m], 16)

            def load_rows(b, n):
                sp.dma_start(xr[n][:, :, :], xs_d[bass.ds(b * BLK, BLK), :].rearrange("(t p) d -> p t d", p=P))\
                  .then_inc(x_in[n], 16)

            for m in range(3):
                load_weights(0, m)
            load_rows(0, 0)
            with sp.Fori(0, NBLK // 2) as i:
                for n in range(2):
                    b = 2 * i + n
                    nxt = (b + 1) % NBLK
                    sp.wait_ge(tr, b * 2 + UP)
                    sp.sem_inc(moved_on, 1)
                    load_rows(nxt, 1 - n)
                    for m in range(3):
                        sp.wait_ge(w_lo, b * PARTS + (m + 1) * KD + UP)
                        sp.sem_inc(moved_on, 1)
                        load_weights(nxt, m)
            for m in range(3):
                sp.wait_ge(w_in[m], (NBLK + 1) * 16 + UP)
            sp.wait_ge(x_in[0], (NBLK // 2 + 1) * 16 + UP)

        def high_part(act, b, n, q):
            m, k = q // KD, q % KD
            if k == 0:
                act.wait_ge(w_in[m], (b + 1) * 16 + UP)
            nc.scalar.activation(wp[n][0][:, m, k, :], raw[:, m, k, :], ACT.Copy).then_inc(w_hi, 1)

        def low_part(dve, b, n, q):
            m, k = q // KD, q % KD
            dve.wait_ge(w_hi, b * PARTS + q + 1 + UP)
            nc.vector.tensor_tensor(wp[n][1][:, m, k, :], raw[:, m, k, :], wp[n][0][:, m, k, :].bitcast(f32),
                                    ALU.subtract).then_inc(w_lo, 1)

        def rows_high(act, b, n):
            for h in range(2):
                act.wait_ge(tr, b * 2 + h + 1 + UP)
                nc.scalar.activation(xT[n][0][:, 2 * h:2 * h + 2, :], tps[h][:, :], ACT.Copy).then_inc(x_hi, 1)

        def rows_low(dve, b, n):
            for h in range(2):
                dve.wait_ge(x_hi, b * 2 + h + 1 + UP)
                nc.vector.tensor_tensor(xT[n][1][:, 2 * h:2 * h + 2, :], tps[h][:, :],
                                        xT[n][0][:, 2 * h:2 * h + 2, :].bitcast(f32), ALU.subtract).then_inc(x_lo, 1)

        @block.gpsimd
        def _(pool):
            with pool.Fori(0, NBLK // 2) as i:
                for n in range(2):
                    b = 2 * i + n
                    for k in range(KD):
                        pool.wait_ge(h_hi, b * KD + k + 1 + UP)
                        nc.gpsimd.tensor_tensor(hp[n][1][:, k, :], hid[:, k, :], hp[n][0][:, k, :].bitcast(f32),
                                                ALU.subtract).then_inc(h_lo, 1)

        @block.vector
        def _(dve):
            for q in range(PARTS):
                low_part(dve, 0, 0, q)
            rows_low(dve, 0, 0)
            with dve.Fori(0, NBLK // 2) as i:
                for n in range(2):
                    b = 2 * i + n
                    dve.wait_ge(h_lo, b * KD + UP)
                    for f in range(KD):
                        dve.wait_ge(g_act, b * KD + f + 1 + UP)
                        nc.vector.tensor_tensor(hid[:, f, :], ups[f % 2][:, 0:BLK], gate[f % 2][:, :], ALU.mult)\
                            .then_inc(h_mul, 1)
                        if f < KD - 1:
                            for q in range(f * PPF, (f + 1) * PPF):
                                low_part(dve, b + 1, 1 - n, q)
                        if f == KD - 2:
                            rows_low(dve, b + 1, 1 - n)
                    for q in range(PARTS - PPF, PARTS):
                        low_part(dve, b + 1, 1 - n, q)

        @block.scalar
        def _(act):
            for q in range(PARTS):
                high_part(act, 0, 0, q)
            rows_high(act, 0, 0)
            with act.Fori(0, NBLK // 2) as i:
                for n in range(2):
                    b = 2 * i + n
                    act.wait_ge(y_full, b * RT + UP)
                    for f in range(KD):
                        act.wait_ge(gu, b * KD + f + 1 + UP)
                        nc.scalar.activation(gate[f % 2][:, :], gps[f % 2][:, 0:BLK], ACT.Silu).then_inc(g_act, 1)
                        if f < KD - 1:
                            high_part(act, b + 1, 1 - n, f * PPF)
                        act.wait_ge(h_mul, b * KD + f + 1 + UP)
                        nc.scalar.activation(hp[n][0][:, f, :], hid[:, f, :], ACT.Copy).then_inc(h_hi, 1)
                        if f < KD - 1:
                            for q in range(f * PPF + 1, (f + 1) * PPF):
                                high_part(act, b + 1, 1 - n, q)
                        if f == KD - 2:
                            rows_high(act, b + 1, 1 - n)
                    for q in range(PARTS - PPF, PARTS):
                        high_part(act, b + 1, 1 - n, q)
                    act.wait_ge(y_out[n], i * 16 + UP)
                    for t in range(RT):
                        act.wait_ge(y_full, b * RT + t + 1 + UP)
                        nc.scalar.activation(y[n][:, t, :], yps[t % 2][:, :], ACT.Copy).then_inc(y_cp, 1)
                    act.wait_ge(y_cp, (b + 1) * RT + UP)
                    act.dma_start(ys_d[bass.ds(b * BLK, BLK), :].rearrange("(t p) d -> p t d", p=P), y[n][:, :, :])\
                       .then_inc(y_out[n], 16)
            for n in range(2):
                act.wait_ge(y_out[n], NBLK // 2 * 16 + UP)

        @block.tensor
        def _(pe):
            def turn(b, n, count):
                pe.wait_ge(x_in[n], count * 16 + UP)
                pe.wait_ge(x_lo, b * 2 + UP)
                for k in range(KD):
                    for t in range(RT):
                        col = (k % 2) * BLK + t * P
                        last = nc.tensor.transpose(tps[k // 2][:, col:col + P],
                                                   xr[n][:, t, k * P:(k + 1) * P], ident_sb[:, :])
                    if k % 2:
                        last.then_inc(tr, 1)

            turn(0, 0, 1)
            with pe.Fori(0, NBLK // 2) as i:
                for n in range(2):
                    b = 2 * i + n
                    pe.wait_ge(x_lo, (b + 1) * 2 + UP)
                    pe.wait_ge(w_lo, b * PARTS + 2 * KD + UP)
                    for f in range(KD):
                        pe.wait_ge(h_mul, b * KD + (f - 1 if f >= 2 else 0) + UP)
                        for m, dst in ((0, gps[f % 2]), (1, ups[f % 2])):
                            for s, (k, (a, w2)) in enumerate([(k, p) for k in range(KD) for p in PASSES]):
                                last = nc.tensor.matmul(dst[:, 0:BLK], wp[n][w2][:, m, k, f * P:(f + 1) * P],
                                                        xT[n][a][:, k, :], start=s == 0, stop=s == 3 * KD - 1)
                        last.then_inc(gu, 1)
                        if f == KD - 2:
                            turn(b + 1, 1 - n, i + 1 + n)
                    pe.wait_ge(w_lo, (b + 1) * PARTS + UP)
                    pe.wait_ge(y_cp, b * RT + UP)
                    for ks in (range(KD - 1), range(KD - 1, KD)):
                        for t in range(RT):
                            for k in ks:
                                if t == 0:
                                    pe.wait_ge(h_lo, b * KD + k + 1 + UP)
                                for s, (a, w2) in enumerate(PASSES):
                                    last = nc.tensor.matmul(yps[t][:, :], hp[n][a][:, k, t * P:(t + 1) * P],
                                                            wp[n][w2][:, 2, k, :], start=k == 0 and s == 0,
                                                            stop=k == KD - 1 and s == len(PASSES) - 1)
                            if k == KD - 1:
                                last.then_inc(y_full, 1)


def combine(nc, scope, x, woutT, attn_d, ys_d, pos, wts, out):
    f32, i32 = mybir.dt.float32, mybir.dt.int32
    ALU, ACT = mybir.AluOpType, mybir.ActivationFunctionType
    with ExitStack() as ctx:
        sems = []
        sb, ps, sem = scope(ctx, "combine", sems)
        sem0 = scope(ctx, "combine_pool")[2]
        wo = sb("wo", [P, NG, D], f32)
        at = [sb(f"attn_chunk{n}", [P, NG, CH], f32) for n in range(2)]
        xr = [sb(f"x_chunk{n}", [P, TPC, D], f32) for n in range(2)]
        y1 = [sb(f"first_choice{n}", [P, TPC, D], f32) for n in range(2)]
        y2 = [sb(f"second_choice{n}", [P, TPC, D], f32) for n in range(2)]
        gate = [sb(f"moe_gate{n}", [P, TPC, D], f32) for n in range(2)]
        res = [sb(f"result{n}", [P, TPC, D], f32) for n in range(2)]
        ix = [sb(f"row_index{n}", [P, 2, TPC], i32) for n in range(2)]
        wt = [sb(f"weights{n}", [P, 2, TPC], f32) for n in range(2)]
        sps = [[ps(f"s_psum{n}_{t}") for t in range(TPC)] for n in range(2)]
        w_in = sem("wo_in")
        in_ = [sem(f"chunk_in{n}") for n in range(2)]
        passed = sem("passed")
        idx, got = sem("index_copied"), [sem0(f"gathered{n}") for n in range(2)]
        wt_cp, y_w = sem("weights_copied"), sem("weighted")
        mix, act_d, s_full, s_mul, add = ([sem(f"{name}{n}") for n in range(2)] for name in (
            "mixed", "gated", "s_full", "s_times_gate", "added"))
        o_out = [sem(f"out_stored{n}") for n in range(2)]
        moved_on = sem("moved_on")
        block = ctx.enter_context(nc.Block())

        def tiles(i, t=TPC - 1):
            return i * TPC + t + 1 + UP

        def free(i):
            return i * TPC + UP

        @block.sync
        def _(sp):
            for s in sems:
                sp.sem_inc(s, UP)
            sp.dma_start(wo[:, :, :], woutT.rearrange("(k p) o -> p k o", p=P)).then_inc(w_in, 16)
            with sp.Fori(0, NCH // 2) as i:
                for n in range(2):
                    c = 2 * i + n
                    sp.wait_ge(s_full[n], free(i))
                    sp.wait_ge(add[n], free(i))
                    sp.sem_inc(moved_on, 1)
                    batch, at_t = c // CPB, (c % CPB) * CH
                    sp.dma_start(at[n][:, :, :], attn_d[bass.ds(batch * NG, NG), :, bass.ds(at_t, CH)]
                                 .rearrange("g p t -> p g t")).then_inc(in_[n], 16)
                    sp.dma_start(xr[n][:, :, :], x[bass.ds(c * CH, CH), :].rearrange("(t p) d -> p t d", p=P))\
                      .then_inc(in_[n], 16)

        @block.gpsimd
        def _(pool):
            with pool.Fori(0, NCH // 2) as i:
                for n in range(2):
                    c = 2 * i + n
                    pool.wait_ge(mix[n], free(i))
                    nc.gpsimd.tensor_copy(ix[n][:, :, :], pos[:, :, bass.ds(c * TPC, TPC)]).then_inc(idx, 1)
                    pool.wait_ge(idx, c + 1 + UP)
                    pool.sem_inc(passed, 1)
                    for t in range(TPC):
                        for m, y in ((0, y1), (1, y2)):
                            nc.gpsimd.indirect_dma_start(y[n][:, t, :], None, ys_d[:, :],
                                                         bass.IndirectOffsetOnAxis(ap=ix[n][:, m, t:t + 1], axis=0),
                                                         bounds_check=NSLOT - 1).then_inc(got[n], 16)

        @block.vector
        def _(dve):
            with dve.Fori(0, NCH // 2) as i:
                for n in range(2):
                    c = 2 * i + n
                    nc.vector.tensor_copy(wt[n][:, :, :], wts[:, :, bass.ds(c * TPC, TPC)]).then_inc(wt_cp, 1)
                    dve.wait_ge(wt_cp, c + 1 + UP)
                    dve.wait_ge(got[n], (i + 1) * 2 * TPC * 16)
                    for t in range(TPC):
                        nc.vector.tensor_scalar(y1[n][:, t, :], y1[n][:, t, :], wt[n][:, 0, t:t + 1], None,
                                                ALU.mult).then_inc(y_w, 1)
                    for t in range(TPC):
                        dve.wait_ge(y_w, c * TPC + t + 1 + UP)
                        nc.vector.scalar_tensor_tensor(out=gate[n][:, t, :], in0=y2[n][:, t, :],
                                                       scalar=wt[n][:, 1, t:t + 1], in1=y1[n][:, t, :],
                                                       op0=ALU.mult, op1=ALU.add).then_inc(mix[n], 1)
                    dve.wait_ge(in_[n], (i + 1) * 32 + UP)
                    dve.wait_ge(o_out[n], i * 16 + UP)
                    for t in range(TPC):
                        dve.wait_ge(act_d[n], tiles(i, t))
                        dve.wait_ge(s_full[n], tiles(i, t))
                        nc.vector.tensor_tensor(res[n][:, t, :], sps[n][t][:, :], gate[n][:, t, :], ALU.mult)\
                            .then_inc(s_mul[n], 1)
                    for t in range(TPC):
                        dve.wait_ge(s_mul[n], tiles(i, t))
                        nc.vector.tensor_tensor(res[n][:, t, :], res[n][:, t, :], xr[n][:, t, :], ALU.add)\
                            .then_inc(add[n], 1)

        @block.scalar
        def _(act):
            with act.Fori(0, NCH // 2) as i:
                for n in range(2):
                    c = 2 * i + n
                    for t in range(TPC):
                        act.wait_ge(mix[n], tiles(i, t))
                        nc.scalar.activation(gate[n][:, t, :], gate[n][:, t, :], ACT.Silu).then_inc(act_d[n], 1)
                    act.wait_ge(add[n], tiles(i))
                    act.dma_start(out[bass.ds(c * CH, CH), :].rearrange("(t p) d -> p t d", p=P), res[n][:, :, :])\
                       .then_inc(o_out[n], 16)
            for n in range(2):
                act.wait_ge(o_out[n], NCH // 2 * 16 + UP)

        @block.tensor
        def _(pe):
            pe.wait_ge(w_in, 16 + UP)
            with pe.Fori(0, NCH // 2) as i:
                for n in range(2):
                    c = 2 * i + n
                    pe.wait_ge(in_[n], (i + 1) * 32 + UP)
                    pe.wait_ge(s_mul[n], free(i))
                    for t in range(TPC):
                        for k in range(NG):
                            last = nc.tensor.matmul(sps[n][t][:, :], at[n][:, k, t * P:(t + 1) * P], wo[:, k, :],
                                                    start=k == 0, stop=k == NG - 1)
                        last.then_inc(s_full[n], 1)


def kernel(L0_attn_x, L0_attn_W_qkv, L0_attn_W_out, L0_ffn_router_w, L0_ffn_router_b, L0_ffn_we_gate,
           L0_ffn_we_up, L0_ffn_we_down):
    import ml_dtypes
    import numpy as np
    from concourse import bacc
    from concourse.bass_utils import run_bass_kernel_spmd

    def arr(a):
        return np.asarray(a)

    wt = arr(L0_attn_W_qkv).T
    qk = wt[:, :2 * D].reshape(D, 2, 2, H // 2, DH // 2, 2).transpose(0, 1, 2, 5, 3, 4).reshape(D, 2 * D)
    wqkvT = np.ascontiguousarray(np.concatenate([qk, wt[:, 2 * D:]], axis=1))
    freqs = (1.0 / np.float32(10000.0) ** (np.arange(0, DH, 2, dtype=np.float32) / np.float32(DH))).astype(np.float32)
    angles = np.outer(np.arange(T, dtype=np.float32), freqs).astype(np.float32)
    cos = np.ascontiguousarray(np.tile(np.cos(angles).T, (H // 2, 1)))
    sin = np.ascontiguousarray(np.tile(np.sin(angles).T, (H // 2, 1)))
    r = np.arange(P)
    bf = ml_dtypes.bfloat16
    arrays = {
        "x": arr(L0_attn_x).reshape(NTOK, D),
        "wqkvT": wqkvT,
        "woutT": np.ascontiguousarray(arr(L0_attn_W_out).T),
        "rwT": arr(L0_ffn_router_w),
        "rb": arr(L0_ffn_router_b).reshape(E, 1),
        "wg": arr(L0_ffn_we_gate),
        "wu": arr(L0_ffn_we_up),
        "wd": arr(L0_ffn_we_down),
        "cos": cos,
        "sin": sin,
        "cmask": np.where(r[None, :] > r[:, None], NEG, 0).astype(bf),
        "cmaskT": np.where(r[:, None] > r[None, :], NEG, 0).astype(bf),
        "identb": np.eye(P).astype(bf),
        "ident": np.eye(P, dtype=np.float32),
        "cst": constants(),
    }
    nc = bacc.Bacc("TRN2", target_bir_lowering=False, num_devices=1)
    args, maps = [], {}
    for name, a in arrays.items():
        maps["in_" + name] = a
        args.append(nc.dram_tensor("in_" + name, a.shape, mybir.dt.from_np(a.dtype), kind="ExternalInput").ap())
    res = nc.dram_tensor("out_rows", (NTOK, D), mybir.dt.float32, kind="ExternalOutput").ap()
    build(nc, *args, res)
    r = run_bass_kernel_spmd(nc, [maps], core_ids=[0])
    return r.results[0]["out_rows"].reshape(B, T, D)
```
